# Optimizing a Trainium2 kernel written in Bass

```python
import numpy as np
import jax
import jax.numpy as jnp

def _softmax(x, axis=-1):
    return jax.nn.softmax(x, axis=axis)

def _gelu(x):
    return jax.nn.gelu(x, approximate=True)

def _silu(x):
    return jax.nn.silu(x)

def _sigmoid(x):
    return jax.nn.sigmoid(x)

def _layernorm(x, axis=-1, eps=1e-05):
    m = jnp.mean(x, axis=axis, keepdims=True)
    v = jnp.var(x, axis=axis, keepdims=True)
    return (x - m) / jnp.sqrt(v + eps)

def _scatter_add(tgt, idx, src, axis=0):
    return tgt.at[idx].add(src)

def _segment_sum(src, seg, n):
    return jax.ops.segment_sum(src, seg, n)
kernel_name = 'mk_adaln_d2_jaxref_r8_b175e1'

def setup_inputs(seed: int=0):
    np.random.seed(seed)
    _w = jnp.asarray

    def _L0_attn_setup():
        import jax, jax.numpy as jnp
        import numpy as np
        B, L, D, N = (2, 256, 128, 16)
        H = D // N
        THETA = 10000.0

        def apply_rope(x):
            l, h = (x.shape[-2], x.shape[-1])
            freqs = THETA ** (-jnp.arange(0, h, 2, dtype=jnp.float32) / h)
            ang = jnp.arange(l, dtype=jnp.float32)[:, None] * freqs
            cos, sin = (jnp.cos(ang), jnp.sin(ang))
            x_even = x[..., 0::2]
            x_odd = x[..., 1::2]
            out_even = cos * x_even - sin * x_odd
            out_odd = sin * x_even + cos * x_odd
            return jnp.stack((out_even, out_odd), axis=-1).reshape(x.shape)
        key = jax.random.key(seed)
        ks = jax.random.split(key, 9)
        s = 0.02
        return {'x': jax.random.normal(ks[0], (B, L, D), dtype=jnp.float32), 'Wq': jax.random.normal(ks[1], (D, D), dtype=jnp.float32) * s, 'bq': jax.random.normal(ks[2], (D,), dtype=jnp.float32) * s, 'Wk': jax.random.normal(ks[3], (D, D), dtype=jnp.float32) * s, 'bk': jax.random.normal(ks[4], (D,), dtype=jnp.float32) * s, 'Wv': jax.random.normal(ks[5], (D, D), dtype=jnp.float32) * s, 'bv': jax.random.normal(ks[6], (D,), dtype=jnp.float32) * s, 'Wo': jax.random.normal(ks[7], (D, D), dtype=jnp.float32) * s, 'bo': jax.random.normal(ks[8], (D,), dtype=jnp.float32) * s, 'scale': jnp.ones((1,), dtype=jnp.float32) * H ** (-0.5)}
    _L0_attn_in = _L0_attn_setup()

    def _L0_ffn_setup():
        import jax, jax.numpy as jnp
        import numpy as np
        H = 128
        E = 32
        I = 64
        TOP_K = 6
        IS = 128
        NORM_MIN = 1e-12
        B, S = (2, 128)
        key = jax.random.key(seed)
        ks = jax.random.split(key, 8)
        sc = 0.02
        return {'hidden_states': jax.random.normal(ks[0], (B, S, H), jnp.float32), 'router_weight': jax.random.normal(ks[1], (E, H), jnp.float32) * sc, 'e_score_bias': jnp.zeros((E,), jnp.float32), 'gate_up_proj': jax.random.normal(ks[2], (E, 2 * I, H), jnp.float32) * sc, 'down_proj': jax.random.normal(ks[3], (E, H, I), jnp.float32) * sc, 'shared_gate_w': jax.random.normal(ks[4], (IS, H), jnp.float32) * sc, 'shared_up_w': jax.random.normal(ks[5], (IS, H), jnp.float32) * sc, 'shared_down_w': jax.random.normal(ks[6], (H, IS), jnp.float32) * sc}
    _L0_ffn_in = _L0_ffn_setup()
    _L0_c = _w((lambda *s: np.random.randn(*s).astype(np.float32) * 0.05)(16, 128))
    _L0_wmod = _w((lambda *s: np.random.randn(*s).astype(np.float32) * 0.05)(128, 6 * 128) * 128 ** (-0.5))

    def _L1_attn_setup():
        import jax, jax.numpy as jnp
        import numpy as np
        _DENSE_LOCAL_W = 32
        _DYADIC = [48, 64, 96, 128, 192, 32, 48, 64, 96, 128, 192]
        OFFSETS = sorted(set(range(_DENSE_LOCAL_W + 1)) | set(_DYADIC))
        B, N, D, H = (2, 512, 128, 16)
        HD = D // H
        NEG = -1e+30

        def _shift(t, o):
            if o == 0:
                return t
            n = t.shape[2]
            return jnp.pad(t, ((0, 0), (0, 0), (o, 0), (0, 0)))[:, :, :n]
        key = jax.random.key(seed)
        ks = jax.random.split(key, 9)
        alphas = jnp.linspace(0.2, 2.0, H)
        delta = jnp.log1p(jnp.asarray(OFFSETS, dtype=jnp.float32))
        pos_bias = -delta[:, None] * alphas[None, :]
        return {'x': jax.random.normal(ks[0], (B, N, D), jnp.float32), 'qkv_w': jax.random.normal(ks[1], (3 * D, D), jnp.float32) * 0.02, 'qkv_b': jax.random.normal(ks[2], (3 * D,), jnp.float32) * 0.01, 'out_w': jax.random.normal(ks[3], (D, D), jnp.float32) * 0.02, 'out_b': jnp.zeros((D,), jnp.float32), 'gate_w': jax.random.normal(ks[4], (D, D), jnp.float32) * 0.02, 'gate_b': jnp.zeros((D,), jnp.float32), 'pos_bias': pos_bias, 'scale_embed': jax.random.normal(ks[5], (len(OFFSETS), HD), jnp.float32) * 0.02, 'if_gain': 1.0 + jax.random.normal(ks[6], (H,), jnp.float32) * 0.05}
    _L1_attn_in = _L1_attn_setup()

    def _L1_ffn_setup():
        import jax, jax.numpy as jnp
        import numpy as np
        key = jax.random.key(seed)
        ks = jax.random.split(key, 5)
        B, T, D, E = (4, 256, 128, 8)
        inputs = jax.random.normal(ks[0], (B, T, D), dtype=jnp.float32)
        Wr = jax.random.normal(ks[1], (D, E), dtype=jnp.float32) * 0.02
        br = jnp.zeros((E,), dtype=jnp.float32)
        W1 = jax.random.normal(ks[2], (E, D, D), dtype=jnp.float32) * 0.02
        b1 = jnp.zeros((E, D), dtype=jnp.float32)
        W2 = jax.random.normal(ks[3], (E, D, D), dtype=jnp.float32) * 0.02
        b2 = jnp.zeros((E, D), dtype=jnp.float32)
        return {'inputs': inputs, 'Wr': Wr, 'br': br, 'W1': W1, 'b1': b1, 'W2': W2, 'b2': b2}
    _L1_ffn_in = _L1_ffn_setup()
    _L1_c = _w((lambda *s: np.random.randn(*s).astype(np.float32) * 0.05)(16, 128))
    _L1_wmod = _w((lambda *s: np.random.randn(*s).astype(np.float32) * 0.05)(128, 6 * 128) * 128 ** (-0.5))
    _d = {'L0_attn_x': _L0_attn_in['x'], 'L0_attn_Wq': _L0_attn_in['Wq'], 'L0_attn_bq': _L0_attn_in['bq'], 'L0_attn_Wk': _L0_attn_in['Wk'], 'L0_attn_bk': _L0_attn_in['bk'], 'L0_attn_Wv': _L0_attn_in['Wv'], 'L0_attn_bv': _L0_attn_in['bv'], 'L0_attn_Wo': _L0_attn_in['Wo'], 'L0_attn_bo': _L0_attn_in['bo'], 'L0_attn_scale': _L0_attn_in['scale'], 'L0_ffn_router_weight': _L0_ffn_in['router_weight'], 'L0_ffn_e_score_bias': _L0_ffn_in['e_score_bias'], 'L0_ffn_gate_up_proj': _L0_ffn_in['gate_up_proj'], 'L0_ffn_down_proj': _L0_ffn_in['down_proj'], 'L0_ffn_shared_gate_w': _L0_ffn_in['shared_gate_w'], 'L0_ffn_shared_up_w': _L0_ffn_in['shared_up_w'], 'L0_ffn_shared_down_w': _L0_ffn_in['shared_down_w'], 'L0_c': _L0_c, 'L0_wmod': _L0_wmod, 'L1_attn_qkv_w': _L1_attn_in['qkv_w'], 'L1_attn_qkv_b': _L1_attn_in['qkv_b'], 'L1_attn_out_w': _L1_attn_in['out_w'], 'L1_attn_out_b': _L1_attn_in['out_b'], 'L1_attn_gate_w': _L1_attn_in['gate_w'], 'L1_attn_gate_b': _L1_attn_in['gate_b'], 'L1_attn_pos_bias': _L1_attn_in['pos_bias'], 'L1_attn_scale_embed': _L1_attn_in['scale_embed'], 'L1_attn_if_gain': _L1_attn_in['if_gain'], 'L1_ffn_Wr': _L1_ffn_in['Wr'], 'L1_ffn_br': _L1_ffn_in['br'], 'L1_ffn_W1': _L1_ffn_in['W1'], 'L1_ffn_b1': _L1_ffn_in['b1'], 'L1_ffn_W2': _L1_ffn_in['W2'], 'L1_ffn_b2': _L1_ffn_in['b2'], 'L1_c': _L1_c, 'L1_wmod': _L1_wmod}
    _x0 = _d['L0_attn_x']
    _d['L0_attn_x'] = jax.random.normal(jax.random.fold_in(jax.random.key(seed), 1), (16, 256, 128), dtype=_x0.dtype)
    del _x0
    return _d

def reference(L0_attn_x, L0_attn_Wq, L0_attn_bq, L0_attn_Wk, L0_attn_bk, L0_attn_Wv, L0_attn_bv, L0_attn_Wo, L0_attn_bo, L0_attn_scale, L0_ffn_router_weight, L0_ffn_e_score_bias, L0_ffn_gate_up_proj, L0_ffn_down_proj, L0_ffn_shared_gate_w, L0_ffn_shared_up_w, L0_ffn_shared_down_w, L0_c, L0_wmod, L1_attn_qkv_w, L1_attn_qkv_b, L1_attn_out_w, L1_attn_out_b, L1_attn_gate_w, L1_attn_gate_b, L1_attn_pos_bias, L1_attn_scale_embed, L1_attn_if_gain, L1_ffn_Wr, L1_ffn_br, L1_ffn_W1, L1_ffn_b1, L1_ffn_W2, L1_ffn_b2, L1_c, L1_wmod):

    def _L0_attn_ref(x, Wq, bq, Wk, bk, Wv, bv, Wo, bo, scale):
        import jax, jax.numpy as jnp
        import numpy as np
        B, L, D, N = (2, 256, 128, 16)
        H = D // N
        THETA = 10000.0

        def apply_rope(x):
            l, h = (x.shape[-2], x.shape[-1])
            freqs = THETA ** (-jnp.arange(0, h, 2, dtype=jnp.float32) / h)
            ang = jnp.arange(l, dtype=jnp.float32)[:, None] * freqs
            cos, sin = (jnp.cos(ang), jnp.sin(ang))
            x_even = x[..., 0::2]
            x_odd = x[..., 1::2]
            out_even = cos * x_even - sin * x_odd
            out_odd = sin * x_even + cos * x_odd
            return jnp.stack((out_even, out_odd), axis=-1).reshape(x.shape)
        b, l, d = x.shape
        q = x @ Wq.T + bq
        k = x @ Wk.T + bk
        v = x @ Wv.T + bv
        q = q.reshape(b, l, N, H).transpose(0, 2, 1, 3)
        k = k.reshape(b, l, N, H).transpose(0, 2, 1, 3)
        v = v.reshape(b, l, N, H).transpose(0, 2, 1, 3)
        q = apply_rope(q) * scale
        k = apply_rope(k)
        dots = jnp.einsum('bnih,bnjh->bnij', q, k)
        i = jnp.arange(l)
        mask = i[:, None] < i[None, :]
        dots = jnp.where(mask, jnp.float32(-100000.0), dots)
        attn = jax.nn.softmax(dots, axis=-1)
        o = jnp.einsum('bnij,bnjh->bnih', attn, v)
        o = o.transpose(0, 2, 1, 3).reshape(b, l, d)
        return o @ Wo.T + bo

    def _L0_ffn_ref(hidden_states, router_weight, e_score_bias, gate_up_proj, down_proj, shared_gate_w, shared_up_w, shared_down_w):
        import jax, jax.numpy as jnp
        import numpy as np
        H = 128
        E = 32
        I = 64
        TOP_K = 6
        IS = 128
        NORM_MIN = 1e-12
        B, S = (2, 128)
        b, s, h = hidden_states.shape
        x = hidden_states.reshape(-1, h)
        T = x.shape[0]
        shared_out = jax.nn.silu(x @ shared_gate_w.T) * (x @ shared_up_w.T) @ shared_down_w.T
        xf = x.astype(jnp.float32)
        router_logits = xf @ router_weight.T
        routing_weights = jax.nn.softmax(router_logits, axis=-1)
        corrected = routing_weights + e_score_bias
        _, top_idx = jax.lax.top_k(corrected, TOP_K)
        top_w = jnp.take_along_axis(routing_weights, top_idx, axis=-1)
        top_w = top_w / jnp.clip(top_w.sum(axis=-1, keepdims=True), NORM_MIN)
        top_w = top_w.astype(x.dtype)
        combine = jnp.zeros((T, E), x.dtype).at[jnp.arange(T)[:, None], top_idx].add(top_w)
        gu = jnp.einsum('th,eih->tei', x, gate_up_proj)
        gate, up = jnp.split(gu, 2, axis=-1)
        hmid = jax.nn.silu(gate) * up
        y = jnp.einsum('tei,ehi->teh', hmid, down_proj)
        out = jnp.einsum('teh,te->th', y, combine) + shared_out
        return out.reshape(b, s, h)

    def _L1_attn_ref(x, qkv_w, qkv_b, out_w, out_b, gate_w, gate_b, pos_bias, scale_embed, if_gain):
        import jax, jax.numpy as jnp
        import numpy as np
        _DENSE_LOCAL_W = 32
        _DYADIC = [48, 64, 96, 128, 192, 32, 48, 64, 96, 128, 192]
        OFFSETS = sorted(set(range(_DENSE_LOCAL_W + 1)) | set(_DYADIC))
        B, N, D, H = (2, 512, 128, 16)
        HD = D // H
        NEG = -1e+30

        def _shift(t, o):
            if o == 0:
                return t
            n = t.shape[2]
            return jnp.pad(t, ((0, 0), (0, 0), (o, 0), (0, 0)))[:, :, :n]
        b, n, d = x.shape
        qkv = x @ qkv_w.T + qkv_b
        q, k, v = jnp.split(qkv, 3, axis=-1)
        heads = lambda t: t.reshape(b, n, H, HD).transpose(0, 2, 1, 3)
        q, k, v = (heads(q), heads(k), heads(v))
        inv = 1.0 / jnp.sqrt(jnp.asarray(HD, x.dtype))
        qs = jnp.einsum('bhnd,od->bhno', q, scale_embed)
        pos = jnp.arange(n)
        logits = []
        for i, o in enumerate(OFFSETS):
            qk = jnp.einsum('bhnd,bhnd->bhn', q, _shift(k, o))
            lg = qk * inv * (1.0 + qs[..., i]) + pos_bias[i][None, :, None]
            lg = jnp.where(pos[None, None, :] >= o, lg, NEG)
            logits.append(lg)
        logits = jnp.stack(logits, axis=-1)
        p = jax.nn.softmax(logits, axis=-1)
        out = jnp.zeros_like(q)
        for i, o in enumerate(OFFSETS):
            out = out + p[..., i][..., None] * _shift(v, o)
        out = out * if_gain[None, :, None, None]
        out_flat = out.transpose(0, 2, 1, 3).reshape(b, n, d)
        gate = jax.nn.sigmoid(x @ gate_w.T + gate_b)
        return out_flat * gate @ out_w.T + out_b

    def _L1_ffn_ref(inputs, Wr, br, W1, b1, W2, b2):
        import jax, jax.numpy as jnp
        import numpy as np
        B, T, D = inputs.shape
        E = Wr.shape[1]
        x = inputs.reshape(B * T, D)
        N = x.shape[0]
        C = N // E
        logits = x @ Wr + br
        probs = jax.nn.softmax(logits, axis=-1)
        gate = jnp.max(probs, axis=-1, keepdims=True)
        idx = jnp.argmax(probs, axis=-1)
        mask = jax.nn.one_hot(idx, E, dtype=jnp.float32)
        pos = (jnp.cumsum(mask, axis=0) * mask).astype(jnp.int32)
        mask = mask * (pos < C).astype(jnp.float32)
        mask_flat = jnp.sum(mask, axis=-1, keepdims=True)
        gate = gate * mask_flat
        combine = (gate * mask_flat * jax.nn.one_hot(idx, E, dtype=jnp.float32))[..., None] * jax.nn.one_hot(pos, C, dtype=jnp.float32)
        dispatch = combine
        expert_in = jnp.einsum('nd,nec->ecd', x, dispatch)
        h = jax.nn.relu(jnp.einsum('ecd,edf->ecf', expert_in, W1) + b1[:, None, :])
        eo = jnp.einsum('ecf,efd->ecd', h, W2) + b2[:, None, :]
        out = jnp.einsum('ecd,nec->nd', eo, combine)
        return out.reshape(B, T, D)
    x = L0_attn_x
    mod = (_silu(L0_c) @ L0_wmod).reshape(L0_c.shape[0], 6, 1, -1)
    sa, ca, ga, sb, cb, gb = (mod[:, 0], mod[:, 1], mod[:, 2], mod[:, 3], mod[:, 4], mod[:, 5])
    ga = (2 * (ga >= 0) - 1) * jnp.maximum(jnp.abs(ga), 0.25)
    gb = (2 * (gb >= 0) - 1) * jnp.maximum(jnp.abs(gb), 0.25)
    h = _layernorm(x, axis=-1) * (1 + ca) + sa
    x = x + ga * _L0_attn_ref(h, L0_attn_Wq, L0_attn_bq, L0_attn_Wk, L0_attn_bk, L0_attn_Wv, L0_attn_bv, L0_attn_Wo, L0_attn_bo, L0_attn_scale)
    h = _layernorm(x, axis=-1) * (1 + cb) + sb
    x = x + gb * _L0_ffn_ref(h, L0_ffn_router_weight, L0_ffn_e_score_bias, L0_ffn_gate_up_proj, L0_ffn_down_proj, L0_ffn_shared_gate_w, L0_ffn_shared_up_w, L0_ffn_shared_down_w)
    mod = (_silu(L1_c) @ L1_wmod).reshape(L1_c.shape[0], 6, 1, -1)
    sa, ca, ga, sb, cb, gb = (mod[:, 0], mod[:, 1], mod[:, 2], mod[:, 3], mod[:, 4], mod[:, 5])
    ga = (2 * (ga >= 0) - 1) * jnp.maximum(jnp.abs(ga), 0.25)
    gb = (2 * (gb >= 0) - 1) * jnp.maximum(jnp.abs(gb), 0.25)
    h = _layernorm(x, axis=-1) * (1 + ca) + sa
    x = x + ga * _L1_attn_ref(h, L1_attn_qkv_w, L1_attn_qkv_b, L1_attn_out_w, L1_attn_out_b, L1_attn_gate_w, L1_attn_gate_b, L1_attn_pos_bias, L1_attn_scale_embed, L1_attn_if_gain)
    h = _layernorm(x, axis=-1) * (1 + cb) + sb
    x = x + gb * _L1_ffn_ref(h, L1_ffn_Wr, L1_ffn_br, L1_ffn_W1, L1_ffn_b1, L1_ffn_W2, L1_ffn_b2)
    return x

_drawn_inputs = setup_inputs


def setup_inputs(seed=0):
    import zlib

    import numpy as np

    out = dict(_drawn_inputs(seed))
    spreads = {'L0_ffn_e_score_bias': (0.0, 0.8),
     'L1_attn_out_b': (0.0, 1.31),
     'L1_attn_gate_b': (0.0, 0.8),
     'L1_ffn_br': (0.0, 0.8),
     'L1_ffn_b1': (0.0, 0.8),
     'L1_ffn_b2': (0.0, 2.0)}
    factors = {'L0_attn_Wq': 8.0,
     'L0_attn_bq': 8.0,
     'L0_attn_Wk': 8.0,
     'L0_attn_bk': 8.0,
     'L0_attn_Wv': 8.0,
     'L0_attn_bv': 8.0,
     'L0_attn_Wo': 8.0,
     'L0_attn_bo': 8.0,
     'L0_ffn_router_weight': 8.0,
     'L0_ffn_gate_up_proj': 8.0,
     'L0_ffn_down_proj': 8.0,
     'L0_ffn_shared_gate_w': 8.0,
     'L0_ffn_shared_up_w': 8.0,
     'L0_ffn_shared_down_w': 8.0,
     'L0_c': 8.0,
     'L0_wmod': 8.0,
     'L1_attn_qkv_w': 8.0,
     'L1_attn_qkv_b': 8.0,
     'L1_attn_out_w': 8.0,
     'L1_attn_gate_w': 8.0,
     'L1_attn_pos_bias': 8.0,
     'L1_attn_scale_embed': 8.0,
     'L1_attn_if_gain': 8.0,
     'L1_ffn_Wr': 8.0,
     'L1_ffn_W1': 8.0,
     'L1_ffn_W2': 8.0}
    for name, (base, spread) in spreads.items():
        noise = np.random.default_rng([zlib.crc32(name.encode()), seed]).standard_normal(out[name].shape)
        drawn = base * np.exp(spread * noise) if base else spread * noise
        out[name] = jnp.asarray(drawn.astype(out[name].dtype))
    for name, factor in factors.items():
        out[name] = (out[name] * factor).astype(out[name].dtype)
    return out
```

```python
from contextlib import ExitStack

import numpy as np

import concourse.bass as bass
from concourse import mybir

ALU = mybir.AluOpType
ACT = mybir.ActivationFunctionType
AX_X = mybir.AxisListType.X
F32 = mybir.dt.float32
BF16 = mybir.dt.bfloat16

P = 128
B, L, D = 16, 256, 128
T = B * L
NT = T // P
TB = L // P
H, HD = 16, 8
HJ, HG = 4, 4
E0, I0, TOP_K = 32, 64, 6
PAIRS = E0 // 2
E1 = 8
CAP = T // E1
MT = 512
OFFSETS = sorted(set(range(33)) | {48, 64, 96, 128, 192})
NO = len(OFFSETS)
ORDER = OFFSETS[::-1]
PAD = max(OFFSETS)
EPS = 1e-5
NEG = -1e30
THETA = 10000.0
NORM_MIN = 1e-12


class Count:

    def __init__(self, base=0):
        self.base, self.n = base, 0

    def up(self, k=1):
        self.n += k
        return k

    def now(self):
        return self.base + self.n


def shape_constants():
    freqs = (THETA ** (-np.arange(0, HD, 2, dtype=np.float32) / HD)).astype(np.float32)
    ang = np.arange(L, dtype=np.float32)[:, None] * freqs
    cos = np.repeat(np.cos(ang), 2, axis=1)
    sin = np.repeat(np.sin(ang), 2, axis=1)
    sin[:, 0::2] *= -1
    q, k = np.arange(P)[:, None], np.arange(P)[None, :]
    later = np.where(k > q, NEG, 0.0).astype(np.float32)
    masks = np.stack([np.tile(later[:, None], (1, 4, 1)), np.tile(later.T[:, None], (1, 4, 1))], 1)
    n = np.arange(L).reshape(TB, P).T[:, :, None]
    early = np.where(n < np.array(ORDER)[None, None, :], NEG, 0.0).astype(np.float32)
    pair = np.zeros((96, PAIRS, P), np.float32)
    one = np.zeros((96, E1 + 1, P), np.float32)
    for part in range(3):
        for e in range(E0):
            pair[32 * part + e, e // 2, 64 * (e % 2):64 * (e % 2) + 64] = 1
        for e in range(E1):
            one[32 * part + e, e] = 1
            one[32 * part + e, E1] = 1
    return {
        "c_ident": np.eye(P, dtype=np.float32),
        "c_cos": np.tile(cos.T, (H, 1)).astype(np.float32),
        "c_sin": np.tile(sin.T, (H, 1)).astype(np.float32),
        "c_masks": masks,
        "c_early": early,
        "c_pair": pair,
        "c_one": one,
        "c_upto": np.triu(np.ones((P, P), np.float32)),
        "c_headsum": np.kron(np.eye(H, dtype=np.float32), np.ones((HD, 1), np.float32)),
    }


def build(nc, t, out):
    ctx = ExitStack()
    with ctx:
        def sb(name, shape, dt=F32):
            return ctx.enter_context(nc.sbuf_tensor(name, shape, dt))

        def sem(name):
            return ctx.enter_context(nc.semaphore(name))

        ps = ctx.enter_context(nc.psum_tensor("ps", [P, 8, 512], F32))

        s = {}
        s["ident"] = sb("ident", [P, P])
        s["identb"] = sb("identb", [P, P], BF16)
        s["x"] = sb("x", [P, NT, D])
        s["modT"] = sb("modT", [P, 2, 6, B])
        s["pm5"] = sb("pm5", [P, TB * 2])
        s["eps"] = sb("eps", [P, TB * 2])

        load_stream(nc, s, t, ps, sb, sem)
        attention0(nc, s, t, ps)
        experts0(nc, s, t, ps)
        attention1(nc, s, t, ps)
        experts1(nc, s, t, ps)
        store_stream(nc, s, out)


def load_stream(nc, s, t, ps, sb, sem):
    x, modT = s["x"], s["modT"]
    with ExitStack() as ctx:
        cT = ctx.enter_context(nc.sbuf_tensor("ls_cT", [P, 2, B], F32))
        sT = ctx.enter_context(nc.sbuf_tensor("ls_sT", [P, 2, B], F32))
        wm = ctx.enter_context(nc.sbuf_tensor("ls_wm", [P, 2, 6 * D], F32))
        g1 = ctx.enter_context(nc.sbuf_tensor("ls_g1", [P, 2, 2, B], F32))
        g2 = ctx.enter_context(nc.sbuf_tensor("ls_g2", [P, 2, 2, B], F32))
        loaded = ctx.enter_context(nc.semaphore("ls_loaded"))
        silu_done = ctx.enter_context(nc.semaphore("ls_silu"))
        mod_done = ctx.enter_context(nc.semaphore("ls_mod"))
        dve = ctx.enter_context(nc.semaphore("ls_dve"))
        block = ctx.enter_context(nc.Block())

        @block.sync
        def _(sp):
            sp.dma_start(cT[:], t["cT"]).then_inc(loaded, 16)
            sp.dma_start(wm[:], t["wmod"]).then_inc(loaded, 16)
            sp.dma_start(s["ident"][:], t["c_ident"]).then_inc(loaded, 16)
            sp.dma_start(x[:], t["L0_attn_x"].rearrange("b (k p) d -> p (b k) d", p=P)).then_inc(loaded, 16)

        @block.scalar
        def _(act):
            act.wait_ge(loaded, 64)
            nc.scalar.activation(sT[:], cT[:], ACT.Silu).then_inc(silu_done, 1)

        @block.tensor
        def _(pe):
            pe.wait_ge(silu_done, 1)
            for layer in range(2):
                for j in range(6):
                    mm = nc.tensor.matmul(ps[:, layer, j * B:(j + 1) * B], wm[:, layer, j * D:(j + 1) * D],
                                          sT[:, layer, :], start=True, stop=True)
            mm.then_inc(mod_done, 1)

        @block.vector
        def _(v):
            c = Count()
            v.wait_ge(loaded, 64)
            nc.vector.tensor_copy(s["identb"][:], s["ident"][:]).then_inc(dve, c.up())
            nc.vector.memset(s["pm5"][:], -0.5).then_inc(dve, c.up())
            nc.vector.memset(s["eps"][:], EPS).then_inc(dve, c.up())
            v.wait_ge(mod_done, 1)
            for layer in range(2):
                nc.vector.tensor_copy(modT[:, layer], ps[:, layer, 0:6 * B].rearrange("p (j b) -> p j b", b=B)
                                      ).then_inc(dve, c.up())
            v.wait_ge(dve, c.now())
            for layer in range(2):
                scales, gates = modT[:, layer, 1:6:3, :], modT[:, layer, 2:6:3, :]
                nc.vector.tensor_scalar(scales, scales, 1.0, None, ALU.add).then_inc(dve, c.up())
                nc.vector.tensor_scalar(g1[:, layer], gates, 0.0, 2.0, ALU.is_ge, ALU.mult).then_inc(dve, c.up())
                nc.vector.tensor_scalar(g2[:, layer], gates, -1.0, None, ALU.mult).then_inc(dve, c.up())
                v.wait_ge(dve, c.now())
                nc.vector.tensor_tensor(g2[:, layer], g2[:, layer], gates, ALU.max).then_inc(dve, c.up())
                v.wait_ge(dve, c.now())
                nc.vector.tensor_scalar(g2[:, layer], g2[:, layer], 0.25, None, ALU.max).then_inc(dve, c.up())
                v.wait_ge(dve, c.now())
                nc.vector.scalar_tensor_tensor(gates, g1[:, layer], -1.0, g2[:, layer], ALU.add, ALU.mult
                                               ).then_inc(dve, c.up())
                v.wait_ge(dve, c.now())


class Batch:

    def __init__(self, x, k):
        self.x, self.k = x, k

    def __add__(self, n):
        return Batch(self.x + n, self.k + n)


def hold(eng, sem, per, b, n):
    if per * b.k + n > 0:
        eng.wait_ge(sem, b.x * per + n)


def pipeline(eng, first, last, start, end, body, turns=3):
    passes = (end - start) // turns
    for k in range(first, start):
        body(Batch(k, k))
    with eng.Fori(0, passes) as i:
        for r in range(turns):
            body(Batch(i * turns + (start + r), start + r))
    for k in range(start + passes * turns, last):
        body(Batch(k, k))


def attention0(nc, s, t, ps):
    x, modT, ident, identb = s["x"], s["modT"], s["ident"], s["identb"]
    TERMS = [(0, 0), (0, 1), (0, 2), (1, 0), (1, 1), (2, 0)]
    ROWS = HD * len(TERMS)
    TOP = 64
    UN = 12
    with ExitStack() as ctx:
        def sb(name, shape, dt=F32):
            return ctx.enter_context(nc.sbuf_tensor("a0_" + name, shape, dt))

        def sem(name):
            return ctx.enter_context(nc.semaphore("a0_" + name))

        w = sb("w", [P, 6, D])
        bcol = sb("bcol", [P, 5])
        bvrow = sb("bvrow", [P, D])
        scale = sb("scale", [P, 1])
        cosq, sinq = sb("cosq", [P, L]), sb("sinq", [P, L])
        cosk, sink = sb("cosk", [P, L]), sb("sink", [P, L])
        maskf = sb("maskf", [P, 2, 4, P])
        mask = sb("mask", [P, 2, 4, P], BF16)
        gabo = sb("gabo", [P, B])
        ga, ca, sa = sb("ga", [P, 2]), sb("ca", [P, 1]), sb("sa", [P, 1])
        stat, mv, rstd = sb("stat", [P, TB, 6]), sb("mv", [P, TB, 2]), sb("rstd", [P, TB])
        y = sb("y", [P, TB, D])
        hT = sb("hT", [P, L])
        ra, rb = sb("ra", [P, 2, L]), sb("rb", [P, 2, L])
        parts = sb("parts", [P, 3, 2, L], BF16)
        vv = sb("vv", [P, 3, TB, H, 32])
        qs = sb("qs", [TOP + 3, 3, H, L], BF16)
        ks = sb("ks", [TOP + 3, 3, H, L], BF16)
        nmax = sb("nmax", [P, TB, HJ, HG])
        nT, nparts = sb("nT", [H, 2, L]), sb("nparts", [H, 3, L], BF16)
        pr = sb("pr", [P, 2, HJ, L + P])
        o = sb("o", [P, HG, L])
        rden = sb("rden", [P, TB, HG, HJ])
        on = sb("on", [P, TB, HJ, HG, HD])
        onT = sb("onT", [P, L])
        yo = sb("yo", [P, L])
        unit = sb("unit", [P, 1])
        parts_d = nc.dram_tensor("a0_parts_d", [P, 3, 2, L], BF16).ap()
        nparts_d = nc.dram_tensor("a0_nparts_d", [H, 3, L], BF16).ap()

        loaded, cleared, masks_done = sem("loaded"), sem("cleared"), sem("masks_done")
        stats_done, rstd_done, y_done = sem("stats_done"), sem("rstd_done"), sem("y_done")
        a_full, a_read = sem("a_full"), sem("a_read")
        rotated, summed, split = sem("rotated"), sem("summed"), sem("split")
        stored, spread = sem("stored"), sem("spread")
        m_full, m_read = sem("m_full"), sem("m_read")
        nT_full, nT_read = sem("nT_full"), sem("nT_read")
        nsplit, nstored, nspread = sem("nsplit"), sem("nstored"), sem("nspread")
        c_full, exp_done = sem("c_full"), sem("exp_done")
        pv_done, o_read = sem("pv_done"), sem("o_read")
        d_full, d_read = sem("d_full"), sem("d_read")
        dve_a, dve_d = sem("dve_a"), sem("dve_d")
        block = ctx.enter_context(nc.Block())
        A_STEPS, D_STEPS = 4, 5
        SPREAD = 16 * 2 * len(TERMS)

        def run(eng, order):
            ahead = {"D": -1, "C": 0, "M": 1, "N": 2, "S": 2, "A": 3}

            def body(b):
                for stage, step in order:
                    c = b + ahead[stage]
                    if 0 <= c.k < B:
                        step(c)
            pipeline(eng, -3, B + 1, 2, B - 3, body)

        @block.sync
        def _(sp):
            sp.dma_start(w[:], t["a0_w"]).then_inc(loaded, 16)
            sp.dma_start(bcol[:], t["a0_b"]).then_inc(loaded, 16)
            sp.dma_start(bvrow[:], t["L0_attn_bv"].partition_broadcast(P)).then_inc(loaded, 16)
            sp.dma_start(scale[:], t["L0_attn_scale"].partition_broadcast(P)).then_inc(loaded, 16)
            sp.dma_start(cosk[:], t["c_cos"]).then_inc(loaded, 16)
            sp.dma_start(sink[:], t["c_sin"]).then_inc(loaded, 16)
            sp.dma_start(maskf[:], t["c_masks"]).then_inc(loaded, 16)
            sp.wait_ge(cleared, 3)

            def spread_parts(b):
                sp.wait_ge(split, b.x + 1)
                sp.dma_start(parts_d, parts[:]).then_inc(stored, 16)
                sp.wait_ge(stored, b.x * 16 + 16)
                for n, (pq, pk) in enumerate(TERMS):
                    for dst, part, which in ((qs, pq, 0), (ks, pk, 1)):
                        sp.dma_start(dst[HD * n:HD * (n + 1), b.k % 3],
                                     parts_d[:, part, which, :].rearrange("(h d) n -> d h n", d=HD)
                                     ).then_inc(spread, 16)

            def spread_max(b):
                sp.wait_ge(nsplit, b.x * 4 + 4)
                sp.dma_start(nparts_d, nparts[:]).then_inc(nstored, 16)
                sp.wait_ge(nstored, b.x * 16 + 16)
                sp.dma_start(qs[TOP:TOP + 3, b.k % 3], nparts_d.rearrange("h t n -> t h n")).then_inc(nspread, 16)

            run(sp, [("S", spread_parts), ("M", spread_max)])

        @block.gpsimd
        def _(pool):
            nc.gpsimd.memset(qs[:], 0.0)
            nc.gpsimd.memset(unit[:], 1.0)
            nc.gpsimd.memset(ks[:], 0.0)
            nc.gpsimd.memset(vv[:], 0.0).then_inc(cleared, 1)
            pool.wait_ge(cleared, 1)
            nc.gpsimd.memset(ks[TOP:TOP + 3], 1.0).then_inc(cleared, 1)
            pool.wait_ge(cleared, 2)
            nc.gpsimd.memset(vv[:, :, :, :, HD], 1.0).then_inc(cleared, 1)

            def rstd_of(b):
                pool.wait_ge(stats_done, b.x + 1)
                nc.gpsimd.tensor_tensor(rstd[:], mv[:, :, 1], s["eps"][:, 0:TB], ALU.add).then_inc(rstd_done, 1)
                pool.wait_ge(rstd_done, b.x * 2 + 1)
                nc.gpsimd.tensor_tensor(rstd[:], rstd[:], s["pm5"][:, 0:TB], ALU.pow).then_inc(rstd_done, 1)

            def split_parts(b):
                pool.wait_ge(rotated, b.x * 2 + 2)
                pool.wait_ge(a_read, b.x * A_STEPS + 3)
                nc.gpsimd.tensor_tensor(ra[:], ra[:], rb[:], ALU.add).then_inc(summed, 1)
                pool.wait_ge(summed, b.x * 4 + 1)
                hold(pool, stored, 16, b, 0)
                nc.gpsimd.tensor_tensor(parts[:, 0], ra[:], unit[:].unsqueeze(2).to_broadcast([P, 2, L]), ALU.mult).then_inc(summed, 1)
                pool.wait_ge(summed, b.x * 4 + 2)
                nc.gpsimd.tensor_tensor(ra[:], ra[:], parts[:, 0], ALU.subtract).then_inc(summed, 1)
                pool.wait_ge(summed, b.x * 4 + 3)
                nc.gpsimd.tensor_tensor(parts[:, 1], ra[:], unit[:].unsqueeze(2).to_broadcast([P, 2, L]), ALU.mult).then_inc(summed, 1)

            def last_part(b):
                pool.wait_ge(summed, b.x * 4 + 4)
                hold(pool, spread, SPREAD, b, 0)
                hold(pool, c_full, UN, b + -2, 0)
                nc.gpsimd.tensor_tensor(parts[:, 2], ra[:], parts[:, 1], ALU.subtract).then_inc(split, 1)

            def split_max(b):
                pool.wait_ge(nT_read, b.x + 1)
                hold(pool, nspread, 16, b, 0)
                nc.gpsimd.tensor_tensor(nparts[:, 0], nT[:, 0], unit[0:H].to_broadcast([H, L]), ALU.mult).then_inc(nsplit, 1)
                pool.wait_ge(nsplit, b.x * 4 + 1)
                nc.gpsimd.tensor_tensor(nT[:, 1], nT[:, 0], nparts[:, 0], ALU.subtract).then_inc(nsplit, 1)
                pool.wait_ge(nsplit, b.x * 4 + 2)
                nc.gpsimd.tensor_tensor(nparts[:, 1], nT[:, 1], unit[0:H].to_broadcast([H, L]), ALU.mult).then_inc(nsplit, 1)
                pool.wait_ge(nsplit, b.x * 4 + 3)
                nc.gpsimd.tensor_tensor(nparts[:, 2], nT[:, 1], nparts[:, 1], ALU.subtract).then_inc(nsplit, 1)

            run(pool, [("S", last_part), ("A", rstd_of), ("M", split_max), ("A", split_parts)])

        @block.scalar
        def _(act):
            def modulate(b):
                hold(act, a_full, A_STEPS, b, 1)
                nc.scalar.activation(hT[:], ps[:, 6, 0:L], ACT.Identity, bias=sa[:], scale=ca[:]).then_inc(a_read, 1)

            def exps(g):
                def step(b):
                    hold(act, pv_done, HG, b, g - 1)
                    for n in range(3):
                        act.wait_ge(c_full, b.x * UN + 3 * g + n + 1)
                        bank = 2 + (3 * g + n) % 2
                        if n < 2:
                            dst, src = pr[:, g % 2, 2 * n:2 * n + 2, 0:L], ps[:, bank].rearrange("p (j n) -> p j n", j=2)
                        else:
                            dst, src = pr[:, g % 2, :, L:L + P], ps[:, bank].rearrange("p (j n) -> p j n", j=HJ)
                        nc.scalar.activation(dst, src, ACT.Exp).then_inc(exp_done, 1)
                return step

            def outputs(a):
                def step(b):
                    act.wait_ge(pv_done, b.x * HG + 2 * a + 2)
                    hold(act, d_full, D_STEPS, b, -3)
                    nc.scalar.activation(o[:, 2 * a:2 * a + 2], ps[:, 4 + a].rearrange("p (g n) -> p g n", n=L),
                                         ACT.Copy).then_inc(o_read, 1)
                return step

            def turned(b):
                act.wait_ge(d_full, b.x * D_STEPS + 3)
                nc.scalar.activation(onT[:], ps[:, 7, 0:L], ACT.Copy).then_inc(d_read, 1)

            def projected(b):
                act.wait_ge(d_full, b.x * D_STEPS + 4)
                nc.scalar.activation(yo[:], ps[:, 7, 0:L], ACT.Identity, bias=ga[:, 1:2], scale=ga[:, 0:1]
                                     ).then_inc(d_read, 1)

            run(act, [("C", exps(0)), ("D", outputs(1)), ("C", exps(1)), ("A", modulate), ("D", turned),
                      ("C", exps(2)), ("D", projected), ("C", outputs(0)), ("C", exps(3))])

        @block.tensor
        def _(pe):
            pe.wait_ge(cleared, 3)
            pe.wait_ge(masks_done, 1)

            def causal(out, form, n):
                nc.tensor.matmul(out, identb[:], mask[:, form, 0:n], start=True, stop=False, skip_group_check=True)

            def scores_c(g):
                def step(b):
                    p = b.k % 3
                    if g == 0:
                        pe.wait_ge(spread, b.x * SPREAD + SPREAD)
                        pe.wait_ge(nspread, b.x * 16 + 16)
                    for n in range(3):
                        hold(pe, exp_done, UN, b, 3 * g + n - 1)
                        bank = ps[:, 2 + (3 * g + n) % 2]
                        if n < 2:
                            blocks = bank.rearrange("p (j n) -> p j n", j=2)
                            causal(blocks[:, :, 0:P], 1, 2)
                            for a in range(2):
                                h = HG * (2 * n + a) + g
                                mm = nc.tensor.matmul(blocks[:, a], ks[:, p, h, 0:P], qs[:, p, h, :],
                                                      start=False, stop=(a == 1), skip_group_check=True)
                        else:
                            blocks = bank.rearrange("p (j n) -> p j n", j=HJ)
                            causal(blocks, 1, HJ)
                            for j in range(HJ):
                                h = HG * j + g
                                mm = nc.tensor.matmul(blocks[:, j], ks[:, p, h, P:L], qs[:, p, h, P:L],
                                                      start=False, stop=(j == HJ - 1), skip_group_check=True)
                        mm.then_inc(c_full, 1)
                return step

            def scores_m(g):
                def step(b):
                    p = b.k % 3
                    if g == 0:
                        pe.wait_ge(spread, b.x * SPREAD + SPREAD)
                    for n in range(3):
                        hold(pe, m_read, UN, b, 3 * g + n - 1)
                        bank = ps[:, (3 * g + n) % 2]
                        if n < 2:
                            blocks = bank.rearrange("p (j n) -> p j n", j=2)
                            causal(blocks[:, :, P:L], 0, 2)
                            for a in range(2):
                                h = HG * (2 * n + a) + g
                                mm = nc.tensor.matmul(blocks[:, a], qs[0:ROWS, p, h, P:L], ks[0:ROWS, p, h, :],
                                                      start=False, stop=(a == 1), skip_group_check=True)
                        else:
                            blocks = bank.rearrange("p (j n) -> p j n", j=HJ)
                            causal(blocks, 0, HJ)
                            for j in range(HJ):
                                h = HG * j + g
                                mm = nc.tensor.matmul(blocks[:, j], qs[0:ROWS, p, h, 0:P], ks[0:ROWS, p, h, 0:P],
                                                      start=False, stop=(j == HJ - 1), skip_group_check=True)
                        mm.then_inc(m_full, 1)
                return step

            def turn_max(b):
                pe.wait_ge(m_read, b.x * UN + UN)
                hold(pe, d_read, D_STEPS, b + -1, 0)
                for k in range(TB):
                    mm = nc.tensor.transpose(ps[0:H, 7, k * P:(k + 1) * P],
                                             nmax[:, k].rearrange("p j g -> p (j g)"), ident[:])
                mm.then_inc(nT_full, 1)

            def outputs(g):
                def step(b):
                    pe.wait_ge(exp_done, b.x * UN + 3 * g + 3)
                    if g == 0:
                        pe.wait_ge(a_read, b.x * A_STEPS + A_STEPS)
                    if g % 2 == 0:
                        hold(pe, o_read, 2, b, g // 2 - 1)
                    for j in range(HJ):
                        h = HG * j + g
                        oo = ps[32 * j:32 * j + 32, 4 + g // 2, (g % 2) * L:(g % 2 + 1) * L]
                        nc.tensor.matmul(oo, vv[:, b.k % 3, 0, h, :], pr[:, g % 2, j, 0:L], start=True, stop=False,
                                         skip_group_check=True, tile_position=(0, 32 * j))
                        mm = nc.tensor.matmul(oo[:, P:L], vv[:, b.k % 3, 1, h, :], pr[:, g % 2, j, L:L + P],
                                              start=False, stop=True, skip_group_check=True,
                                              tile_position=(0, 32 * j))
                    mm.then_inc(pv_done, 1)
                return step

            def turn_tokens(b):
                hold(pe, a_read, A_STEPS, b, 0)
                pe.wait_ge(y_done, b.x + 1)
                for k in range(TB):
                    mm = nc.tensor.transpose(ps[:, 6, k * P:(k + 1) * P], y[:, k, :], ident[:])
                mm.then_inc(a_full, 1)

            def project(which):
                def step(b):
                    pe.wait_ge(a_read, b.x * A_STEPS + which + 1)
                    if which < 2:
                        for k in range(2):
                            mm = nc.tensor.matmul(ps[:, 6, k * L:(k + 1) * L], w[:, 2 * which + k, :], hT[:],
                                                  start=True, stop=True)
                    else:
                        for k in range(TB):
                            mm = nc.tensor.matmul(ps[:, 6, k * P:(k + 1) * P], hT[:, k * P:(k + 1) * P], w[:, 4, :],
                                                  start=True, stop=True)
                    mm.then_inc(a_full, 1)
                return step

            def turn_outputs(k):
                def step(b):
                    if k == 0:
                        pe.wait_ge(o_read, b.x * 2 + 2)
                        hold(pe, d_read, D_STEPS, b, 0)
                        pe.wait_ge(nT_read, b.x + 2 if b.k + 2 <= B else B)
                    else:
                        pe.wait_ge(d_read, b.x * D_STEPS + 1)
                    for g in range(HG):
                        mm = nc.tensor.transpose(ps[:, 7, g * P:(g + 1) * P], o[:, g, k * P:(k + 1) * P], ident[:])
                    mm.then_inc(d_full, 1)
                return step

            def turn_normal(b):
                pe.wait_ge(d_read, b.x * D_STEPS + 2)
                for k in range(TB):
                    mm = nc.tensor.transpose(ps[:, 7, k * P:(k + 1) * P], on[:, k].rearrange("p j g d -> p (j g d)"),
                                             ident[:])
                mm.then_inc(d_full, 1)

            def project_out(b):
                pe.wait_ge(d_read, b.x * D_STEPS + 3)
                nc.tensor.matmul(ps[:, 7, 0:L], w[:, 5, :], onT[:], start=True, stop=True).then_inc(d_full, 1)

            def turn_back(b):
                pe.wait_ge(d_read, b.x * D_STEPS + 4)
                for k in range(TB):
                    mm = nc.tensor.transpose(ps[:, 7, k * P:(k + 1) * P], yo[:, k * P:(k + 1) * P], ident[:])
                mm.then_inc(d_full, 1)

            run(pe, [("C", scores_c(0)), ("D", outputs(3)), ("M", scores_m(1)), ("S", project(2)),
                     ("D", turn_outputs(0)), ("M", scores_m(2)), ("A", turn_tokens), ("D", turn_outputs(1)),
                     ("C", scores_c(1)), ("C", outputs(0)), ("D", turn_normal), ("M", scores_m(3)),
                     ("A", project(0)), ("D", project_out), ("C", scores_c(2)), ("C", outputs(1)),
                     ("D", turn_back), ("M", turn_max), ("A", project(1)), ("N", scores_m(0)),
                     ("C", scores_c(3)), ("C", outputs(2))])

        @block.vector
        def _(v):
            v.wait_ge(loaded, 112)
            nc.vector.tensor_scalar(cosq[:], cosk[:], scale[:], None, ALU.mult)
            nc.vector.tensor_scalar(sinq[:], sink[:], scale[:], None, ALU.mult)
            nc.vector.tensor_scalar(gabo[:], modT[:, 0, 2, :], bcol[:, 4:5], None, ALU.mult)
            nc.vector.tensor_copy(mask[:], maskf[:]).then_inc(masks_done, 1)
            v.wait_ge(masks_done, 1)
            v.wait_ge(cleared, 3)

            def statistics(b):
                for k in range(TB):
                    nc.vector.bn_stats(stat[:, k, :], x[:, bass.ds(b.x * TB + k, 1), :].rearrange("p a d -> p (a d)")
                                       ).then_inc(dve_a, 1)
                v.wait_ge(dve_a, b.x * TB + TB)
                hold(v, a_read, A_STEPS, b, 0)
                nc.vector.tensor_copy(ca[:], modT[:, 0, 1, bass.ds(b.x, 1)])
                nc.vector.tensor_copy(sa[:], modT[:, 0, 0, bass.ds(b.x, 1)])
                for k in range(TB):
                    n = nc.vector.bn_aggr(mv[:, k, :], stat[:, k, :])
                n.then_inc(stats_done, 1)

            def normalise(b):
                v.wait_ge(rstd_done, b.x * 2 + 2)
                for k in range(TB):
                    n = nc.vector.tensor_scalar(y[:, k, :], x[:, bass.ds(b.x * TB + k, 1), :].rearrange("p a d -> p (a d)"),
                                                mv[:, k, 0:1], rstd[:, k:k + 1], ALU.subtract, ALU.mult)
                n.then_inc(y_done, 1)

            def rotate(which):
                def step(b):
                    cs, sn = ((cosq, sinq), (cosk, sink))[which]
                    if which == 0:
                        hold(v, split, 1, b, 0)
                    v.wait_ge(a_full, b.x * A_STEPS + 2 + which)
                    nc.vector.scalar_tensor_tensor(ra[:, which, :], ps[:, 6, 0:L], bcol[:, 2 * which:2 * which + 1],
                                                   cs[:], ALU.add, ALU.mult).then_inc(rotated, 1)
                    nc.vector.scalar_tensor_tensor(rb[:, which, :], ps[:, 6, L:2 * L],
                                                   bcol[:, 2 * which + 1:2 * which + 2], sn[:],
                                                   ALU.add, ALU.mult).then_inc(a_read, 1)
                return step

            def values(b):
                v.wait_ge(a_full, b.x * A_STEPS + 4)
                for k in range(TB):
                    n = nc.vector.tensor_tensor(vv[:, b.k % 3, k, :, 0:HD],
                                                ps[:, 6, k * P:(k + 1) * P].rearrange("p (h d) -> p h d", d=HD),
                                                bvrow[:].rearrange("p (h d) -> p h d", d=HD), ALU.add)
                n.then_inc(a_read, 1)

            def maxima(g):
                def step(b):
                    for n in range(3):
                        v.wait_ge(m_full, b.x * UN + 3 * g + n + 1)
                        bank = ps[:, (3 * g + n) % 2]
                        if n < 2:
                            dst, src = nmax[:, 1, 2 * n:2 * n + 2, g], bank.rearrange("p (j n) -> p j n", j=2)
                        else:
                            dst, src = nmax[:, 0, :, g], bank.rearrange("p (j n) -> p j n", j=HJ)
                        nc.vector.tensor_reduce(dst, src, AX_X, ALU.max, negate=True).then_inc(m_read, 1)
                return step

            def take_max(b):
                v.wait_ge(nT_full, b.x + 1)
                hold(v, nsplit, 4, b, 0)
                nc.vector.tensor_copy(nT[:, 0], ps[0:H, 7, 0:L]).then_inc(nT_read, 1)

            def divide(k):
                def step(b):
                    oT = ps[:, 7].rearrange("p (g j r) -> p g j r", g=HG, j=HJ)
                    v.wait_ge(d_full, b.x * D_STEPS + 1 + k)
                    nc.vector.reciprocal(rden[:, k], oT[:, :, :, HD]).then_inc(dve_d, 1)
                    if k == 0:
                        nc.vector.tensor_copy(ga[:, 0:1], modT[:, 0, 2, bass.ds(b.x, 1)])
                        nc.vector.tensor_copy(ga[:, 1:2], gabo[:, bass.ds(b.x, 1)])
                    v.wait_ge(dve_d, b.x * TB + k + 1)
                    nc.vector.tensor_tensor(on[:, k].rearrange("p j g d -> p g j d"), oT[:, :, :, 0:HD],
                                            rden[:, k].unsqueeze(3).to_broadcast([P, HG, HJ, HD]), ALU.mult
                                            ).then_inc(d_read, 1)
                return step

            def residual(b):
                v.wait_ge(d_full, b.x * D_STEPS + 5)
                xs = x[:, bass.ds(b.x * TB, TB), :]
                nc.vector.tensor_tensor(xs, xs, ps[:, 7, 0:L].rearrange("p (k d) -> p k d", d=D), ALU.add
                                        ).then_inc(d_read, 1)

            run(v, [("M", maxima(1)), ("S", values), ("A", statistics), ("D", divide(0)), ("M", maxima(2)),
                    ("A", normalise), ("D", divide(1)), ("M", maxima(3)), ("A", rotate(0)), ("D", residual),
                    ("M", take_max), ("A", rotate(1)), ("N", maxima(0))])


def experts0(nc, s, t, ps):
    x, modT, ident = s["x"], s["modT"], s["ident"]
    NI, K, UNITS = T // MT, MT // P, PAIRS + 1
    HALVES = MT // L
    with ExitStack() as ctx:
        def sb(name, shape, dt=F32):
            return ctx.enter_context(nc.sbuf_tensor("e0_" + name, shape, dt))

        def sem(name):
            return ctx.enter_context(nc.semaphore("e0_" + name))

        wg, wu, wd = sb("wg", [P, UNITS, P]), sb("wu", [P, UNITS, P]), sb("wd", [P, UNITS, D])
        wr = sb("wr", [P, E0])
        bias = sb("bias", [P, E0])
        pairf, pair = sb("pairf", [96, PAIRS, P]), sb("pair", [96, PAIRS, P], BF16)
        gb, cb, sbb = sb("gb", [P, HALVES]), sb("cb", [P, HALVES]), sb("sb", [P, HALVES])
        stat, mv, rstd = sb("stat", [P, K, 6]), sb("mv", [P, K, 2]), sb("rstd", [P, K])
        y, hT = sb("y", [P, K, D]), sb("hT", [P, MT])
        mx, ex, den, rw = sb("mx", [P, K]), sb("ex", [P, K, E0]), sb("den", [P, K]), sb("rw", [P, K, E0])
        cor = sb("cor", [P, K, E0 + 2])
        top, rep, sel = sb("top", [P, K, 8]), sb("rep", [P, K, E0 + 2]), sb("sel", [P, K, E0])
        rest, c3 = sb("rest", [E0, 2, MT]), sb("c3", [96, MT], BF16)
        sg, hm = sb("sg", [P, 2, MT]), sb("hm", [P, 2, MT])
        pause = sb("pause", [P, 1])
        up = sb("up", [P, 2, MT])
        yo = sb("yo", [P, MT])

        loaded = sem("loaded")
        stats_done, rstd_done, y_done, mod_done = sem("stats_done"), sem("rstd_done"), sem("y_done"), sem("mod_done")
        small_full, small_free = sem("small_full"), sem("small_free")
        logits_done, exp_done, comb_done, split_done = sem("logits"), sem("exp"), sem("comb"), sem("split")
        unit_full = sem("unit_full")
        silu_done = sem("silu_done")
        hidden_done = sem("hidden_done")
        down_done = sem("down_done")
        up_done = sem("up_done")
        sum_read, dve, setup = sem("sum_read"), sem("dve"), sem("setup")
        block = ctx.enter_context(nc.Block())
        DVE, SMALL = 25, 4

        @block.sync
        def _(sp):
            for dst, name in ((wg, "e0_wg"), (wu, "e0_wu"), (wd, "e0_wd"), (wr, "e0_wr"), (pairf, "c_pair")):
                sp.dma_start(dst[:], t[name]).then_inc(loaded, 16)
            sp.dma_start(bias[:], t["L0_ffn_e_score_bias"].partition_broadcast(P)).then_inc(loaded, 16)

        @block.gpsimd
        def _(pool):
            with pool.Fori(0, NI) as i:
                pool.wait_ge(stats_done, i + 1)
                nc.gpsimd.tensor_tensor(rstd[:], mv[:, :, 1], s["eps"][:, 0:K], ALU.add).then_inc(rstd_done, 1)
                pool.wait_ge(rstd_done, i * 2 + 1)
                nc.gpsimd.tensor_tensor(rstd[:], rstd[:], s["pm5"][:, 0:K], ALU.pow).then_inc(rstd_done, 1)

        @block.scalar
        def _(act):
            with act.Fori(0, NI) as i:
                act.wait_ge(mod_done, i + 1)
                act.wait_ge(small_full, i * SMALL + 1)
                for k in range(HALVES):
                    a = nc.scalar.activation(hT[:, k * L:(k + 1) * L], ps[:, 1, k * L:(k + 1) * L], ACT.Identity,
                                             bias=sbb[:, k:k + 1], scale=cb[:, k:k + 1])
                a.then_inc(small_free, 1)
                act.wait_ge(logits_done, i + 1)
                nc.scalar.activation(ex[:], ex[:], ACT.Exp).then_inc(exp_done, 1)
                for u in range(UNITS):
                    act.wait_ge(unit_full, i * UNITS + u + 1)
                    if u >= 2:
                        act.wait_ge(hidden_done, i * UNITS + u - 1)
                    nc.scalar.activation(sg[:, u % 2], ps[:, 2 + u % 2], ACT.Silu).then_inc(silu_done, 1)
                act.wait_ge(down_done, (i + 1) * UNITS)
                for k in range(HALVES):
                    a = nc.scalar.activation(yo[:, k * L:(k + 1) * L], ps[:, 0, k * L:(k + 1) * L], ACT.Copy,
                                             scale=gb[:, k:k + 1])
                a.then_inc(sum_read, 1)

        @block.tensor
        def _(pe):
            pe.wait_ge(setup, 1)
            with pe.Fori(0, NI) as i:
                pe.wait_ge(small_free, i * SMALL + 1)
                pe.wait_ge(y_done, i + 1)
                for k in range(K):
                    mm = nc.tensor.transpose(ps[:, 1, k * P:(k + 1) * P], y[:, k, :], ident[:])
                mm.then_inc(small_full, 1)
                pe.wait_ge(small_free, i * SMALL + 2)
                for k in range(K):
                    mm = nc.tensor.matmul(ps[:, 1, k * E0:(k + 1) * E0], hT[:, k * P:(k + 1) * P], wr[:],
                                          start=True, stop=True)
                mm.then_inc(small_full, 1)
                for u in range(UNITS + 1):
                    if u < UNITS:
                        if u >= 2:
                            pe.wait_ge(hidden_done, i * UNITS + u - 1)
                        nc.tensor.matmul(ps[:, 2 + u % 2, :], wg[:, u, :], hT[:], start=True, stop=True)
                        mm = nc.tensor.matmul(ps[:, 4 + u % 2, :], wu[:, u, :], hT[:], start=True, stop=True)
                        if u == 1:
                            pe.wait_ge(small_free, i * SMALL + 3)
                            pe.wait_ge(comb_done, i + 1)
                            for k in range(K):
                                tr = nc.tensor.transpose(ps[0:E0, 1, k * P:(k + 1) * P], sel[:, k, :], ident[:])
                            tr.then_inc(small_full, 1)
                            pe.wait_ge(split_done, i + 1)
                        if u >= 1:
                            mm = nc.tensor.matmul(ps[:, 6 + u % 2, :], pair[:, u - 1, :], c3[:], start=True, stop=True)
                        mm.then_inc(unit_full, 1)
                    if u >= 1:
                        pe.wait_ge(hidden_done, i * UNITS + u)
                        nc.tensor.matmul(ps[:, 0, :], wd[:, u - 1, :], hm[:, (u - 1) % 2, :],
                                         start=(u == 1), stop=(u == UNITS), skip_group_check=True
                                         ).then_inc(down_done, 1)
                pe.wait_ge(sum_read, i + 1)
                pe.wait_ge(small_free, i * SMALL + 4)
                for k in range(K):
                    mm = nc.tensor.transpose(ps[:, 1, k * P:(k + 1) * P], yo[:, k * P:(k + 1) * P], ident[:])
                mm.then_inc(small_full, 1)

        @block.vector
        def _(v):
            v.wait_ge(loaded, 96)
            nc.vector.memset(cor[:], NEG)
            nc.vector.tensor_copy(pair[:], pairf[:]).then_inc(setup, 1)
            nc.vector.memset(mx[:], 0.0).then_inc(small_free, 1)
            v.wait_ge(small_free, 1)
            with v.Fori(0, NI) as i:
                c = Count(i * DVE)
                for k in range(K):
                    nc.vector.bn_stats(stat[:, k, :], x[:, bass.ds(i * K + k, 1), :].rearrange("p a d -> p (a d)")
                                       ).then_inc(dve, c.up())
                v.wait_ge(dve, c.now())
                nc.vector.tensor_copy(gb[:], modT[:, 0, 5, bass.ds(i * HALVES, HALVES)])
                nc.vector.tensor_copy(cb[:], modT[:, 0, 4, bass.ds(i * HALVES, HALVES)])
                nc.vector.tensor_copy(sbb[:], modT[:, 0, 3, bass.ds(i * HALVES, HALVES)]).then_inc(mod_done, 1)
                for k in range(K):
                    n = nc.vector.bn_aggr(mv[:, k, :], stat[:, k, :])
                n.then_inc(stats_done, 1)
                v.wait_ge(rstd_done, i * 2 + 2)
                for k in range(K):
                    n = nc.vector.tensor_scalar(y[:, k, :], x[:, bass.ds(i * K + k, 1), :].rearrange("p a d -> p (a d)"),
                                                mv[:, k, 0:1], rstd[:, k:k + 1], ALU.subtract, ALU.mult)
                n.then_inc(y_done, 1)
                v.wait_ge(small_full, i * SMALL + 2)
                lg = ps[:, 1, 0:K * E0].rearrange("p (k e) -> p k e", e=E0)
                wide = [P, K, E0]
                nc.vector.tensor_reduce(mx[:], lg, AX_X, ALU.max).then_inc(dve, c.up())
                v.wait_ge(dve, c.now())
                nc.vector.tensor_tensor(ex[:], lg, mx[:].unsqueeze(2).to_broadcast(wide), ALU.subtract
                                        ).then_inc(logits_done, 1)
                v.wait_ge(exp_done, i + 1)
                nc.vector.tensor_reduce(den[:], ex[:], AX_X, ALU.add).then_inc(dve, c.up())
                v.wait_ge(dve, c.now())
                nc.vector.reciprocal(den[:], den[:]).then_inc(dve, c.up())
                v.wait_ge(dve, c.now())
                nc.vector.tensor_tensor(rw[:], ex[:], den[:].unsqueeze(2).to_broadcast(wide), ALU.mult
                                        ).then_inc(dve, c.up())
                v.wait_ge(dve, c.now())
                nc.vector.tensor_tensor(cor[:, :, 0:E0], rw[:], bias[:].unsqueeze(1).to_broadcast(wide), ALU.add
                                        ).then_inc(dve, c.up())
                v.wait_ge(dve, c.now())
                nc.vector.memset(pause[:], 0.0)
                for k in range(K):
                    nc.vector.max(top[:, k, :], cor[:, k, :]).then_inc(dve, c.up())
                v.wait_ge(dve, c.now())
                nc.vector.memset(top[:, :, TOP_K:8], NEG).then_inc(dve, c.up())
                v.wait_ge(dve, c.now())
                nc.vector.memset(pause[:], 0.0)
                for k in range(K):
                    nc.vector.match_replace(rep[:, k, :], top[:, k, :], cor[:, k, :], -NEG).then_inc(dve, c.up())
                v.wait_ge(dve, c.now())
                nc.vector.tensor_tensor(sel[:], rep[:, :, 0:E0], cor[:, :, 0:E0], ALU.not_equal).then_inc(dve, c.up())
                v.wait_ge(dve, c.now())
                nc.vector.tensor_tensor(sel[:], sel[:], rw[:], ALU.mult).then_inc(dve, c.up())
                v.wait_ge(dve, c.now())
                nc.vector.tensor_reduce(den[:], sel[:], AX_X, ALU.add).then_inc(dve, c.up())
                v.wait_ge(dve, c.now())
                nc.vector.tensor_scalar(den[:], den[:], NORM_MIN, None, ALU.max).then_inc(dve, c.up())
                v.wait_ge(dve, c.now())
                nc.vector.reciprocal(den[:], den[:]).then_inc(small_free, 1)
                v.wait_ge(small_free, i * SMALL + 3)
                nc.vector.tensor_tensor(sel[:], sel[:], den[:].unsqueeze(2).to_broadcast(wide), ALU.mult
                                        ).then_inc(comb_done, 1)
                v.wait_ge(small_full, i * SMALL + 3)
                cT = ps[0:E0, 1, :]
                nc.vector.tensor_copy(c3[0:E0, :], cT).then_inc(dve, c.up())
                v.wait_ge(dve, c.now())
                nc.vector.tensor_tensor(rest[:, 0, :], cT, c3[0:E0, :], ALU.subtract).then_inc(dve, c.up())
                v.wait_ge(dve, c.now())
                nc.vector.tensor_copy(c3[E0:2 * E0, :], rest[:, 0, :]).then_inc(dve, c.up())
                v.wait_ge(dve, c.now())
                nc.vector.tensor_tensor(rest[:, 1, :], rest[:, 0, :], c3[E0:2 * E0, :], ALU.subtract
                                        ).then_inc(small_free, 1)
                v.wait_ge(small_free, i * SMALL + 4)
                nc.vector.tensor_copy(c3[2 * E0:3 * E0, :], rest[:, 1, :]).then_inc(split_done, 1)
                for u in range(UNITS):
                    v.wait_ge(silu_done, i * UNITS + u + 1)
                    if u >= 2:
                        v.wait_ge(down_done, i * UNITS + u - 1)
                    if u == 0:
                        nc.vector.tensor_tensor(hm[:, 0], sg[:, 0], ps[:, 4], ALU.mult).then_inc(hidden_done, 1)
                        continue
                    nc.vector.tensor_tensor(up[:, u % 2], sg[:, u % 2], ps[:, 4 + u % 2], ALU.mult
                                            ).then_inc(up_done, 1)
                    v.wait_ge(up_done, i * PAIRS + u)
                    nc.vector.tensor_tensor(hm[:, u % 2], up[:, u % 2], ps[:, 6 + u % 2], ALU.mult
                                            ).then_inc(hidden_done, 1)
                v.wait_ge(small_full, i * SMALL + 4)
                xs = x[:, bass.ds(i * K, K), :]
                nc.vector.tensor_tensor(xs, xs, ps[:, 1, :].rearrange("p (k d) -> p k d", d=D), ALU.add
                                        ).then_inc(small_free, 1)
                assert c.n == DVE, c.n


def experts1(nc, s, t, ps):
    x, modT, ident = s["x"], s["modT"], s["ident"]
    NI, K = T // MT, MT // P
    HALVES = MT // L
    with ExitStack() as ctx:
        def sb(name, shape, dt=F32):
            return ctx.enter_context(nc.sbuf_tensor("e1_" + name, shape, dt))

        def sem(name):
            return ctx.enter_context(nc.semaphore("e1_" + name))

        w1, w2 = sb("w1", [P, E1, D]), sb("w2", [P, E1, D])
        b1, b2 = sb("b1", [P, E1]), sb("b2", [E1, D])
        wr, br = sb("wr", [P, E1]), sb("br", [P, E1])
        rank = sb("rank", [P, E1])
        onef, one = sb("onef", [96, E1 + 1, P]), sb("one", [96, E1 + 1, P], BF16)
        uptof, upto, ones = sb("uptof", [P, P]), sb("upto", [P, P], BF16), sb("ones", [P, P], BF16)
        gb, cb, sbb = sb("gb", [P, HALVES]), sb("cb", [P, HALVES]), sb("sb", [P, HALVES])
        stat, mv, rstd = sb("stat", [P, K, 6]), sb("mv", [P, K, 2]), sb("rstd", [P, K])
        y, hT, hg = sb("y", [P, K, D]), sb("hT", [P, MT]), sb("hg", [P, MT])
        lg, mx, den = sb("lg", [P, K, E1]), sb("mx", [P, K]), sb("den", [P, K])
        ex, oh, wt = sb("ex", [P, K, E1]), sb("oh", [P, K, E1]), sb("wt", [P, K, E1])
        gate = sb("gate", [P, K])
        ohb = sb("ohb", [P, K, E1], BF16)
        before = sb("before", [P, K + 1, E1])
        beforeb = sb("beforeb", [P, K, E1], BF16)
        rest, c3, wT = sb("rest", [E1, 2, MT]), sb("c3", [96, MT], BF16), sb("wT", [E1, MT])
        r, hm = sb("r", [P, 2, MT]), sb("hm", [P, 2, MT])
        yo = sb("yo", [P, MT])

        loaded = sem("loaded")
        stats_done, rstd_done, y_done, mod_done = sem("stats_done"), sem("rstd_done"), sem("y_done"), sem("mod_done")
        small_full, small_free = sem("small_full"), sem("small_free")
        logits_done, exp_done, chosen, w_done = sem("logits"), sem("exp"), sem("chosen"), sem("w_done")
        counted, split_done = sem("counted"), sem("split")
        sum_full, hg_done = sem("sum_full"), sem("hg_done")
        unit_full, relu_done, hidden_done = sem("unit_full"), sem("relu_done"), sem("hidden_done")
        down_done = sem("down_done")
        out_read, dve, setup = sem("out_read"), sem("dve"), sem("setup")
        block = ctx.enter_context(nc.Block())
        DVE, SMALL = 25, 4

        @block.sync
        def _(sp):
            for dst, name in ((w1, "e1_w1"), (w2, "e1_w2"), (b1, "e1_b1"), (b2, "L1_ffn_b2"), (wr, "L1_ffn_Wr"),
                              (onef, "c_one"), (uptof, "c_upto")):
                sp.dma_start(dst[:], t[name]).then_inc(loaded, 16)
            sp.dma_start(br[:], t["L1_ffn_br"].partition_broadcast(P)).then_inc(loaded, 16)

        @block.gpsimd
        def _(pool):
            with pool.Fori(0, NI) as i:
                pool.wait_ge(stats_done, i + 1)
                nc.gpsimd.tensor_tensor(rstd[:], mv[:, :, 1], s["eps"][:, 0:K], ALU.add).then_inc(rstd_done, 1)
                pool.wait_ge(rstd_done, i * 2 + 1)
                nc.gpsimd.tensor_tensor(rstd[:], rstd[:], s["pm5"][:, 0:K], ALU.pow).then_inc(rstd_done, 1)

        @block.scalar
        def _(act):
            with act.Fori(0, NI) as i:
                act.wait_ge(mod_done, i + 1)
                act.wait_ge(small_full, i * SMALL + 1)
                for k in range(HALVES):
                    a = nc.scalar.activation(hT[:, k * L:(k + 1) * L], ps[:, 1, k * L:(k + 1) * L], ACT.Identity,
                                             bias=sbb[:, k:k + 1], scale=cb[:, k:k + 1])
                a.then_inc(small_free, 1)
                act.wait_ge(logits_done, i + 1)
                nc.scalar.activation(ex[:], ex[:], ACT.Exp).then_inc(exp_done, 1)
                for u in range(E1):
                    act.wait_ge(unit_full, i * E1 + u + 1)
                    if u >= 2:
                        act.wait_ge(hidden_done, i * E1 + u - 1)
                    nc.scalar.activation(r[:, u % 2], ps[:, 2 + u % 2], ACT.Relu, bias=b1[:, u:u + 1]
                                         ).then_inc(relu_done, 1)
                act.wait_ge(down_done, (i + 1) * E1)
                for k in range(HALVES):
                    a = nc.scalar.activation(yo[:, k * L:(k + 1) * L], ps[:, 0, k * L:(k + 1) * L], ACT.Copy,
                                             scale=gb[:, k:k + 1])
                a.then_inc(out_read, 1)

        @block.tensor
        def _(pe):
            pe.wait_ge(setup, 1)
            with pe.Fori(0, NI) as i:
                pe.wait_ge(small_free, i * SMALL + 1)
                pe.wait_ge(y_done, i + 1)
                for k in range(K):
                    mm = nc.tensor.transpose(ps[:, 1, k * P:(k + 1) * P], y[:, k, :], ident[:])
                mm.then_inc(small_full, 1)
                pe.wait_ge(small_free, i * SMALL + 2)
                for k in range(K):
                    mm = nc.tensor.matmul(ps[:, 1, k * E1:(k + 1) * E1], hT[:, k * P:(k + 1) * P], wr[:],
                                          start=True, stop=True)
                mm.then_inc(small_full, 1)
                pe.wait_ge(chosen, i + 1)
                nc.tensor.matmul(ps[:, 7, 0:K * E1], upto[:], ohb[:].rearrange("p k e -> p (k e)"),
                                 start=True, stop=False)
                nc.tensor.matmul(ps[:, 7, 0:K * E1], ones[:], beforeb[:].rearrange("p k e -> p (k e)"),
                                 start=False, stop=True).then_inc(counted, 1)
                pe.wait_ge(w_done, i + 1)
                pe.wait_ge(small_free, i * SMALL + 3)
                for k in range(K):
                    mm = nc.tensor.transpose(ps[0:E1, 1, k * P:(k + 1) * P], wt[:, k, :], ident[:])
                mm.then_inc(small_full, 1)
                pe.wait_ge(split_done, i + 1)
                nc.tensor.matmul(ps[:, 6, :], one[:, E1, :], c3[:], start=True, stop=True).then_inc(sum_full, 1)
                nc.tensor.matmul(ps[:, 0, :], b2[:], wT[:], start=True, stop=False, skip_group_check=True)
                pe.wait_ge(hg_done, i + 1)
                for u in range(E1 + 1):
                    if u < E1:
                        if u >= 2:
                            pe.wait_ge(hidden_done, i * E1 + u - 1)
                        nc.tensor.matmul(ps[:, 2 + u % 2, :], w1[:, u, :], hg[:], start=True, stop=True)
                        nc.tensor.matmul(ps[:, 4 + u % 2, :], one[:, u, :], c3[:], start=True, stop=True
                                         ).then_inc(unit_full, 1)
                    if u >= 1:
                        pe.wait_ge(hidden_done, i * E1 + u)
                        nc.tensor.matmul(ps[:, 0, :], w2[:, u - 1, :], hm[:, (u - 1) % 2, :],
                                         start=False, stop=(u == E1), skip_group_check=True).then_inc(down_done, 1)
                pe.wait_ge(out_read, i + 1)
                pe.wait_ge(small_free, i * SMALL + 4)
                for k in range(K):
                    mm = nc.tensor.transpose(ps[:, 1, k * P:(k + 1) * P], yo[:, k * P:(k + 1) * P], ident[:])
                mm.then_inc(small_full, 1)

        @block.vector
        def _(v):
            v.wait_ge(loaded, 128)
            nc.vector.memset(ones[:], 1.0)
            nc.vector.memset(before[:], 0.0)
            nc.vector.memset(c3[:], 0.0)
            for e in range(E1):
                nc.vector.memset(rank[:, e:e + 1], float(E1 - e))
            nc.vector.tensor_copy(one[:], onef[:])
            nc.vector.tensor_copy(upto[:], uptof[:]).then_inc(setup, 1)
            nc.vector.memset(mx[:], 0.0).then_inc(small_free, 1)
            v.wait_ge(small_free, 1)
            with v.Fori(0, NI) as i:
                c = Count(i * DVE)
                for k in range(K):
                    nc.vector.bn_stats(stat[:, k, :], x[:, bass.ds(i * K + k, 1), :].rearrange("p a d -> p (a d)")
                                       ).then_inc(dve, c.up())
                v.wait_ge(dve, c.now())
                nc.vector.tensor_copy(gb[:], modT[:, 1, 5, bass.ds(i * HALVES, HALVES)])
                nc.vector.tensor_copy(cb[:], modT[:, 1, 4, bass.ds(i * HALVES, HALVES)])
                nc.vector.tensor_copy(sbb[:], modT[:, 1, 3, bass.ds(i * HALVES, HALVES)]).then_inc(mod_done, 1)
                for k in range(K):
                    n = nc.vector.bn_aggr(mv[:, k, :], stat[:, k, :])
                n.then_inc(stats_done, 1)
                v.wait_ge(rstd_done, i * 2 + 2)
                for k in range(K):
                    n = nc.vector.tensor_scalar(y[:, k, :], x[:, bass.ds(i * K + k, 1), :].rearrange("p a d -> p (a d)"),
                                                mv[:, k, 0:1], rstd[:, k:k + 1], ALU.subtract, ALU.mult)
                n.then_inc(y_done, 1)
                v.wait_ge(small_full, i * SMALL + 2)
                wide = [P, K, E1]
                nc.vector.tensor_tensor(lg[:], ps[:, 1, 0:K * E1].rearrange("p (k e) -> p k e", e=E1),
                                        br[:].unsqueeze(1).to_broadcast(wide), ALU.add).then_inc(small_free, 1)
                v.wait_ge(small_free, i * SMALL + 3)
                nc.vector.tensor_reduce(mx[:], lg[:], AX_X, ALU.max).then_inc(dve, c.up())
                v.wait_ge(dve, c.now())
                nc.vector.tensor_tensor(ex[:], lg[:], mx[:].unsqueeze(2).to_broadcast(wide), ALU.subtract
                                        ).then_inc(logits_done, 1)
                v.wait_ge(exp_done, i + 1)
                nc.vector.tensor_reduce(den[:], ex[:], AX_X, ALU.add).then_inc(dve, c.up())
                v.wait_ge(dve, c.now())
                nc.vector.reciprocal(den[:], den[:]).then_inc(dve, c.up())
                v.wait_ge(dve, c.now())
                nc.vector.tensor_tensor(ex[:], ex[:], den[:].unsqueeze(2).to_broadcast(wide), ALU.mult
                                        ).then_inc(dve, c.up())
                v.wait_ge(dve, c.now())
                nc.vector.tensor_reduce(gate[:], ex[:], AX_X, ALU.max).then_inc(dve, c.up())
                v.wait_ge(dve, c.now())
                nc.vector.tensor_tensor(oh[:], ex[:], gate[:].unsqueeze(2).to_broadcast(wide), ALU.is_equal
                                        ).then_inc(dve, c.up())
                v.wait_ge(dve, c.now())
                nc.vector.tensor_tensor(oh[:], oh[:], rank[:].unsqueeze(1).to_broadcast(wide), ALU.mult
                                        ).then_inc(dve, c.up())
                v.wait_ge(dve, c.now())
                nc.vector.tensor_reduce(mx[:], oh[:], AX_X, ALU.max).then_inc(dve, c.up())
                v.wait_ge(dve, c.now())
                nc.vector.tensor_tensor(oh[:], oh[:], mx[:].unsqueeze(2).to_broadcast(wide), ALU.is_equal
                                        ).then_inc(dve, c.up())
                v.wait_ge(dve, c.now())
                for k in range(K):
                    nc.vector.tensor_tensor(before[:, k + 1, :], before[:, k, :], oh[:, k, :], ALU.add
                                            ).then_inc(dve, c.up())
                    v.wait_ge(dve, c.now())
                nc.vector.tensor_copy(ohb[:], oh[:]).then_inc(dve, c.up())
                nc.vector.tensor_copy(beforeb[:], before[:, 0:K, :]).then_inc(chosen, 1)
                v.wait_ge(chosen, i + 1)
                nc.vector.tensor_copy(before[:, 0, :], before[:, K, :]).then_inc(dve, c.up())
                nc.vector.tensor_tensor(wt[:], oh[:], gate[:].unsqueeze(2).to_broadcast(wide), ALU.mult
                                        ).then_inc(dve, c.up())
                v.wait_ge(dve, c.now())
                v.wait_ge(counted, i + 1)
                nc.vector.tensor_scalar(oh[:], ps[:, 7, 0:K * E1].rearrange("p (k e) -> p k e", e=E1), float(CAP),
                                        None, ALU.is_lt).then_inc(dve, c.up())
                v.wait_ge(dve, c.now())
                nc.vector.tensor_tensor(wt[:], wt[:], oh[:], ALU.mult).then_inc(w_done, 1)
                v.wait_ge(small_full, i * SMALL + 3)
                nc.vector.tensor_copy(wT[:], ps[0:E1, 1, :]).then_inc(small_free, 1)
                v.wait_ge(small_free, i * SMALL + 4)
                nc.vector.tensor_copy(c3[0:E1, :], wT[:]).then_inc(dve, c.up())
                v.wait_ge(dve, c.now())
                nc.vector.tensor_tensor(rest[:, 0, :], wT[:], c3[0:E1, :], ALU.subtract).then_inc(dve, c.up())
                v.wait_ge(dve, c.now())
                nc.vector.tensor_copy(c3[32:32 + E1, :], rest[:, 0, :]).then_inc(dve, c.up())
                v.wait_ge(dve, c.now())
                nc.vector.tensor_tensor(rest[:, 1, :], rest[:, 0, :], c3[32:32 + E1, :], ALU.subtract
                                        ).then_inc(dve, c.up())
                v.wait_ge(dve, c.now())
                nc.vector.tensor_copy(c3[64:64 + E1, :], rest[:, 1, :]).then_inc(split_done, 1)
                v.wait_ge(sum_full, i + 1)
                nc.vector.tensor_tensor(hg[:], hT[:], ps[:, 6, :], ALU.mult).then_inc(hg_done, 1)
                for u in range(E1):
                    v.wait_ge(relu_done, i * E1 + u + 1)
                    if u >= 2:
                        v.wait_ge(down_done, i * E1 + u - 1)
                    nc.vector.tensor_tensor(hm[:, u % 2], r[:, u % 2], ps[:, 4 + u % 2], ALU.mult
                                            ).then_inc(hidden_done, 1)
                v.wait_ge(small_full, i * SMALL + 4)
                xs = x[:, bass.ds(i * K, K), :]
                nc.vector.tensor_tensor(xs, xs, ps[:, 1, :].rearrange("p (k d) -> p k d", d=D), ALU.add
                                        ).then_inc(small_free, 1)
                assert c.n == DVE, c.n


def attention1(nc, s, t, ps):
    x, modT, ident = s["x"], s["modT"], s["ident"]
    UNITS = [list(range(a, min(a + 4, NO))) for a in range(0, NO, 4)]
    STEPS = 6 + len(UNITS)
    HALF_NO = NO // 2
    INV = float(1.0 / np.sqrt(np.float32(HD)))
    with ExitStack() as ctx:
        def sb(name, shape, dt=F32):
            return ctx.enter_context(nc.sbuf_tensor("a1_" + name, shape, dt))

        def sem(name):
            return ctx.enter_context(nc.semaphore("a1_" + name))

        w = sb("w", [P, 5, D])
        bcol = sb("bcol", [P, 5])
        hbg = sb("hbg", [P, 1])
        ifg = sb("ifg", [P, 1])
        inv = sb("inv", [P, 1])
        emb = sb("emb", [P, NO * H])
        headsum = sb("headsum", [P, H])
        pb = sb("pb", [P, TB, NO * H])
        pbr = sb("pbr", [P, NO * H])
        early = sb("early", [P, TB, NO])
        gabo = sb("gabo", [P, B])
        ga, ca, sa = sb("ga", [P, 2]), sb("ca", [P, 1]), sb("sa", [P, 1])
        stat, mv, rstd = sb("stat", [P, TB, 6]), sb("mv", [P, TB, 2]), sb("rstd", [P, TB])
        y, hT = sb("y", [P, TB, D]), sb("hT", [P, L])
        q, kp, vp = sb("q", [P, L]), sb("kp", [P, PAD + L]), sb("vp", [P, PAD + L])
        th, gs = sb("th", [P, L]), sb("gs", [P, L])
        prod = sb("prod", [P, NO, L])
        g = sb("g", [P, TB, NO * H])
        lg = sb("lg", [P, TB, NO * H])
        mx, den = sb("mx", [P, TB, H]), sb("den", [P, TB, H])
        pe8 = sb("pe8", [P, TB, NO * H, HD])
        denw = sb("denw", [P, TB, D])
        yv = sb("yv", [P, 2, 4, L])
        acc = sb("acc", [P, 4, L])
        og = sb("og", [P, L])
        yo = sb("yo", [P, L])

        loaded, setup = sem("loaded"), sem("setup")
        stats_done, rstd_done, y_done, mod_done = sem("stats_done"), sem("rstd_done"), sem("y_done"), sem("mod_done")
        psum_full = sem("psum_full")
        half_free = [sem("half0_free"), sem("half1_free")]
        gate_done, prod_v, prod_g = sem("gate_done"), sem("prod_v"), sem("prod_g")
        shifted, exp_done, den_done = sem("shifted"), sem("exp_done"), sem("den_done")
        last_done = sem("last_done")
        biased = sem("biased")
        added, og_done, dve, pool_done = sem("added"), sem("og_done"), sem("dve"), sem("pool_done")
        block = ctx.enter_context(nc.Block())
        DVE = 8

        def shift(pad, o0, n):
            a = pad[:, 0:L]
            return bass.AP(tensor=a.tensor, offset=PAD - ORDER[o0], ap=[list(a.ap[0]), [1, n], [1, L]])

        def runs(unit):
            out = []
            for o in unit:
                if out and ORDER[o] == ORDER[out[-1][0] + out[-1][1] - 1] - 1:
                    out[-1][1] += 1
                else:
                    out.append([o, 1])
            return out

        VUNITS, GUNITS = UNITS[:6], UNITS[6:]

        def half(step):
            return 4 * (step % 2)

        @block.sync
        def _(sp):
            for dst, name in ((w, "a1_w"), (bcol, "a1_b"), (ifg, "a1_ifg"), (emb, "a1_emb"), (headsum, "c_headsum"),
                              (early, "c_early")):
                sp.dma_start(dst[:], t[name]).then_inc(loaded, 16)
            sp.dma_start(pbr[:], t["a1_pb"].partition_broadcast(P)).then_inc(loaded, 16)

        @block.gpsimd
        def _(pool):
            nc.gpsimd.memset(kp[:], 0.0)
            nc.gpsimd.memset(inv[:], INV)
            nc.gpsimd.memset(vp[:], 0.0).then_inc(setup, 1)
            pool.wait_ge(setup, 2)
            with pool.Fori(0, B) as i:
                pool.wait_ge(stats_done, i + 1)
                nc.gpsimd.tensor_tensor(rstd[:], mv[:, :, 1], s["eps"][:, 0:TB], ALU.add).then_inc(rstd_done, 1)
                pool.wait_ge(rstd_done, i * 2 + 1)
                nc.gpsimd.tensor_tensor(rstd[:], rstd[:], s["pm5"][:, 0:TB], ALU.pow).then_inc(rstd_done, 1)
                pool.wait_ge(gate_done, i + 1)
                for unit in GUNITS:
                    for o0, n in runs(unit):
                        m = nc.gpsimd.tensor_tensor(prod[:, o0:o0 + n, :], q[:].unsqueeze(1).to_broadcast([P, n, L]),
                                                    shift(kp, o0, n), ALU.mult)
                    m.then_inc(prod_g, 1)
                pool.wait_ge(half_free[1], i * (STEPS // 2) + 3)
                nc.gpsimd.tensor_tensor(lg[:], lg[:], pb[:], ALU.add).then_inc(biased, 1)
                for u, unit in enumerate(UNITS[1:]):
                    n = len(unit)
                    if u < len(UNITS) - 2:
                        step = 5 + u
                        pool.wait_ge(half_free[step % 2], i * (STEPS // 2) + step // 2 + 2)
                    else:
                        pool.wait_ge(last_done, i + 1)
                    if u:
                        pool.wait_ge(added, i * len(UNITS) + u)
                    nc.gpsimd.tensor_tensor(acc[:, 0:n], acc[:, 0:n], yv[:, (u + 1) % 2, 0:n], ALU.add
                                            ).then_inc(added, 1)
                pool.wait_ge(added, i * len(UNITS) + len(UNITS) - 1)
                nc.gpsimd.tensor_tensor(acc[:, 0:2], acc[:, 0:2], acc[:, 2:4], ALU.add).then_inc(added, 1)

        @block.scalar
        def _(act):
            act.wait_ge(setup, 2)
            with act.Fori(0, B) as i:
                full = i * STEPS
                act.wait_ge(mod_done, i + 1)
                act.wait_ge(psum_full, full + 1)
                nc.scalar.activation(hT[:], ps[:, 0, 0:L], ACT.Identity, bias=sa[:], scale=ca[:]
                                     ).then_inc(half_free[0], 1)
                act.wait_ge(psum_full, full + 2)
                nc.scalar.activation(th[:], ps[:, 5, L:2 * L], ACT.Tanh, bias=hbg[:], scale=0.5)
                nc.scalar.activation(q[:], ps[:, 4, 0:L], ACT.Identity, bias=bcol[:, 0:1])
                nc.scalar.activation(kp[:, PAD:], ps[:, 4, L:2 * L], ACT.Identity, bias=bcol[:, 1:2]
                                     ).then_inc(gate_done, 1)
                nc.scalar.activation(vp[:, PAD:], ps[:, 5, 0:L], ACT.Identity, bias=bcol[:, 2:3]
                                     ).then_inc(half_free[1], 1)
                act.wait_ge(psum_full, full + 3)
                for k in range(TB):
                    a = nc.scalar.activation(g[:, k, :].rearrange("p (a m) -> p a m", a=2),
                                             ps[:, 2 * k:2 * k + 2, 0:HALF_NO * H], ACT.Identity,
                                             bias=inv[:], scale=INV)
                a.then_inc(half_free[0], 1)
                act.wait_ge(shifted, i + 1)
                for u, unit in enumerate(UNITS):
                    rows = slice(unit[0] * H, (unit[-1] + 1) * H)
                    nc.scalar.activation(pe8[:, :, rows, :],
                                         lg[:, :, rows].unsqueeze(3).to_broadcast([P, TB, len(unit) * H, HD]),
                                         ACT.Exp).then_inc(exp_done, 1)
                act.wait_ge(psum_full, full + STEPS - 1)
                hf = half(STEPS - 2)
                nc.scalar.activation(yo[:], ps[:, hf, 0:L], ACT.Identity, bias=ga[:, 1:2], scale=ga[:, 0:1]
                                     ).then_inc(half_free[STEPS % 2], 1)

        @block.tensor
        def _(pe):
            pe.wait_ge(setup, 2)
            with pe.Fori(0, B) as i:
                n_half = [Count(i * (STEPS // 2) + 1), Count(i * (STEPS // 2) + 1)]

                def begin(step):
                    pe.wait_ge(half_free[step % 2], n_half[step % 2].now())
                    n_half[step % 2].up()

                def after(step):
                    pe.wait_ge(half_free[step % 2], n_half[step % 2].now())

                begin(0)
                pe.wait_ge(y_done, i + 1)
                for k in range(TB):
                    mm = nc.tensor.transpose(ps[:, 0, k * P:(k + 1) * P], y[:, k, :], ident[:])
                mm.then_inc(psum_full, 1)
                begin(1)
                after(0)
                for k in range(4):
                    mm = nc.tensor.matmul(ps[:, 4 + k // 2, (k % 2) * L:(k % 2 + 1) * L], w[:, k, :], hT[:],
                                          start=True, stop=True)
                mm.then_inc(psum_full, 1)
                begin(2)
                after(1)
                for k in range(TB):
                    for a in range(2):
                        m = HALF_NO * H
                        mm = nc.tensor.matmul(ps[:, 2 * k + a, 0:m], q[:, k * P:(k + 1) * P], emb[:, a * m:(a + 1) * m],
                                              start=True, stop=True)
                mm.then_inc(psum_full, 1)
                begin(3)
                for n, unit in enumerate(UNITS):
                    if unit in VUNITS:
                        pe.wait_ge(prod_v, i * len(VUNITS) + n + 1)
                    else:
                        pe.wait_ge(prod_g, i * len(GUNITS) + n - len(VUNITS) + 1)
                    for o in unit:
                        for k in range(TB):
                            bank, col = 4 + 2 * k + o // HALF_NO, (o % HALF_NO) * H
                            mm = nc.tensor.matmul(ps[:, bank, col:col + H], prod[:, o, k * P:(k + 1) * P], headsum[:],
                                                  start=True, stop=True)
                mm.then_inc(psum_full, 1)
                for u, unit in enumerate(UNITS):
                    begin(4 + u)
                    pe.wait_ge(exp_done, i * len(UNITS) + u + 1)
                    for n, o in enumerate(unit):
                        for k in range(TB):
                            row = pe8[:, k, o * H:(o + 1) * H, :].rearrange("p h d -> p (h d)")
                            mm = nc.tensor.transpose(
                                ps[:, half(u) + n // 2, (n % 2) * L + k * P:(n % 2) * L + (k + 1) * P], row, ident[:])
                    if u == len(UNITS) - 1:
                        pe.wait_ge(den_done, i + 1)
                        for k in range(TB):
                            mm = nc.tensor.transpose(ps[:, half(u) + 2, k * P:(k + 1) * P], denw[:, k, :], ident[:])
                    mm.then_inc(psum_full, 1)
                begin(STEPS - 2)
                pe.wait_ge(og_done, i + 1)
                hf = half(STEPS - 2)
                nc.tensor.matmul(ps[:, hf, 0:L], w[:, 4, :], og[:], start=True, stop=True).then_inc(psum_full, 1)
                begin(STEPS - 1)
                after(STEPS - 2)
                hf = half(STEPS - 1)
                for k in range(TB):
                    mm = nc.tensor.transpose(ps[:, hf, k * P:(k + 1) * P], yo[:, k * P:(k + 1) * P], ident[:])
                mm.then_inc(psum_full, 1)

        @block.vector
        def _(v):
            v.wait_ge(loaded, 112)
            v.wait_ge(setup, 1)
            c = Count()
            nc.vector.tensor_scalar(hbg[:], bcol[:, 3:4], 0.5, None, ALU.mult)
            nc.vector.tensor_scalar(ifg[:], ifg[:], 0.5, None, ALU.mult)
            nc.vector.tensor_scalar(gabo[:], modT[:, 1, 2, :], bcol[:, 4:5], None, ALU.mult)
            for k in range(TB):
                n = nc.vector.tensor_tensor(pb[:, k].rearrange("p (o h) -> p o h", h=H),
                                            pbr[:].rearrange("p (o h) -> p o h", h=H),
                                            early[:, k].unsqueeze(2).to_broadcast([P, NO, H]), ALU.add)
            n.then_inc(setup, 1)
            nc.vector.memset(mx[:], 0.0).then_inc(half_free[0], 1)
            nc.vector.memset(den[:], 0.0).then_inc(half_free[1], 1)
            v.wait_ge(setup, 2)
            v.wait_ge(half_free[0], 1)
            v.wait_ge(half_free[1], 1)
            with v.Fori(0, B) as i:
                c = Count(i * DVE)
                full = i * STEPS
                for k in range(TB):
                    nc.vector.bn_stats(stat[:, k, :], x[:, bass.ds(i * TB + k, 1), :].rearrange("p a d -> p (a d)")
                                       ).then_inc(dve, c.up())
                v.wait_ge(dve, c.now())
                nc.vector.tensor_copy(ga[:, 0:1], modT[:, 1, 2, bass.ds(i, 1)])
                nc.vector.tensor_copy(ga[:, 1:2], gabo[:, bass.ds(i, 1)])
                nc.vector.tensor_copy(ca[:], modT[:, 1, 1, bass.ds(i, 1)])
                nc.vector.tensor_copy(sa[:], modT[:, 1, 0, bass.ds(i, 1)]).then_inc(mod_done, 1)
                for k in range(TB):
                    n = nc.vector.bn_aggr(mv[:, k, :], stat[:, k, :])
                n.then_inc(stats_done, 1)
                v.wait_ge(rstd_done, i * 2 + 2)
                for k in range(TB):
                    n = nc.vector.tensor_scalar(y[:, k, :], x[:, bass.ds(i * TB + k, 1), :].rearrange("p a d -> p (a d)"),
                                                mv[:, k, 0:1], rstd[:, k:k + 1], ALU.subtract, ALU.mult)
                n.then_inc(y_done, 1)
                v.wait_ge(gate_done, i + 1)
                for unit in VUNITS:
                    for o0, n in runs(unit):
                        m = nc.vector.tensor_tensor(prod[:, o0:o0 + n, :], q[:].unsqueeze(1).to_broadcast([P, n, L]),
                                                    shift(kp, o0, n), ALU.mult)
                    m.then_inc(prod_v, 1)
                nc.vector.tensor_scalar(gs[:], th[:], ifg[:], ifg[:], ALU.mult, ALU.add).then_inc(dve, c.up())
                v.wait_ge(psum_full, full + 4)
                v.wait_ge(half_free[0], i * (STEPS // 2) + 3)
                for k in range(TB):
                    n = nc.vector.tensor_tensor(lg[:, k, :].rearrange("p (a m) -> p a m", a=2),
                                                ps[:, 4 + 2 * k:6 + 2 * k, 0:HALF_NO * H],
                                                g[:, k, :].rearrange("p (a m) -> p a m", a=2), ALU.mult)
                    n.then_inc(half_free[1] if k else dve, 1 if k else c.up())
                v.wait_ge(half_free[1], i * (STEPS // 2) + 3)
                v.wait_ge(biased, i + 1)
                byhead = lg[:].rearrange("p k (o h) -> p k h o", h=H)
                byoffset = lg[:].rearrange("p k (o h) -> p k o h", h=H)
                wide = [P, NO, H]
                nc.vector.tensor_reduce(mx[:], byhead, AX_X, ALU.max).then_inc(dve, c.up())
                v.wait_ge(dve, c.now())
                for k in range(TB):
                    n = nc.vector.tensor_tensor(byoffset[:, k], byoffset[:, k], mx[:, k].unsqueeze(1).to_broadcast(wide),
                                                ALU.subtract)
                n.then_inc(shifted, 1)
                for u, unit in enumerate(UNITS):
                    if u == len(UNITS) - 1:
                        v.wait_ge(exp_done, (i + 1) * len(UNITS))
                        nc.vector.tensor_reduce(den[:], pe8[:, :, :, 0].rearrange("p k (o h) -> p k h o", h=H), AX_X, ALU.add
                                                ).then_inc(dve, c.up())
                        v.wait_ge(dve, c.now())
                        nc.vector.reciprocal(den[:], den[:]).then_inc(dve, c.up())
                        v.wait_ge(dve, c.now())
                        nc.vector.tensor_copy(denw[:].rearrange("p k (h d) -> p k h d", d=HD),
                                              den[:].unsqueeze(3).to_broadcast([P, TB, H, HD])).then_inc(den_done, 1)
                    v.wait_ge(psum_full, full + 5 + u)
                    if u >= 3:
                        v.wait_ge(added, i * len(UNITS) + u - 2)
                    dst = acc if u == 0 else yv[:, u % 2]
                    for o0, n in runs(unit):
                        a = o0 - unit[0]
                        pt = ps[:, half(u):half(u) + 2, :].rearrange("p b (a n) -> p (b a) n", n=L)
                        m = nc.vector.tensor_tensor(dst[:, a:a + n, :], pt[:, a:a + n, :], shift(vp, o0, n), ALU.mult)
                    if u < len(UNITS) - 1:
                        m.then_inc(half_free[u % 2], 1)
                        continue
                    m.then_inc(last_done, 1)
                    nc.vector.tensor_tensor(gs[:], gs[:], ps[:, half(u) + 2, 0:L], ALU.mult
                                            ).then_inc(half_free[u % 2], 1)
                v.wait_ge(added, (i + 1) * len(UNITS))
                nc.vector.tensor_tensor(og[:], acc[:, 0], acc[:, 1], ALU.add).then_inc(dve, c.up())
                v.wait_ge(dve, c.now())
                v.wait_ge(half_free[1], (i + 1) * (STEPS // 2))
                nc.vector.tensor_tensor(og[:], og[:], gs[:], ALU.mult).then_inc(og_done, 1)
                v.wait_ge(psum_full, full + STEPS)
                xs = x[:, bass.ds(i * TB, TB), :]
                hf = half(STEPS - 1)
                nc.vector.tensor_tensor(xs, xs, ps[:, hf, 0:L].rearrange("p (k d) -> p k d", d=D), ALU.add
                                        ).then_inc(half_free[(STEPS - 1) % 2], 1)
                assert c.n == DVE, c.n


def store_stream(nc, s, out):
    with nc.semaphore("st_stored") as stored, nc.Block() as block:
        @block.sync
        def _(sp):
            sp.dma_start(out.rearrange("b (k p) d -> p (b k) d", p=P), s["x"][:]).then_inc(stored, 16)
            sp.wait_ge(stored, 16)


def layout(inputs):
    a = {k: np.ascontiguousarray(v) for k, v in inputs.items()}
    swap = np.arange(D).reshape(-1, 2)[:, ::-1].reshape(-1)
    t = {
        "L0_attn_x": a["L0_attn_x"],
        "L0_attn_bv": a["L0_attn_bv"],
        "L0_attn_scale": a["L0_attn_scale"],
        "cT": np.stack([a["L0_c"].T, a["L1_c"].T], 1),
        "wmod": np.stack([a["L0_wmod"], a["L1_wmod"]], 1),
        "a0_w": np.stack([a["L0_attn_Wq"].T, a["L0_attn_Wq"][swap].T, a["L0_attn_Wk"].T, a["L0_attn_Wk"][swap].T,
                          a["L0_attn_Wv"].T, a["L0_attn_Wo"].T], 1),
        "a0_b": np.stack([a["L0_attn_bq"], a["L0_attn_bq"][swap], a["L0_attn_bk"], a["L0_attn_bk"][swap],
                          a["L0_attn_bo"]], 1),
    }
    gu = a["L0_ffn_gate_up_proj"].reshape(PAIRS, 2, 2, I0, D)
    pack = lambda w, first: np.concatenate([first.T[None], w.transpose(0, 3, 1, 2).reshape(PAIRS, D, P)]).transpose(1, 0, 2)
    t["e0_wg"] = pack(gu[:, :, 0], a["L0_ffn_shared_gate_w"])
    t["e0_wu"] = pack(gu[:, :, 1], a["L0_ffn_shared_up_w"])
    down = a["L0_ffn_down_proj"].reshape(PAIRS, 2, D, I0).transpose(0, 1, 3, 2).reshape(PAIRS, P, D)
    t["e0_wd"] = np.concatenate([a["L0_ffn_shared_down_w"].T[None], down]).transpose(1, 0, 2)
    t["e0_wr"] = a["L0_ffn_router_weight"].T
    t["L0_ffn_e_score_bias"] = a["L0_ffn_e_score_bias"]
    qkv, qb = a["L1_attn_qkv_w"].reshape(3, D, D), a["L1_attn_qkv_b"].reshape(3, D)
    t["a1_w"] = np.stack([*qkv, a["L1_attn_gate_w"], a["L1_attn_out_w"]]).transpose(2, 0, 1)
    t["a1_b"] = np.stack([*qb, a["L1_attn_gate_b"], a["L1_attn_out_b"]], 1)
    t["a1_ifg"] = np.repeat(a["L1_attn_if_gain"], HD)[:, None]
    emb = np.zeros((H, HD, NO, H), np.float32)
    for h in range(H):
        emb[h, :, :, h] = a["L1_attn_scale_embed"][::-1].T
    t["a1_emb"] = emb.reshape(D, NO * H)
    t["a1_pb"] = a["L1_attn_pos_bias"][::-1].reshape(-1)
    t["e1_w1"] = a["L1_ffn_W1"].transpose(1, 0, 2)
    t["e1_w2"] = a["L1_ffn_W2"].transpose(1, 0, 2)
    t["e1_b1"] = a["L1_ffn_b1"].T
    for name in ("L1_ffn_b2", "L1_ffn_Wr", "L1_ffn_br"):
        t[name] = a[name]
    t.update(shape_constants())
    return {k: np.ascontiguousarray(v) for k, v in t.items()}


def kernel(**inputs):
    import concourse.bacc as bacc
    from concourse.bass_utils import run_bass_kernel_spmd

    nc = bacc.Bacc("TRN2", target_bir_lowering=False, num_devices=1)
    arrays = layout(inputs)
    t = {name: nc.dram_tensor(name + "_dram", a.shape, mybir.dt.from_np(a.dtype), kind="ExternalInput").ap()
         for name, a in arrays.items()}
    out = nc.dram_tensor("out_dram", (B, L, D), F32, kind="ExternalOutput").ap()
    build(nc, t, out)
    r = run_bass_kernel_spmd(nc, [{name + "_dram": a for name, a in arrays.items()}], core_ids=[0])
    return r.results[0]["out_dram"]
```

```python
from contextlib import ExitStack

import numpy as np

import concourse.bass as bass
from concourse import mybir

ALU = mybir.AluOpType
ACT = mybir.ActivationFunctionType
AX_X = mybir.AxisListType.X
F32 = mybir.dt.float32
BF16 = mybir.dt.bfloat16

P = 128
B, L, D = 16, 256, 128
T = B * L
NT = T // P
TB = L // P
H, HD = 16, 8
HJ, HG = 4, 4
E0, I0, TOP_K = 32, 64, 6
PAIRS = E0 // 2
E1 = 8
CAP = T // E1
MT = 512
OFFSETS = sorted(set(range(33)) | {48, 64, 96, 128, 192})
NO = len(OFFSETS)
ORDER = OFFSETS[::-1]
PAD = max(OFFSETS)
EPS = 1e-5
NEG = -1e30
THETA = 10000.0
NORM_MIN = 1e-12


class Count:

    def __init__(self, base=0):
        self.base, self.n = base, 0

    def up(self, k=1):
        self.n += k
        return k

    def now(self):
        return self.base + self.n


def shape_constants():
    freqs = (THETA ** (-np.arange(0, HD, 2, dtype=np.float32) / HD)).astype(np.float32)
    ang = np.arange(L, dtype=np.float32)[:, None] * freqs
    cos = np.repeat(np.cos(ang), 2, axis=1)
    sin = np.repeat(np.sin(ang), 2, axis=1)
    sin[:, 0::2] *= -1
    q, k = np.arange(P)[:, None], np.arange(P)[None, :]
    later = np.where(k > q, NEG, 0.0).astype(np.float32)
    masks = np.stack([np.tile(later[:, None], (1, 4, 1)), np.tile(later.T[:, None], (1, 4, 1))], 1)
    n = np.arange(L).reshape(TB, P).T[:, :, None]
    early = np.where(n < np.array(ORDER)[None, None, :], NEG, 0.0).astype(np.float32)
    pair = np.zeros((96, PAIRS, P), np.float32)
    one = np.zeros((96, E1 + 1, P), np.float32)
    for part in range(3):
        for e in range(E0):
            pair[32 * part + e, e // 2, 64 * (e % 2):64 * (e % 2) + 64] = 1
        for e in range(E1):
            one[32 * part + e, e] = 1
            one[32 * part + e, E1] = 1
    return {
        "c_ident": np.eye(P, dtype=np.float32),
        "c_cos": np.tile(cos.T, (H, 1)).astype(np.float32),
        "c_sin": np.tile(sin.T, (H, 1)).astype(np.float32),
        "c_masks": masks,
        "c_early": early,
        "c_pair": pair,
        "c_one": one,
        "c_upto": np.triu(np.ones((P, P), np.float32)),
        "c_headsum": np.pad(np.kron(np.eye(H, dtype=np.float32), np.ones((HD, 1), np.float32)),
                            ((0, 0), (3 * H, 3 * H))),
    }


def build(nc, t, out):
    ctx = ExitStack()
    with ctx:
        def sb(name, shape, dt=F32):
            return ctx.enter_context(nc.sbuf_tensor(name, shape, dt))

        def sem(name):
            return ctx.enter_context(nc.semaphore(name))

        ps = ctx.enter_context(nc.psum_tensor("ps", [P, 8, 512], F32))

        s = {}
        s["ident"] = sb("ident", [P, P])
        s["identb"] = sb("identb", [P, P], BF16)
        s["x"] = sb("x", [P, NT, D])
        s["modT"] = sb("modT", [P, 2, 6, B])
        s["pm5"] = sb("pm5", [P, TB * 2])
        s["eps"] = sb("eps", [P, TB * 2])

        load_stream(nc, s, t, ps, sb, sem)
        attention0(nc, s, t, ps)
        experts0(nc, s, t, ps)
        attention1(nc, s, t, ps)
        experts1(nc, s, t, ps)
        store_stream(nc, s, out)


def load_stream(nc, s, t, ps, sb, sem):
    x, modT = s["x"], s["modT"]
    with ExitStack() as ctx:
        cT = ctx.enter_context(nc.sbuf_tensor("ls_cT", [P, 2, B], F32))
        sT = ctx.enter_context(nc.sbuf_tensor("ls_sT", [P, 2, B], F32))
        wm = ctx.enter_context(nc.sbuf_tensor("ls_wm", [P, 2, 6 * D], F32))
        g1 = ctx.enter_context(nc.sbuf_tensor("ls_g1", [P, 2, 2, B], F32))
        g2 = ctx.enter_context(nc.sbuf_tensor("ls_g2", [P, 2, 2, B], F32))
        loaded = ctx.enter_context(nc.semaphore("ls_loaded"))
        silu_done = ctx.enter_context(nc.semaphore("ls_silu"))
        mod_done = ctx.enter_context(nc.semaphore("ls_mod"))
        dve = ctx.enter_context(nc.semaphore("ls_dve"))
        block = ctx.enter_context(nc.Block())

        @block.sync
        def _(sp):
            sp.dma_start(cT[:], t["cT"]).then_inc(loaded, 16)
            sp.dma_start(wm[:], t["wmod"]).then_inc(loaded, 16)
            sp.dma_start(s["ident"][:], t["c_ident"]).then_inc(loaded, 16)
            sp.dma_start(x[:], t["L0_attn_x"].rearrange("b (k p) d -> p (b k) d", p=P)).then_inc(loaded, 16)

        @block.scalar
        def _(act):
            act.wait_ge(loaded, 64)
            nc.scalar.activation(sT[:], cT[:], ACT.Silu).then_inc(silu_done, 1)

        @block.tensor
        def _(pe):
            pe.wait_ge(silu_done, 1)
            for layer in range(2):
                for j in range(6):
                    mm = nc.tensor.matmul(ps[:, layer, j * B:(j + 1) * B], wm[:, layer, j * D:(j + 1) * D],
                                          sT[:, layer, :], start=True, stop=True)
            mm.then_inc(mod_done, 1)

        @block.vector
        def _(v):
            c = Count()
            v.wait_ge(loaded, 64)
            nc.vector.tensor_copy(s["identb"][:], s["ident"][:]).then_inc(dve, c.up())
            nc.vector.memset(s["pm5"][:], -0.5).then_inc(dve, c.up())
            nc.vector.memset(s["eps"][:], EPS).then_inc(dve, c.up())
            v.wait_ge(mod_done, 1)
            for layer in range(2):
                nc.vector.tensor_copy(modT[:, layer], ps[:, layer, 0:6 * B].rearrange("p (j b) -> p j b", b=B)
                                      ).then_inc(dve, c.up())
            v.wait_ge(dve, c.now())
            for layer in range(2):
                scales, gates = modT[:, layer, 1:6:3, :], modT[:, layer, 2:6:3, :]
                nc.vector.tensor_scalar(scales, scales, 1.0, None, ALU.add).then_inc(dve, c.up())
                nc.vector.tensor_scalar(g1[:, layer], gates, 0.0, 2.0, ALU.is_ge, ALU.mult).then_inc(dve, c.up())
                nc.vector.tensor_scalar(g2[:, layer], gates, -1.0, None, ALU.mult).then_inc(dve, c.up())
                v.wait_ge(dve, c.now())
                nc.vector.tensor_tensor(g2[:, layer], g2[:, layer], gates, ALU.max).then_inc(dve, c.up())
                v.wait_ge(dve, c.now())
                nc.vector.tensor_scalar(g2[:, layer], g2[:, layer], 0.25, None, ALU.max).then_inc(dve, c.up())
                v.wait_ge(dve, c.now())
                nc.vector.scalar_tensor_tensor(gates, g1[:, layer], -1.0, g2[:, layer], ALU.add, ALU.mult
                                               ).then_inc(dve, c.up())
                v.wait_ge(dve, c.now())


class Batch:

    def __init__(self, x, k):
        self.x, self.k = x, k

    def __add__(self, n):
        return Batch(self.x + n, self.k + n)


def hold(eng, sem, per, b, n):
    if per * b.k + n > 0:
        eng.wait_ge(sem, b.x * per + n)


def pipeline(eng, first, last, start, end, body, turns=3):
    passes = (end - start) // turns
    for k in range(first, start):
        body(Batch(k, k))
    with eng.Fori(0, passes) as i:
        for r in range(turns):
            body(Batch(i * turns + (start + r), start + r))
    for k in range(start + passes * turns, last):
        body(Batch(k, k))


def attention0(nc, s, t, ps):
    x, modT, ident, identb = s["x"], s["modT"], s["ident"], s["identb"]
    TERMS = [(0, 0), (0, 1), (0, 2), (1, 0), (1, 1), (2, 0)]
    ROWS = HD * len(TERMS)
    TOP = 64
    UN = 12
    with ExitStack() as ctx:
        def sb(name, shape, dt=F32):
            return ctx.enter_context(nc.sbuf_tensor("a0_" + name, shape, dt))

        def sem(name):
            return ctx.enter_context(nc.semaphore("a0_" + name))

        w = sb("w", [P, 6, D])
        bcol = sb("bcol", [P, 5])
        bvrow = sb("bvrow", [P, D])
        scale = sb("scale", [P, 1])
        cosq, sinq = sb("cosq", [P, L]), sb("sinq", [P, L])
        cosk, sink = sb("cosk", [P, L]), sb("sink", [P, L])
        maskf = sb("maskf", [P, 2, 4, P])
        mask = sb("mask", [P, 2, 4, P], BF16)
        gabo = sb("gabo", [P, B])
        ga, ca, sa = sb("ga", [P, 2]), sb("ca", [P, 1]), sb("sa", [P, 1])
        stat, mv, rstd = sb("stat", [P, TB, 6]), sb("mv", [P, TB, 2]), sb("rstd", [P, TB])
        y = sb("y", [P, TB, D])
        hT = sb("hT", [P, L])
        ra, rb = sb("ra", [P, 2, L]), sb("rb", [P, 2, L])
        parts = sb("parts", [P, 3, 2, L], BF16)
        vv = sb("vv", [P, 3, TB, H, 32])
        qs = sb("qs", [TOP + 3, 3, H, L], BF16)
        ks = sb("ks", [TOP + 3, 3, H, L], BF16)
        nmax = sb("nmax", [P, TB, HJ, HG])
        nT, nparts = sb("nT", [H, 2, L]), sb("nparts", [H, 3, L], BF16)
        pr = sb("pr", [P, 2, HJ, L + P])
        o = sb("o", [P, HG, L])
        rden = sb("rden", [P, TB, HG, HJ])
        on = sb("on", [P, TB, HJ, HG, HD])
        onT = sb("onT", [P, L])
        yo = sb("yo", [P, L])
        unit = sb("unit", [P, 1])
        parts_d = nc.dram_tensor("a0_parts_d", [P, 3, 2, L], BF16).ap()
        nparts_d = nc.dram_tensor("a0_nparts_d", [H, 3, L], BF16).ap()

        loaded, cleared, masks_done = sem("loaded"), sem("cleared"), sem("masks_done")
        stats_done, rstd_done, y_done = sem("stats_done"), sem("rstd_done"), sem("y_done")
        a_full, a_read = sem("a_full"), sem("a_read")
        rotated, summed, split = sem("rotated"), sem("summed"), sem("split")
        stored, spread = sem("stored"), sem("spread")
        m_full, m_read = sem("m_full"), sem("m_read")
        nT_full, nT_read = sem("nT_full"), sem("nT_read")
        nsplit, nstored, nspread = sem("nsplit"), sem("nstored"), sem("nspread")
        c_full, exp_done = sem("c_full"), sem("exp_done")
        pv_done, o_read = sem("pv_done"), sem("o_read")
        d_full, d_read = sem("d_full"), sem("d_read")
        dve_a, dve_d = sem("dve_a"), sem("dve_d")
        block = ctx.enter_context(nc.Block())
        A_STEPS, D_STEPS = 4, 5
        SPREAD = 16 * 2 * len(TERMS)

        def run(eng, order):
            ahead = {"D": -1, "C": 0, "M": 1, "N": 2, "S": 2, "A": 3}

            def body(b):
                for stage, step in order:
                    c = b + ahead[stage]
                    if 0 <= c.k < B:
                        step(c)
            pipeline(eng, -3, B + 1, 2, B - 3, body)

        @block.sync
        def _(sp):
            sp.dma_start(w[:], t["a0_w"]).then_inc(loaded, 16)
            sp.dma_start(bcol[:], t["a0_b"]).then_inc(loaded, 16)
            sp.dma_start(bvrow[:], t["L0_attn_bv"].partition_broadcast(P)).then_inc(loaded, 16)
            sp.dma_start(scale[:], t["L0_attn_scale"].partition_broadcast(P)).then_inc(loaded, 16)
            sp.dma_start(cosk[:], t["c_cos"]).then_inc(loaded, 16)
            sp.dma_start(sink[:], t["c_sin"]).then_inc(loaded, 16)
            sp.dma_start(maskf[:], t["c_masks"]).then_inc(loaded, 16)
            sp.wait_ge(cleared, 3)

            def spread_parts(b):
                sp.wait_ge(split, b.x + 1)
                sp.dma_start(parts_d, parts[:]).then_inc(stored, 16)
                sp.wait_ge(stored, b.x * 16 + 16)
                for n, (pq, pk) in enumerate(TERMS):
                    for dst, part, which in ((qs, pq, 0), (ks, pk, 1)):
                        sp.dma_start(dst[HD * n:HD * (n + 1), b.k % 3],
                                     parts_d[:, part, which, :].rearrange("(h d) n -> d h n", d=HD)
                                     ).then_inc(spread, 16)

            def spread_max(b):
                sp.wait_ge(nsplit, b.x * 4 + 4)
                sp.dma_start(nparts_d, nparts[:]).then_inc(nstored, 16)
                sp.wait_ge(nstored, b.x * 16 + 16)
                sp.dma_start(qs[TOP:TOP + 3, b.k % 3], nparts_d.rearrange("h t n -> t h n")).then_inc(nspread, 16)

            run(sp, [("S", spread_parts), ("M", spread_max)])

        @block.gpsimd
        def _(pool):
            nc.gpsimd.memset(qs[:], 0.0)
            nc.gpsimd.memset(unit[:], 1.0)
            nc.gpsimd.memset(ks[:], 0.0)
            nc.gpsimd.memset(vv[:], 0.0).then_inc(cleared, 1)
            pool.wait_ge(cleared, 1)
            nc.gpsimd.memset(ks[TOP:TOP + 3], 1.0).then_inc(cleared, 1)
            pool.wait_ge(cleared, 2)
            nc.gpsimd.memset(vv[:, :, :, :, HD], 1.0).then_inc(cleared, 1)

            def rstd_of(b):
                pool.wait_ge(stats_done, b.x + 1)
                nc.gpsimd.tensor_tensor(rstd[:], mv[:, :, 1], s["eps"][:, 0:TB], ALU.add).then_inc(rstd_done, 1)
                pool.wait_ge(rstd_done, b.x * 2 + 1)
                nc.gpsimd.tensor_tensor(rstd[:], rstd[:], s["pm5"][:, 0:TB], ALU.pow).then_inc(rstd_done, 1)

            def split_parts(b):
                pool.wait_ge(rotated, b.x * 2 + 2)
                pool.wait_ge(a_read, b.x * A_STEPS + 3)
                nc.gpsimd.tensor_tensor(ra[:], ra[:], rb[:], ALU.add).then_inc(summed, 1)
                pool.wait_ge(summed, b.x * 4 + 1)
                hold(pool, stored, 16, b, 0)
                nc.gpsimd.tensor_tensor(parts[:, 0], ra[:], unit[:].unsqueeze(2).to_broadcast([P, 2, L]), ALU.mult).then_inc(summed, 1)
                pool.wait_ge(summed, b.x * 4 + 2)
                nc.gpsimd.tensor_tensor(ra[:], ra[:], parts[:, 0], ALU.subtract).then_inc(summed, 1)
                pool.wait_ge(summed, b.x * 4 + 3)
                nc.gpsimd.tensor_tensor(parts[:, 1], ra[:], unit[:].unsqueeze(2).to_broadcast([P, 2, L]), ALU.mult).then_inc(summed, 1)

            def last_part(b):
                pool.wait_ge(summed, b.x * 4 + 4)
                hold(pool, spread, SPREAD, b, 0)
                hold(pool, c_full, UN, b + -2, 0)
                nc.gpsimd.tensor_tensor(parts[:, 2], ra[:], parts[:, 1], ALU.subtract).then_inc(split, 1)

            def split_max(b):
                pool.wait_ge(nT_read, b.x + 1)
                hold(pool, nspread, 16, b, 0)
                nc.gpsimd.tensor_tensor(nparts[:, 0], nT[:, 0], unit[0:H].to_broadcast([H, L]), ALU.mult).then_inc(nsplit, 1)
                pool.wait_ge(nsplit, b.x * 4 + 1)
                nc.gpsimd.tensor_tensor(nT[:, 1], nT[:, 0], nparts[:, 0], ALU.subtract).then_inc(nsplit, 1)
                pool.wait_ge(nsplit, b.x * 4 + 2)
                nc.gpsimd.tensor_tensor(nparts[:, 1], nT[:, 1], unit[0:H].to_broadcast([H, L]), ALU.mult).then_inc(nsplit, 1)
                pool.wait_ge(nsplit, b.x * 4 + 3)
                nc.gpsimd.tensor_tensor(nparts[:, 2], nT[:, 1], nparts[:, 1], ALU.subtract).then_inc(nsplit, 1)

            run(pool, [("S", last_part), ("A", rstd_of), ("M", split_max), ("A", split_parts)])

        @block.scalar
        def _(act):
            def modulate(b):
                hold(act, a_full, A_STEPS, b, 1)
                nc.scalar.activation(hT[:], ps[:, 6, 0:L], ACT.Identity, bias=sa[:], scale=ca[:]).then_inc(a_read, 1)

            def exps(g):
                def step(b):
                    hold(act, pv_done, HG, b, g - 1)
                    for n in range(3):
                        act.wait_ge(c_full, b.x * UN + 3 * g + n + 1)
                        bank = 2 + (3 * g + n) % 2
                        if n < 2:
                            dst, src = pr[:, g % 2, 2 * n:2 * n + 2, 0:L], ps[:, bank].rearrange("p (j n) -> p j n", j=2)
                        else:
                            dst, src = pr[:, g % 2, :, L:L + P], ps[:, bank].rearrange("p (j n) -> p j n", j=HJ)
                        nc.scalar.activation(dst, src, ACT.Exp).then_inc(exp_done, 1)
                return step

            def outputs(a):
                def step(b):
                    act.wait_ge(pv_done, b.x * HG + 2 * a + 2)
                    hold(act, d_full, D_STEPS, b, -3)
                    nc.scalar.activation(o[:, 2 * a:2 * a + 2], ps[:, 4 + a].rearrange("p (g n) -> p g n", n=L),
                                         ACT.Copy).then_inc(o_read, 1)
                return step

            def turned(b):
                act.wait_ge(d_full, b.x * D_STEPS + 3)
                nc.scalar.activation(onT[:], ps[:, 7, 0:L], ACT.Copy).then_inc(d_read, 1)

            def projected(b):
                act.wait_ge(d_full, b.x * D_STEPS + 4)
                nc.scalar.activation(yo[:], ps[:, 7, 0:L], ACT.Identity, bias=ga[:, 1:2], scale=ga[:, 0:1]
                                     ).then_inc(d_read, 1)

            run(act, [("C", exps(0)), ("D", outputs(1)), ("C", exps(1)), ("A", modulate), ("D", turned),
                      ("C", exps(2)), ("D", projected), ("C", outputs(0)), ("C", exps(3))])

        @block.tensor
        def _(pe):
            pe.wait_ge(cleared, 3)
            pe.wait_ge(masks_done, 1)

            def causal(out, form, n):
                nc.tensor.matmul(out, identb[:], mask[:, form, 0:n], start=True, stop=False, skip_group_check=True)

            def scores_c(g):
                def step(b):
                    p = b.k % 3
                    if g == 0:
                        pe.wait_ge(spread, b.x * SPREAD + SPREAD)
                        pe.wait_ge(nspread, b.x * 16 + 16)
                    for n in range(3):
                        hold(pe, exp_done, UN, b, 3 * g + n - 1)
                        bank = ps[:, 2 + (3 * g + n) % 2]
                        if n < 2:
                            blocks = bank.rearrange("p (j n) -> p j n", j=2)
                            causal(blocks[:, :, 0:P], 1, 2)
                            for a in range(2):
                                h = HG * (2 * n + a) + g
                                mm = nc.tensor.matmul(blocks[:, a], ks[:, p, h, 0:P], qs[:, p, h, :],
                                                      start=False, stop=(a == 1), skip_group_check=True)
                        else:
                            blocks = bank.rearrange("p (j n) -> p j n", j=HJ)
                            causal(blocks, 1, HJ)
                            for j in range(HJ):
                                h = HG * j + g
                                mm = nc.tensor.matmul(blocks[:, j], ks[:, p, h, P:L], qs[:, p, h, P:L],
                                                      start=False, stop=(j == HJ - 1), skip_group_check=True)
                        mm.then_inc(c_full, 1)
                return step

            def scores_m(g):
                def step(b):
                    p = b.k % 3
                    if g == 0:
                        pe.wait_ge(spread, b.x * SPREAD + SPREAD)
                    for n in range(3):
                        hold(pe, m_read, UN, b, 3 * g + n - 1)
                        bank = ps[:, (3 * g + n) % 2]
                        if n < 2:
                            blocks = bank.rearrange("p (j n) -> p j n", j=2)
                            causal(blocks[:, :, P:L], 0, 2)
                            for a in range(2):
                                h = HG * (2 * n + a) + g
                                mm = nc.tensor.matmul(blocks[:, a], qs[0:ROWS, p, h, P:L], ks[0:ROWS, p, h, :],
                                                      start=False, stop=(a == 1), skip_group_check=True)
                        else:
                            blocks = bank.rearrange("p (j n) -> p j n", j=HJ)
                            causal(blocks, 0, HJ)
                            for j in range(HJ):
                                h = HG * j + g
                                mm = nc.tensor.matmul(blocks[:, j], qs[0:ROWS, p, h, 0:P], ks[0:ROWS, p, h, 0:P],
                                                      start=False, stop=(j == HJ - 1), skip_group_check=True)
                        mm.then_inc(m_full, 1)
                return step

            def turn_max(b):
                pe.wait_ge(m_read, b.x * UN + UN)
                hold(pe, d_read, D_STEPS, b + -1, 0)
                for k in range(TB):
                    mm = nc.tensor.transpose(ps[0:H, 7, k * P:(k + 1) * P],
                                             nmax[:, k].rearrange("p j g -> p (j g)"), ident[:])
                mm.then_inc(nT_full, 1)

            def outputs(g):
                def step(b):
                    pe.wait_ge(exp_done, b.x * UN + 3 * g + 3)
                    if g == 0:
                        pe.wait_ge(a_read, b.x * A_STEPS + A_STEPS)
                    if g % 2 == 0:
                        hold(pe, o_read, 2, b, g // 2 - 1)
                    for j in range(HJ):
                        h = HG * j + g
                        oo = ps[32 * j:32 * j + 32, 4 + g // 2, (g % 2) * L:(g % 2 + 1) * L]
                        nc.tensor.matmul(oo, vv[:, b.k % 3, 0, h, :], pr[:, g % 2, j, 0:L], start=True, stop=False,
                                         skip_group_check=True, tile_position=(0, 32 * j))
                        mm = nc.tensor.matmul(oo[:, P:L], vv[:, b.k % 3, 1, h, :], pr[:, g % 2, j, L:L + P],
                                              start=False, stop=True, skip_group_check=True,
                                              tile_position=(0, 32 * j))
                    mm.then_inc(pv_done, 1)
                return step

            def turn_tokens(b):
                hold(pe, a_read, A_STEPS, b, 0)
                pe.wait_ge(y_done, b.x + 1)
                for k in range(TB):
                    mm = nc.tensor.transpose(ps[:, 6, k * P:(k + 1) * P], y[:, k, :], ident[:])
                mm.then_inc(a_full, 1)

            def project(which):
                def step(b):
                    pe.wait_ge(a_read, b.x * A_STEPS + which + 1)
                    if which < 2:
                        for k in range(2):
                            mm = nc.tensor.matmul(ps[:, 6, k * L:(k + 1) * L], w[:, 2 * which + k, :], hT[:],
                                                  start=True, stop=True)
                    else:
                        for k in range(TB):
                            mm = nc.tensor.matmul(ps[:, 6, k * P:(k + 1) * P], hT[:, k * P:(k + 1) * P], w[:, 4, :],
                                                  start=True, stop=True)
                    mm.then_inc(a_full, 1)
                return step

            def turn_outputs(k):
                def step(b):
                    if k == 0:
                        pe.wait_ge(o_read, b.x * 2 + 2)
                        hold(pe, d_read, D_STEPS, b, 0)
                        pe.wait_ge(nT_read, b.x + 2 if b.k + 2 <= B else B)
                    else:
                        pe.wait_ge(d_read, b.x * D_STEPS + 1)
                    for g in range(HG):
                        mm = nc.tensor.transpose(ps[:, 7, g * P:(g + 1) * P], o[:, g, k * P:(k + 1) * P], ident[:])
                    mm.then_inc(d_full, 1)
                return step

            def turn_normal(b):
                pe.wait_ge(d_read, b.x * D_STEPS + 2)
                for k in range(TB):
                    mm = nc.tensor.transpose(ps[:, 7, k * P:(k + 1) * P], on[:, k].rearrange("p j g d -> p (j g d)"),
                                             ident[:])
                mm.then_inc(d_full, 1)

            def project_out(b):
                pe.wait_ge(d_read, b.x * D_STEPS + 3)
                nc.tensor.matmul(ps[:, 7, 0:L], w[:, 5, :], onT[:], start=True, stop=True).then_inc(d_full, 1)

            def turn_back(b):
                pe.wait_ge(d_read, b.x * D_STEPS + 4)
                for k in range(TB):
                    mm = nc.tensor.transpose(ps[:, 7, k * P:(k + 1) * P], yo[:, k * P:(k + 1) * P], ident[:])
                mm.then_inc(d_full, 1)

            run(pe, [("C", scores_c(0)), ("D", outputs(3)), ("M", scores_m(1)), ("S", project(2)),
                     ("D", turn_outputs(0)), ("M", scores_m(2)), ("A", turn_tokens), ("D", turn_outputs(1)),
                     ("C", scores_c(1)), ("C", outputs(0)), ("D", turn_normal), ("M", scores_m(3)),
                     ("A", project(0)), ("D", project_out), ("C", scores_c(2)), ("C", outputs(1)),
                     ("D", turn_back), ("M", turn_max), ("A", project(1)), ("N", scores_m(0)),
                     ("C", scores_c(3)), ("C", outputs(2))])

        @block.vector
        def _(v):
            v.wait_ge(loaded, 112)
            nc.vector.tensor_scalar(cosq[:], cosk[:], scale[:], None, ALU.mult)
            nc.vector.tensor_scalar(sinq[:], sink[:], scale[:], None, ALU.mult)
            nc.vector.tensor_scalar(gabo[:], modT[:, 0, 2, :], bcol[:, 4:5], None, ALU.mult)
            nc.vector.tensor_copy(mask[:], maskf[:]).then_inc(masks_done, 1)
            v.wait_ge(masks_done, 1)
            v.wait_ge(cleared, 3)

            def statistics(b):
                for k in range(TB):
                    nc.vector.bn_stats(stat[:, k, :], x[:, bass.ds(b.x * TB + k, 1), :].rearrange("p a d -> p (a d)")
                                       ).then_inc(dve_a, 1)
                v.wait_ge(dve_a, b.x * TB + TB)
                hold(v, a_read, A_STEPS, b, 0)
                nc.vector.tensor_copy(ca[:], modT[:, 0, 1, bass.ds(b.x, 1)])
                nc.vector.tensor_copy(sa[:], modT[:, 0, 0, bass.ds(b.x, 1)])
                for k in range(TB):
                    n = nc.vector.bn_aggr(mv[:, k, :], stat[:, k, :])
                n.then_inc(stats_done, 1)

            def normalise(b):
                v.wait_ge(rstd_done, b.x * 2 + 2)
                for k in range(TB):
                    n = nc.vector.tensor_scalar(y[:, k, :], x[:, bass.ds(b.x * TB + k, 1), :].rearrange("p a d -> p (a d)"),
                                                mv[:, k, 0:1], rstd[:, k:k + 1], ALU.subtract, ALU.mult)
                n.then_inc(y_done, 1)

            def rotate(which):
                def step(b):
                    cs, sn = ((cosq, sinq), (cosk, sink))[which]
                    if which == 0:
                        hold(v, split, 1, b, 0)
                    v.wait_ge(a_full, b.x * A_STEPS + 2 + which)
                    nc.vector.scalar_tensor_tensor(ra[:, which, :], ps[:, 6, 0:L], bcol[:, 2 * which:2 * which + 1],
                                                   cs[:], ALU.add, ALU.mult).then_inc(rotated, 1)
                    nc.vector.scalar_tensor_tensor(rb[:, which, :], ps[:, 6, L:2 * L],
                                                   bcol[:, 2 * which + 1:2 * which + 2], sn[:],
                                                   ALU.add, ALU.mult).then_inc(a_read, 1)
                return step

            def values(b):
                v.wait_ge(a_full, b.x * A_STEPS + 4)
                for k in range(TB):
                    n = nc.vector.tensor_tensor(vv[:, b.k % 3, k, :, 0:HD],
                                                ps[:, 6, k * P:(k + 1) * P].rearrange("p (h d) -> p h d", d=HD),
                                                bvrow[:].rearrange("p (h d) -> p h d", d=HD), ALU.add)
                n.then_inc(a_read, 1)

            def maxima(g):
                def step(b):
                    for n in range(3):
                        v.wait_ge(m_full, b.x * UN + 3 * g + n + 1)
                        bank = ps[:, (3 * g + n) % 2]
                        if n < 2:
                            dst, src = nmax[:, 1, 2 * n:2 * n + 2, g], bank.rearrange("p (j n) -> p j n", j=2)
                        else:
                            dst, src = nmax[:, 0, :, g], bank.rearrange("p (j n) -> p j n", j=HJ)
                        nc.vector.tensor_reduce(dst, src, AX_X, ALU.max, negate=True).then_inc(m_read, 1)
                return step

            def take_max(b):
                v.wait_ge(nT_full, b.x + 1)
                hold(v, nsplit, 4, b, 0)
                nc.vector.tensor_copy(nT[:, 0], ps[0:H, 7, 0:L]).then_inc(nT_read, 1)

            def divide(k):
                def step(b):
                    oT = ps[:, 7].rearrange("p (g j r) -> p g j r", g=HG, j=HJ)
                    v.wait_ge(d_full, b.x * D_STEPS + 1 + k)
                    nc.vector.reciprocal(rden[:, k], oT[:, :, :, HD]).then_inc(dve_d, 1)
                    if k == 0:
                        nc.vector.tensor_copy(ga[:, 0:1], modT[:, 0, 2, bass.ds(b.x, 1)])
                        nc.vector.tensor_copy(ga[:, 1:2], gabo[:, bass.ds(b.x, 1)])
                    v.wait_ge(dve_d, b.x * TB + k + 1)
                    nc.vector.tensor_tensor(on[:, k].rearrange("p j g d -> p g j d"), oT[:, :, :, 0:HD],
                                            rden[:, k].unsqueeze(3).to_broadcast([P, HG, HJ, HD]), ALU.mult
                                            ).then_inc(d_read, 1)
                return step

            def residual(b):
                v.wait_ge(d_full, b.x * D_STEPS + 5)
                xs = x[:, bass.ds(b.x * TB, TB), :]
                nc.vector.tensor_tensor(xs, xs, ps[:, 7, 0:L].rearrange("p (k d) -> p k d", d=D), ALU.add
                                        ).then_inc(d_read, 1)

            run(v, [("M", maxima(1)), ("S", values), ("A", statistics), ("D", divide(0)), ("M", maxima(2)),
                    ("A", normalise), ("D", divide(1)), ("M", maxima(3)), ("A", rotate(0)), ("D", residual),
                    ("M", take_max), ("A", rotate(1)), ("N", maxima(0))])


def experts0(nc, s, t, ps):
    x, modT, ident = s["x"], s["modT"], s["ident"]
    NI, K, UNITS = T // MT, MT // P, PAIRS + 1
    HALVES = MT // L
    with ExitStack() as ctx:
        def sb(name, shape, dt=F32):
            return ctx.enter_context(nc.sbuf_tensor("e0_" + name, shape, dt))

        def sem(name):
            return ctx.enter_context(nc.semaphore("e0_" + name))

        wg, wu, wd = sb("wg", [P, UNITS, P]), sb("wu", [P, UNITS, P]), sb("wd", [P, UNITS, D])
        wr = sb("wr", [P, E0])
        bias = sb("bias", [P, E0])
        pairf, pair = sb("pairf", [96, PAIRS, P]), sb("pair", [96, PAIRS, P], BF16)
        gb, cb, sbb = sb("gb", [P, HALVES]), sb("cb", [P, HALVES]), sb("sb", [P, HALVES])
        stat, mv, rstd = sb("stat", [P, K, 6]), sb("mv", [P, K, 2]), sb("rstd", [P, K])
        y, hT = sb("y", [P, K, D]), sb("hT", [P, MT])
        mx, ex, den, rw = sb("mx", [P, K]), sb("ex", [P, K, E0]), sb("den", [P, K]), sb("rw", [P, K, E0])
        cor = sb("cor", [P, K, E0 + 2])
        top, rep, sel = sb("top", [P, K, 8]), sb("rep", [P, K, E0 + 2]), sb("sel", [P, K, E0])
        rest, c3 = sb("rest", [E0, 2, MT]), sb("c3", [96, MT], BF16)
        sg, hm = sb("sg", [P, 2, MT]), sb("hm", [P, 2, MT])
        pause = sb("pause", [P, 1])
        up = sb("up", [P, 2, MT])
        yo = sb("yo", [P, MT])

        loaded = sem("loaded")
        stats_done, rstd_done, y_done, mod_done = sem("stats_done"), sem("rstd_done"), sem("y_done"), sem("mod_done")
        small_full, small_free = sem("small_full"), sem("small_free")
        logits_done, exp_done, comb_done, split_done = sem("logits"), sem("exp"), sem("comb"), sem("split")
        unit_full = sem("unit_full")
        silu_done = sem("silu_done")
        hidden_done = sem("hidden_done")
        down_done = sem("down_done")
        up_done = sem("up_done")
        sum_read, dve, setup = sem("sum_read"), sem("dve"), sem("setup")
        block = ctx.enter_context(nc.Block())
        DVE, SMALL = 25, 4

        @block.sync
        def _(sp):
            for dst, name in ((wg, "e0_wg"), (wu, "e0_wu"), (wd, "e0_wd"), (wr, "e0_wr"), (pairf, "c_pair")):
                sp.dma_start(dst[:], t[name]).then_inc(loaded, 16)
            sp.dma_start(bias[:], t["L0_ffn_e_score_bias"].partition_broadcast(P)).then_inc(loaded, 16)

        @block.gpsimd
        def _(pool):
            with pool.Fori(0, NI) as i:
                pool.wait_ge(stats_done, i + 1)
                nc.gpsimd.tensor_tensor(rstd[:], mv[:, :, 1], s["eps"][:, 0:K], ALU.add).then_inc(rstd_done, 1)
                pool.wait_ge(rstd_done, i * 2 + 1)
                nc.gpsimd.tensor_tensor(rstd[:], rstd[:], s["pm5"][:, 0:K], ALU.pow).then_inc(rstd_done, 1)

        @block.scalar
        def _(act):
            with act.Fori(0, NI) as i:
                act.wait_ge(mod_done, i + 1)
                act.wait_ge(small_full, i * SMALL + 1)
                for k in range(HALVES):
                    a = nc.scalar.activation(hT[:, k * L:(k + 1) * L], ps[:, 1, k * L:(k + 1) * L], ACT.Identity,
                                             bias=sbb[:, k:k + 1], scale=cb[:, k:k + 1])
                a.then_inc(small_free, 1)
                act.wait_ge(logits_done, i + 1)
                nc.scalar.activation(ex[:], ex[:], ACT.Exp).then_inc(exp_done, 1)
                for u in range(UNITS):
                    act.wait_ge(unit_full, i * UNITS + u + 1)
                    if u >= 2:
                        act.wait_ge(hidden_done, i * UNITS + u - 1)
                    nc.scalar.activation(sg[:, u % 2], ps[:, 2 + u % 2], ACT.Silu).then_inc(silu_done, 1)
                act.wait_ge(down_done, (i + 1) * UNITS)
                for k in range(HALVES):
                    a = nc.scalar.activation(yo[:, k * L:(k + 1) * L], ps[:, 0, k * L:(k + 1) * L], ACT.Copy,
                                             scale=gb[:, k:k + 1])
                a.then_inc(sum_read, 1)

        @block.tensor
        def _(pe):
            pe.wait_ge(setup, 1)
            with pe.Fori(0, NI) as i:
                pe.wait_ge(small_free, i * SMALL + 1)
                pe.wait_ge(y_done, i + 1)
                for k in range(K):
                    mm = nc.tensor.transpose(ps[:, 1, k * P:(k + 1) * P], y[:, k, :], ident[:])
                mm.then_inc(small_full, 1)
                pe.wait_ge(small_free, i * SMALL + 2)
                for k in range(K):
                    mm = nc.tensor.matmul(ps[:, 1, k * E0:(k + 1) * E0], hT[:, k * P:(k + 1) * P], wr[:],
                                          start=True, stop=True)
                mm.then_inc(small_full, 1)
                for u in range(UNITS + 1):
                    if u < UNITS:
                        if u >= 2:
                            pe.wait_ge(hidden_done, i * UNITS + u - 1)
                        nc.tensor.matmul(ps[:, 2 + u % 2, :], wg[:, u, :], hT[:], start=True, stop=True)
                        mm = nc.tensor.matmul(ps[:, 4 + u % 2, :], wu[:, u, :], hT[:], start=True, stop=True)
                        if u == 1:
                            pe.wait_ge(small_free, i * SMALL + 3)
                            pe.wait_ge(comb_done, i + 1)
                            for k in range(K):
                                tr = nc.tensor.transpose(ps[0:E0, 1, k * P:(k + 1) * P], sel[:, k, :], ident[:])
                            tr.then_inc(small_full, 1)
                            pe.wait_ge(split_done, i + 1)
                        if u >= 1:
                            mm = nc.tensor.matmul(ps[:, 6 + u % 2, :], pair[:, u - 1, :], c3[:], start=True, stop=True)
                        mm.then_inc(unit_full, 1)
                    if u >= 1:
                        pe.wait_ge(hidden_done, i * UNITS + u)
                        nc.tensor.matmul(ps[:, 0, :], wd[:, u - 1, :], hm[:, (u - 1) % 2, :],
                                         start=(u == 1), stop=(u == UNITS), skip_group_check=True
                                         ).then_inc(down_done, 1)
                pe.wait_ge(sum_read, i + 1)
                pe.wait_ge(small_free, i * SMALL + 4)
                for k in range(K):
                    mm = nc.tensor.transpose(ps[:, 1, k * P:(k + 1) * P], yo[:, k * P:(k + 1) * P], ident[:])
                mm.then_inc(small_full, 1)

        @block.vector
        def _(v):
            v.wait_ge(loaded, 96)
            nc.vector.memset(cor[:], NEG)
            nc.vector.tensor_copy(pair[:], pairf[:]).then_inc(setup, 1)
            nc.vector.memset(mx[:], 0.0).then_inc(small_free, 1)
            v.wait_ge(small_free, 1)
            with v.Fori(0, NI) as i:
                c = Count(i * DVE)
                for k in range(K):
                    nc.vector.bn_stats(stat[:, k, :], x[:, bass.ds(i * K + k, 1), :].rearrange("p a d -> p (a d)")
                                       ).then_inc(dve, c.up())
                v.wait_ge(dve, c.now())
                nc.vector.tensor_copy(gb[:], modT[:, 0, 5, bass.ds(i * HALVES, HALVES)])
                nc.vector.tensor_copy(cb[:], modT[:, 0, 4, bass.ds(i * HALVES, HALVES)])
                nc.vector.tensor_copy(sbb[:], modT[:, 0, 3, bass.ds(i * HALVES, HALVES)]).then_inc(mod_done, 1)
                for k in range(K):
                    n = nc.vector.bn_aggr(mv[:, k, :], stat[:, k, :])
                n.then_inc(stats_done, 1)
                v.wait_ge(rstd_done, i * 2 + 2)
                for k in range(K):
                    n = nc.vector.tensor_scalar(y[:, k, :], x[:, bass.ds(i * K + k, 1), :].rearrange("p a d -> p (a d)"),
                                                mv[:, k, 0:1], rstd[:, k:k + 1], ALU.subtract, ALU.mult)
                n.then_inc(y_done, 1)
                v.wait_ge(small_full, i * SMALL + 2)
                lg = ps[:, 1, 0:K * E0].rearrange("p (k e) -> p k e", e=E0)
                wide = [P, K, E0]
                nc.vector.tensor_reduce(mx[:], lg, AX_X, ALU.max).then_inc(dve, c.up())
                v.wait_ge(dve, c.now())
                nc.vector.tensor_tensor(ex[:], lg, mx[:].unsqueeze(2).to_broadcast(wide), ALU.subtract
                                        ).then_inc(logits_done, 1)
                v.wait_ge(exp_done, i + 1)
                nc.vector.tensor_reduce(den[:], ex[:], AX_X, ALU.add).then_inc(dve, c.up())
                v.wait_ge(dve, c.now())
                nc.vector.reciprocal(den[:], den[:]).then_inc(dve, c.up())
                v.wait_ge(dve, c.now())
                nc.vector.tensor_tensor(rw[:], ex[:], den[:].unsqueeze(2).to_broadcast(wide), ALU.mult
                                        ).then_inc(dve, c.up())
                v.wait_ge(dve, c.now())
                nc.vector.tensor_tensor(cor[:, :, 0:E0], rw[:], bias[:].unsqueeze(1).to_broadcast(wide), ALU.add
                                        ).then_inc(dve, c.up())
                v.wait_ge(dve, c.now())
                nc.vector.memset(pause[:], 0.0)
                for k in range(K):
                    nc.vector.max(top[:, k, :], cor[:, k, :]).then_inc(dve, c.up())
                v.wait_ge(dve, c.now())
                nc.vector.memset(top[:, :, TOP_K:8], NEG).then_inc(dve, c.up())
                v.wait_ge(dve, c.now())
                nc.vector.memset(pause[:], 0.0)
                for k in range(K):
                    nc.vector.match_replace(rep[:, k, :], top[:, k, :], cor[:, k, :], -NEG).then_inc(dve, c.up())
                v.wait_ge(dve, c.now())
                nc.vector.tensor_tensor(sel[:], rep[:, :, 0:E0], cor[:, :, 0:E0], ALU.not_equal).then_inc(dve, c.up())
                v.wait_ge(dve, c.now())
                nc.vector.tensor_tensor(sel[:], sel[:], rw[:], ALU.mult).then_inc(dve, c.up())
                v.wait_ge(dve, c.now())
                nc.vector.tensor_reduce(den[:], sel[:], AX_X, ALU.add).then_inc(dve, c.up())
                v.wait_ge(dve, c.now())
                nc.vector.tensor_scalar(den[:], den[:], NORM_MIN, None, ALU.max).then_inc(dve, c.up())
                v.wait_ge(dve, c.now())
                nc.vector.reciprocal(den[:], den[:]).then_inc(small_free, 1)
                v.wait_ge(small_free, i * SMALL + 3)
                nc.vector.tensor_tensor(sel[:], sel[:], den[:].unsqueeze(2).to_broadcast(wide), ALU.mult
                                        ).then_inc(comb_done, 1)
                v.wait_ge(small_full, i * SMALL + 3)
                cT = ps[0:E0, 1, :]
                nc.vector.tensor_copy(c3[0:E0, :], cT).then_inc(dve, c.up())
                v.wait_ge(dve, c.now())
                nc.vector.tensor_tensor(rest[:, 0, :], cT, c3[0:E0, :], ALU.subtract).then_inc(dve, c.up())
                v.wait_ge(dve, c.now())
                nc.vector.tensor_copy(c3[E0:2 * E0, :], rest[:, 0, :]).then_inc(dve, c.up())
                v.wait_ge(dve, c.now())
                nc.vector.tensor_tensor(rest[:, 1, :], rest[:, 0, :], c3[E0:2 * E0, :], ALU.subtract
                                        ).then_inc(small_free, 1)
                v.wait_ge(small_free, i * SMALL + 4)
                nc.vector.tensor_copy(c3[2 * E0:3 * E0, :], rest[:, 1, :]).then_inc(split_done, 1)
                for u in range(UNITS):
                    v.wait_ge(silu_done, i * UNITS + u + 1)
                    if u >= 2:
                        v.wait_ge(down_done, i * UNITS + u - 1)
                    if u == 0:
                        nc.vector.tensor_tensor(hm[:, 0], sg[:, 0], ps[:, 4], ALU.mult).then_inc(hidden_done, 1)
                        continue
                    nc.vector.tensor_tensor(up[:, u % 2], sg[:, u % 2], ps[:, 4 + u % 2], ALU.mult
                                            ).then_inc(up_done, 1)
                    v.wait_ge(up_done, i * PAIRS + u)
                    nc.vector.tensor_tensor(hm[:, u % 2], up[:, u % 2], ps[:, 6 + u % 2], ALU.mult
                                            ).then_inc(hidden_done, 1)
                v.wait_ge(small_full, i * SMALL + 4)
                xs = x[:, bass.ds(i * K, K), :]
                nc.vector.tensor_tensor(xs, xs, ps[:, 1, :].rearrange("p (k d) -> p k d", d=D), ALU.add
                                        ).then_inc(small_free, 1)
                assert c.n == DVE, c.n


def experts1(nc, s, t, ps):
    x, modT, ident = s["x"], s["modT"], s["ident"]
    NI, K = T // MT, MT // P
    HALVES = MT // L
    with ExitStack() as ctx:
        def sb(name, shape, dt=F32):
            return ctx.enter_context(nc.sbuf_tensor("e1_" + name, shape, dt))

        def sem(name):
            return ctx.enter_context(nc.semaphore("e1_" + name))

        w1, w2 = sb("w1", [P, E1, D]), sb("w2", [P, E1, D])
        b1, b2 = sb("b1", [P, E1]), sb("b2", [E1, D])
        wr, br = sb("wr", [P, E1]), sb("br", [P, E1])
        rank = sb("rank", [P, E1])
        onef, one = sb("onef", [96, E1 + 1, P]), sb("one", [96, E1 + 1, P], BF16)
        uptof, upto, ones = sb("uptof", [P, P]), sb("upto", [P, P], BF16), sb("ones", [P, P], BF16)
        gb, cb, sbb = sb("gb", [P, HALVES]), sb("cb", [P, HALVES]), sb("sb", [P, HALVES])
        stat, mv, rstd = sb("stat", [P, K, 6]), sb("mv", [P, K, 2]), sb("rstd", [P, K])
        y, hT, hg = sb("y", [P, K, D]), sb("hT", [P, MT]), sb("hg", [P, MT])
        lg, mx, den = sb("lg", [P, K, E1]), sb("mx", [P, K]), sb("den", [P, K])
        ex, oh, wt = sb("ex", [P, K, E1]), sb("oh", [P, K, E1]), sb("wt", [P, K, E1])
        gate = sb("gate", [P, K])
        ohb = sb("ohb", [P, K, E1], BF16)
        before = sb("before", [P, K + 1, E1])
        beforeb = sb("beforeb", [P, K, E1], BF16)
        rest, c3, wT = sb("rest", [E1, 2, MT]), sb("c3", [96, MT], BF16), sb("wT", [E1, MT])
        r, hm = sb("r", [P, 2, MT]), sb("hm", [P, 2, MT])
        yo = sb("yo", [P, MT])

        loaded = sem("loaded")
        stats_done, rstd_done, y_done, mod_done = sem("stats_done"), sem("rstd_done"), sem("y_done"), sem("mod_done")
        small_full, small_free = sem("small_full"), sem("small_free")
        logits_done, exp_done, chosen, w_done = sem("logits"), sem("exp"), sem("chosen"), sem("w_done")
        counted, split_done = sem("counted"), sem("split")
        sum_full, hg_done = sem("sum_full"), sem("hg_done")
        unit_full, relu_done, hidden_done = sem("unit_full"), sem("relu_done"), sem("hidden_done")
        down_done = sem("down_done")
        out_read, dve, setup = sem("out_read"), sem("dve"), sem("setup")
        block = ctx.enter_context(nc.Block())
        DVE, SMALL = 25, 4

        @block.sync
        def _(sp):
            for dst, name in ((w1, "e1_w1"), (w2, "e1_w2"), (b1, "e1_b1"), (b2, "L1_ffn_b2"), (wr, "L1_ffn_Wr"),
                              (onef, "c_one"), (uptof, "c_upto")):
                sp.dma_start(dst[:], t[name]).then_inc(loaded, 16)
            sp.dma_start(br[:], t["L1_ffn_br"].partition_broadcast(P)).then_inc(loaded, 16)

        @block.gpsimd
        def _(pool):
            with pool.Fori(0, NI) as i:
                pool.wait_ge(stats_done, i + 1)
                nc.gpsimd.tensor_tensor(rstd[:], mv[:, :, 1], s["eps"][:, 0:K], ALU.add).then_inc(rstd_done, 1)
                pool.wait_ge(rstd_done, i * 2 + 1)
                nc.gpsimd.tensor_tensor(rstd[:], rstd[:], s["pm5"][:, 0:K], ALU.pow).then_inc(rstd_done, 1)

        @block.scalar
        def _(act):
            with act.Fori(0, NI) as i:
                act.wait_ge(mod_done, i + 1)
                act.wait_ge(small_full, i * SMALL + 1)
                for k in range(HALVES):
                    a = nc.scalar.activation(hT[:, k * L:(k + 1) * L], ps[:, 1, k * L:(k + 1) * L], ACT.Identity,
                                             bias=sbb[:, k:k + 1], scale=cb[:, k:k + 1])
                a.then_inc(small_free, 1)
                act.wait_ge(logits_done, i + 1)
                nc.scalar.activation(ex[:], ex[:], ACT.Exp).then_inc(exp_done, 1)
                for u in range(E1):
                    act.wait_ge(unit_full, i * E1 + u + 1)
                    if u >= 2:
                        act.wait_ge(hidden_done, i * E1 + u - 1)
                    nc.scalar.activation(r[:, u % 2], ps[:, 2 + u % 2], ACT.Relu, bias=b1[:, u:u + 1]
                                         ).then_inc(relu_done, 1)
                act.wait_ge(down_done, (i + 1) * E1)
                for k in range(HALVES):
                    a = nc.scalar.activation(yo[:, k * L:(k + 1) * L], ps[:, 0, k * L:(k + 1) * L], ACT.Copy,
                                             scale=gb[:, k:k + 1])
                a.then_inc(out_read, 1)

        @block.tensor
        def _(pe):
            pe.wait_ge(setup, 1)
            with pe.Fori(0, NI) as i:
                pe.wait_ge(small_free, i * SMALL + 1)
                pe.wait_ge(y_done, i + 1)
                for k in range(K):
                    mm = nc.tensor.transpose(ps[:, 1, k * P:(k + 1) * P], y[:, k, :], ident[:])
                mm.then_inc(small_full, 1)
                pe.wait_ge(small_free, i * SMALL + 2)
                for k in range(K):
                    mm = nc.tensor.matmul(ps[:, 1, k * E1:(k + 1) * E1], hT[:, k * P:(k + 1) * P], wr[:],
                                          start=True, stop=True)
                mm.then_inc(small_full, 1)
                pe.wait_ge(chosen, i + 1)
                nc.tensor.matmul(ps[:, 7, 0:K * E1], upto[:], ohb[:].rearrange("p k e -> p (k e)"),
                                 start=True, stop=False)
                nc.tensor.matmul(ps[:, 7, 0:K * E1], ones[:], beforeb[:].rearrange("p k e -> p (k e)"),
                                 start=False, stop=True).then_inc(counted, 1)
                pe.wait_ge(w_done, i + 1)
                pe.wait_ge(small_free, i * SMALL + 3)
                for k in range(K):
                    mm = nc.tensor.transpose(ps[0:E1, 1, k * P:(k + 1) * P], wt[:, k, :], ident[:])
                mm.then_inc(small_full, 1)
                pe.wait_ge(split_done, i + 1)
                nc.tensor.matmul(ps[:, 6, :], one[:, E1, :], c3[:], start=True, stop=True).then_inc(sum_full, 1)
                nc.tensor.matmul(ps[:, 0, :], b2[:], wT[:], start=True, stop=False, skip_group_check=True)
                pe.wait_ge(hg_done, i + 1)
                for u in range(E1 + 1):
                    if u < E1:
                        if u >= 2:
                            pe.wait_ge(hidden_done, i * E1 + u - 1)
                        nc.tensor.matmul(ps[:, 2 + u % 2, :], w1[:, u, :], hg[:], start=True, stop=True)
                        nc.tensor.matmul(ps[:, 4 + u % 2, :], one[:, u, :], c3[:], start=True, stop=True
                                         ).then_inc(unit_full, 1)
                    if u >= 1:
                        pe.wait_ge(hidden_done, i * E1 + u)
                        nc.tensor.matmul(ps[:, 0, :], w2[:, u - 1, :], hm[:, (u - 1) % 2, :],
                                         start=False, stop=(u == E1), skip_group_check=True).then_inc(down_done, 1)
                pe.wait_ge(out_read, i + 1)
                pe.wait_ge(small_free, i * SMALL + 4)
                for k in range(K):
                    mm = nc.tensor.transpose(ps[:, 1, k * P:(k + 1) * P], yo[:, k * P:(k + 1) * P], ident[:])
                mm.then_inc(small_full, 1)

        @block.vector
        def _(v):
            v.wait_ge(loaded, 128)
            nc.vector.memset(ones[:], 1.0)
            nc.vector.memset(before[:], 0.0)
            nc.vector.memset(c3[:], 0.0)
            for e in range(E1):
                nc.vector.memset(rank[:, e:e + 1], float(E1 - e))
            nc.vector.tensor_copy(one[:], onef[:])
            nc.vector.tensor_copy(upto[:], uptof[:]).then_inc(setup, 1)
            nc.vector.memset(mx[:], 0.0).then_inc(small_free, 1)
            v.wait_ge(small_free, 1)
            with v.Fori(0, NI) as i:
                c = Count(i * DVE)
                for k in range(K):
                    nc.vector.bn_stats(stat[:, k, :], x[:, bass.ds(i * K + k, 1), :].rearrange("p a d -> p (a d)")
                                       ).then_inc(dve, c.up())
                v.wait_ge(dve, c.now())
                nc.vector.tensor_copy(gb[:], modT[:, 1, 5, bass.ds(i * HALVES, HALVES)])
                nc.vector.tensor_copy(cb[:], modT[:, 1, 4, bass.ds(i * HALVES, HALVES)])
                nc.vector.tensor_copy(sbb[:], modT[:, 1, 3, bass.ds(i * HALVES, HALVES)]).then_inc(mod_done, 1)
                for k in range(K):
                    n = nc.vector.bn_aggr(mv[:, k, :], stat[:, k, :])
                n.then_inc(stats_done, 1)
                v.wait_ge(rstd_done, i * 2 + 2)
                for k in range(K):
                    n = nc.vector.tensor_scalar(y[:, k, :], x[:, bass.ds(i * K + k, 1), :].rearrange("p a d -> p (a d)"),
                                                mv[:, k, 0:1], rstd[:, k:k + 1], ALU.subtract, ALU.mult)
                n.then_inc(y_done, 1)
                v.wait_ge(small_full, i * SMALL + 2)
                wide = [P, K, E1]
                nc.vector.tensor_tensor(lg[:], ps[:, 1, 0:K * E1].rearrange("p (k e) -> p k e", e=E1),
                                        br[:].unsqueeze(1).to_broadcast(wide), ALU.add).then_inc(small_free, 1)
                v.wait_ge(small_free, i * SMALL + 3)
                nc.vector.tensor_reduce(mx[:], lg[:], AX_X, ALU.max).then_inc(dve, c.up())
                v.wait_ge(dve, c.now())
                nc.vector.tensor_tensor(ex[:], lg[:], mx[:].unsqueeze(2).to_broadcast(wide), ALU.subtract
                                        ).then_inc(logits_done, 1)
                v.wait_ge(exp_done, i + 1)
                nc.vector.tensor_reduce(den[:], ex[:], AX_X, ALU.add).then_inc(dve, c.up())
                v.wait_ge(dve, c.now())
                nc.vector.reciprocal(den[:], den[:]).then_inc(dve, c.up())
                v.wait_ge(dve, c.now())
                nc.vector.tensor_tensor(ex[:], ex[:], den[:].unsqueeze(2).to_broadcast(wide), ALU.mult
                                        ).then_inc(dve, c.up())
                v.wait_ge(dve, c.now())
                nc.vector.tensor_reduce(gate[:], ex[:], AX_X, ALU.max).then_inc(dve, c.up())
                v.wait_ge(dve, c.now())
                nc.vector.tensor_tensor(oh[:], ex[:], gate[:].unsqueeze(2).to_broadcast(wide), ALU.is_equal
                                        ).then_inc(dve, c.up())
                v.wait_ge(dve, c.now())
                nc.vector.tensor_tensor(oh[:], oh[:], rank[:].unsqueeze(1).to_broadcast(wide), ALU.mult
                                        ).then_inc(dve, c.up())
                v.wait_ge(dve, c.now())
                nc.vector.tensor_reduce(mx[:], oh[:], AX_X, ALU.max).then_inc(dve, c.up())
                v.wait_ge(dve, c.now())
                nc.vector.tensor_tensor(oh[:], oh[:], mx[:].unsqueeze(2).to_broadcast(wide), ALU.is_equal
                                        ).then_inc(dve, c.up())
                v.wait_ge(dve, c.now())
                for k in range(K):
                    nc.vector.tensor_tensor(before[:, k + 1, :], before[:, k, :], oh[:, k, :], ALU.add
                                            ).then_inc(dve, c.up())
                    v.wait_ge(dve, c.now())
                nc.vector.tensor_copy(ohb[:], oh[:]).then_inc(dve, c.up())
                nc.vector.tensor_copy(beforeb[:], before[:, 0:K, :]).then_inc(chosen, 1)
                v.wait_ge(chosen, i + 1)
                nc.vector.tensor_copy(before[:, 0, :], before[:, K, :]).then_inc(dve, c.up())
                nc.vector.tensor_tensor(wt[:], oh[:], gate[:].unsqueeze(2).to_broadcast(wide), ALU.mult
                                        ).then_inc(dve, c.up())
                v.wait_ge(dve, c.now())
                v.wait_ge(counted, i + 1)
                nc.vector.tensor_scalar(oh[:], ps[:, 7, 0:K * E1].rearrange("p (k e) -> p k e", e=E1), float(CAP),
                                        None, ALU.is_lt).then_inc(dve, c.up())
                v.wait_ge(dve, c.now())
                nc.vector.tensor_tensor(wt[:], wt[:], oh[:], ALU.mult).then_inc(w_done, 1)
                v.wait_ge(small_full, i * SMALL + 3)
                nc.vector.tensor_copy(wT[:], ps[0:E1, 1, :]).then_inc(small_free, 1)
                v.wait_ge(small_free, i * SMALL + 4)
                nc.vector.tensor_copy(c3[0:E1, :], wT[:]).then_inc(dve, c.up())
                v.wait_ge(dve, c.now())
                nc.vector.tensor_tensor(rest[:, 0, :], wT[:], c3[0:E1, :], ALU.subtract).then_inc(dve, c.up())
                v.wait_ge(dve, c.now())
                nc.vector.tensor_copy(c3[32:32 + E1, :], rest[:, 0, :]).then_inc(dve, c.up())
                v.wait_ge(dve, c.now())
                nc.vector.tensor_tensor(rest[:, 1, :], rest[:, 0, :], c3[32:32 + E1, :], ALU.subtract
                                        ).then_inc(dve, c.up())
                v.wait_ge(dve, c.now())
                nc.vector.tensor_copy(c3[64:64 + E1, :], rest[:, 1, :]).then_inc(split_done, 1)
                v.wait_ge(sum_full, i + 1)
                nc.vector.tensor_tensor(hg[:], hT[:], ps[:, 6, :], ALU.mult).then_inc(hg_done, 1)
                for u in range(E1):
                    v.wait_ge(relu_done, i * E1 + u + 1)
                    if u >= 2:
                        v.wait_ge(down_done, i * E1 + u - 1)
                    nc.vector.tensor_tensor(hm[:, u % 2], r[:, u % 2], ps[:, 4 + u % 2], ALU.mult
                                            ).then_inc(hidden_done, 1)
                v.wait_ge(small_full, i * SMALL + 4)
                xs = x[:, bass.ds(i * K, K), :]
                nc.vector.tensor_tensor(xs, xs, ps[:, 1, :].rearrange("p (k d) -> p k d", d=D), ALU.add
                                        ).then_inc(small_free, 1)
                assert c.n == DVE, c.n


def attention1(nc, s, t, ps):
    x, modT, ident = s["x"], s["modT"], s["ident"]
    UNITS = [list(range(a, min(a + 4, NO))) for a in range(0, NO, 4)]
    NU = len(UNITS)
    GUNITS = [NU - 3, NU - 2]
    VUNITS = [u for u in range(NU) if u not in GUNITS]
    NG, NV = len(GUNITS), len(VUNITS)
    RING = NU - 1
    W = NO * H
    WK = -(-W // 64) * 64
    INV = float(1.0 / np.sqrt(np.float32(HD)))
    assert NU % 2 == 0
    with ExitStack() as ctx:
        def sb(name, shape, dt=F32):
            return ctx.enter_context(nc.sbuf_tensor("a1_" + name, shape, dt))

        def sem(name):
            return ctx.enter_context(nc.semaphore("a1_" + name))

        w = sb("w", [P, 5, D])
        bcol = sb("bcol", [P, 5])
        hbg = sb("hbg", [P, 1])
        ifg = sb("ifg", [P, 1])
        inv = sb("inv", [P, 1])
        emb = sb("emb", [P, W])
        headsum = sb("headsum", [P, 7 * H])
        pb = sb("pb", [P, TB, W])
        pbr = sb("pbr", [P, W])
        early = sb("early", [P, TB, NO])
        gabo = sb("gabo", [P, B])
        ga, ca, sa = sb("ga", [P, 2]), sb("ca", [P, 1]), sb("sa", [P, 1])
        stat, mv, rstd = sb("stat", [P, TB, 6]), sb("mv", [P, TB, 2]), sb("rstd", [P, TB])
        y, hT = sb("y", [P, TB, D]), sb("hT", [P, L])
        q = sb("q", [P, 3, L])
        kp, vp = sb("kp", [P, 3, PAD + L]), sb("vp", [P, 3, PAD + L])
        gs = sb("gs", [P, 3, L])
        acc = sb("acc", [P, 3, 4, L])
        th = sb("th", [P, L])
        prod = sb("prod", [P, NO, L])
        g = sb("g", [P, TB * W])
        lg = sb("lg", [P, TB * W])
        mx, den = sb("mx", [P, TB, H]), sb("den", [P, TB, H])
        pe8 = sb("pe8", [P, TB, W, HD])
        denw = sb("denw", [P, TB, D])
        yv = sb("yv", [P, RING, 4, L])
        og = sb("og", [P, L])
        yo = sb("yo", [P, L])

        loaded, setup = sem("loaded"), sem("setup")
        stats_done, rstd_done, y_done = sem("stats_done"), sem("rstd_done"), sem("y_done")
        a_full, a_read = sem("a_full"), sem("a_read")
        g_full, g_read = sem("g_full"), sem("g_read")
        d_full, d_read = sem("d_full"), sem("d_read")
        r_full, r_read = sem("r_full"), sem("r_read")
        th_done, gs_done = sem("th_done"), sem("gs_done")
        prod_v, prod_g = sem("prod_v"), sem("prod_g")
        qk_full, qk_read = sem("qk_full"), sem("qk_read")
        biased, max_done, shifted = sem("biased"), sem("max_done"), sem("shifted")
        exp_done = sem("exp_done")
        pv_full, pv_read = sem("pv_full"), sem("pv_read")
        added = sem("added")
        summed, den_done = sem("summed"), sem("den_done")
        og_done = sem("og_done")
        dve_a = sem("dve_a")
        block = ctx.enter_context(nc.Block())
        A, G, DD = 3, 3, 2

        def shift(pad, b, o0, n):
            a = pad[:, b.k % 3, PAD - ORDER[o0]:PAD - ORDER[o0] + L]
            return bass.AP(tensor=a.tensor, offset=a.offset, ap=[list(a.ap[0]), [1, n], [1, L]])

        def runs(unit):
            out = []
            for o in unit:
                if out and ORDER[o] == ORDER[out[-1][0] + out[-1][1] - 1] - 1:
                    out[-1][1] += 1
                else:
                    out.append([o, 1])
            return out

        def latest(b, n):
            return b + n if b.k + n < B else Batch(B - 1, B - 1)

        def run(eng, order):
            ahead = {"D": -1, "V": 0, "R": 0, "Q": 1, "A": 2, "N": 2}

            def body(b):
                for stage, step in order:
                    c = b + ahead[stage]
                    if 0 <= c.k < B:
                        step(c)
            pipeline(eng, -2, B + 1, 1, B - 2, body)

        @block.sync
        def _(sp):
            for dst, name in ((w, "a1_w"), (bcol, "a1_b"), (ifg, "a1_ifg"), (emb, "a1_emb"), (headsum, "c_headsum"),
                              (early, "c_early")):
                sp.dma_start(dst[:], t[name]).then_inc(loaded, 16)
            sp.dma_start(pbr[:], t["a1_pb"].partition_broadcast(P)).then_inc(loaded, 16)

        @block.gpsimd
        def _(pool):
            nc.gpsimd.memset(inv[:], INV)
            nc.gpsimd.memset(kp[:, :, 0:PAD], 0.0)
            nc.gpsimd.memset(vp[:, :, 0:PAD], 0.0).then_inc(setup, 1)
            pool.wait_ge(setup, 2)

            def rstd_of(b):
                pool.wait_ge(stats_done, b.x + 1)
                nc.gpsimd.tensor_tensor(rstd[:], mv[:, :, 1], s["eps"][:, 0:TB], ALU.add).then_inc(rstd_done, 1)
                pool.wait_ge(rstd_done, b.x * 2 + 1)
                nc.gpsimd.tensor_tensor(rstd[:], rstd[:], s["pm5"][:, 0:TB], ALU.pow).then_inc(rstd_done, 1)

            def products(u):
                def step(b):
                    pool.wait_ge(a_read, b.x * A + 2)
                    hold(pool, qk_full, 1, b, 0)
                    for o0, n in runs(UNITS[u]):
                        m = nc.gpsimd.tensor_tensor(prod[:, o0:o0 + n, :],
                                                    q[:, b.k % 3].unsqueeze(1).to_broadcast([P, n, L]),
                                                    shift(kp, b, o0, n), ALU.mult)
                    m.then_inc(prod_g, 1)
                return step

            def add(u):
                def step(b):
                    a = acc[:, b.k % 3]
                    if u < NU:
                        n = len(UNITS[u])
                        pool.wait_ge(pv_read, b.x * NU + u + 1)
                        hold(pool, added, NU + 1, b, u - 1)
                        nc.gpsimd.tensor_tensor(a[:, 0:n], a[:, 0:n], yv[:, (u - 1) % RING, 0:n], ALU.add
                                                ).then_inc(added, 1)
                    else:
                        pool.wait_ge(added, b.x * (NU + 1) + NU - 1)
                        nc.gpsimd.tensor_tensor(a[:, 0:2], a[:, 0:2], a[:, 2:4], ALU.add).then_inc(added, 1)
                        pool.wait_ge(added, b.x * (NU + 1) + NU)
                        nc.gpsimd.tensor_tensor(a[:, 0], a[:, 0], a[:, 1], ALU.add).then_inc(added, 1)
                return step

            run(pool, [("Q", products(GUNITS[0]))] + [("V", add(1)), ("A", rstd_of), ("V", add(2)),
                 ("V", add(3)), ("Q", products(GUNITS[1]))] + [("V", add(u)) for u in range(4, NU + 1)])

        @block.scalar
        def _(act):
            act.wait_ge(setup, 2)

            def modulate(b):
                act.wait_ge(a_full, b.x * A + 1)
                nc.scalar.activation(hT[:], ps[:, 7, 0:L], ACT.Identity, bias=sa[:], scale=ca[:]).then_inc(a_read, 1)

            def queries_keys(b):
                act.wait_ge(a_full, b.x * A + 2)
                hold(act, qk_full, 1, b + -2, 0)
                nc.scalar.activation(q[:, b.k % 3], ps[:, 7, 0:L], ACT.Identity, bias=bcol[:, 0:1])
                nc.scalar.activation(kp[:, b.k % 3, PAD:], ps[:, 7, L:2 * L], ACT.Identity, bias=bcol[:, 1:2]
                                     ).then_inc(a_read, 1)

            def values_gate(b):
                act.wait_ge(a_full, b.x * A + 3)
                hold(act, pv_read, NU, b + -2, 0)
                hold(act, og_done, 1, b + -2, 0)
                nc.scalar.activation(th[:], ps[:, 7, L:2 * L], ACT.Tanh, bias=hbg[:], scale=0.5).then_inc(th_done, 1)
                nc.scalar.activation(vp[:, b.k % 3, PAD:], ps[:, 7, 0:L], ACT.Identity, bias=bcol[:, 2:3]
                                     ).then_inc(a_read, 1)
                act.wait_ge(th_done, b.x + 1)
                nc.scalar.activation(gs[:, b.k % 3], th[:], ACT.Identity, bias=ifg[:], scale=ifg[:]
                                     ).then_inc(gs_done, 1)

            def factors(n):
                def step(b):
                    cols = slice(512 * n, min(512 * n + 512, TB * W))
                    act.wait_ge(g_full, b.x * G + n + 1)
                    hold(act, qk_read, 1, b, 0)
                    nc.scalar.activation(g[:, cols], ps[:, 7, 0:cols.stop - cols.start], ACT.Identity,
                                         bias=inv[:], scale=INV).then_inc(g_read, 1)
                return step

            def exps(u):
                def step(b):
                    act.wait_ge(shifted, b.x + 1)
                    rows = slice(UNITS[u][0] * H, (UNITS[u][-1] + 1) * H)
                    nc.scalar.activation(pe8[:, :, rows, :],
                                         lg[:].rearrange("p (k w) -> p k w", k=TB)[:, :, rows].unsqueeze(3)
                                         .to_broadcast([P, TB, len(UNITS[u]) * H, HD]), ACT.Exp).then_inc(exp_done, 1)
                return step

            def projected(b):
                act.wait_ge(d_full, b.x * DD + 1)
                nc.scalar.activation(yo[:], ps[:, 7, 0:L], ACT.Identity, bias=ga[:, 1:2], scale=ga[:, 0:1]
                                     ).then_inc(d_read, 1)

            run(act, [("V", exps(0)), ("Q", factors(2)), ("V", exps(1)), ("V", exps(2))] +
                [("V", exps(u)) for u in range(3, NU)] +
                [("D", projected), ("A", modulate), ("A", queries_keys), ("A", values_gate),
                 ("N", factors(0)), ("N", factors(1))])

        @block.tensor
        def _(pe):
            pe.wait_ge(setup, 2)

            def turn_tokens(b):
                hold(pe, d_read, DD, b + -2, 0)
                hold(pe, g_read, G, b, 0)
                hold(pe, a_read, A, b, 0)
                pe.wait_ge(y_done, b.x + 1)
                for k in range(TB):
                    mm = nc.tensor.transpose(ps[:, 7, k * P:(k + 1) * P], y[:, k, :], ident[:])
                mm.then_inc(a_full, 1)

            def project(which):
                def step(b):
                    pe.wait_ge(a_read, b.x * A + 1 + which)
                    if which == 0:
                        hold(pe, r_read, 1, b + -1, 0)
                    for k in range(2):
                        mm = nc.tensor.matmul(ps[:, 7, k * L:(k + 1) * L], w[:, 2 * which + k, :], hT[:],
                                              start=True, stop=True)
                    mm.then_inc(a_full, 1)
                return step

            def factors(n):
                def step(b):
                    if n == 0:
                        pe.wait_ge(a_read, b.x * A + 3)
                    else:
                        pe.wait_ge(g_read, b.x * G + n)
                    for k in range(TB):
                        lo, hi = max(512 * n, W * k), min(512 * n + 512, W * (k + 1))
                        if lo < hi:
                            mm = nc.tensor.matmul(ps[:, 7, lo - 512 * n:hi - 512 * n], q[:, b.k % 3, k * P:(k + 1) * P],
                                                  emb[:, lo - W * k:hi - W * k], start=True, stop=True)
                    mm.then_inc(g_full, 1)
                return step

            def head_sums(u):
                def step(b):
                    if u == 0:
                        hold(pe, qk_read, 1, b, 0)
                    if u in VUNITS:
                        pe.wait_ge(prod_v, b.x * NV + VUNITS.index(u) + 1)
                    else:
                        pe.wait_ge(prod_g, b.x * NG + GUNITS.index(u) + 1)
                    n = len(UNITS[u])
                    for k in range(TB):
                        col = k * WK + UNITS[u][0] * H
                        for j, o in enumerate(UNITS[u]):
                            mm = nc.tensor.matmul(ps[:, 4 + col // 512, col % 512:col % 512 + n * H],
                                                  prod[:, o, k * P:(k + 1) * P],
                                                  headsum[:, (3 - j) * H:(3 - j + n) * H], start=(j == 0), stop=(j == n - 1))
                    if u == NU - 1:
                        mm.then_inc(qk_full, 1)
                return step

            def turn_exps(u):
                def step(b):
                    hold(pe, pv_read, NU, b, u - 1)
                    pe.wait_ge(exp_done, b.x * NU + u + 1)
                    for n, o in enumerate(UNITS[u]):
                        for k in range(TB):
                            row = pe8[:, k, o * H:(o + 1) * H, :].rearrange("p h d -> p (h d)")
                            mm = nc.tensor.transpose(
                                ps[:, 2 * (u % 2) + n // 2, (n % 2) * L + k * P:(n % 2) * L + (k + 1) * P], row, ident[:])
                    mm.then_inc(pv_full, 1)
                return step

            def turn_reciprocals(b):
                hold(pe, d_read, DD, b, 0)
                pe.wait_ge(g_read, latest(b, 1).x * G + G)
                pe.wait_ge(a_read, b.x * A + 2 * A + 1 if b.k + 2 < B else B * A)
                pe.wait_ge(den_done, b.x + 1)
                for k in range(TB):
                    mm = nc.tensor.transpose(ps[:, 7, k * P:(k + 1) * P], denw[:, k, :], ident[:])
                mm.then_inc(r_full, 1)

            def project_out(b):
                pe.wait_ge(g_read, latest(b, 2).x * G + G)
                pe.wait_ge(r_read, b.x + 1)
                hold(pe, d_read, DD, b, 0)
                pe.wait_ge(og_done, b.x + 1)
                nc.tensor.matmul(ps[:, 7, 0:L], w[:, 4, :], og[:], start=True, stop=True).then_inc(d_full, 1)

            def turn_back(b):
                pe.wait_ge(d_read, b.x * DD + 1)
                for k in range(TB):
                    mm = nc.tensor.transpose(ps[:, 7, k * P:(k + 1) * P], yo[:, k * P:(k + 1) * P], ident[:])
                mm.then_inc(d_full, 1)

            run(pe, [("V", turn_exps(0)), ("V", turn_exps(1)), ("Q", head_sums(2)), ("V", turn_exps(2)),
                     ("Q", head_sums(7)), ("V", turn_exps(3)), ("Q", head_sums(3)), ("V", turn_exps(4)),
                     ("D", project_out), ("Q", head_sums(4)), ("V", turn_exps(5)), ("D", turn_back),
                     ("Q", head_sums(5)), ("V", turn_exps(6)), ("A", turn_tokens), ("Q", head_sums(6)),
                     ("V", turn_exps(7)), ("R", turn_reciprocals), ("Q", head_sums(8)), ("V", turn_exps(8)),
                     ("Q", head_sums(9)), ("A", project(0)), ("V", turn_exps(9)),
                     ("A", project(1)), ("N", factors(0)), ("N", head_sums(0)), ("N", factors(1)),
                     ("N", head_sums(1)), ("N", factors(2))])

        @block.vector
        def _(v):
            v.wait_ge(loaded, 112)
            v.wait_ge(setup, 1)
            nc.vector.tensor_scalar(hbg[:], bcol[:, 3:4], 0.5, None, ALU.mult)
            nc.vector.tensor_scalar(ifg[:], ifg[:], 0.5, None, ALU.mult)
            nc.vector.tensor_scalar(gabo[:], modT[:, 1, 2, :], bcol[:, 4:5], None, ALU.mult)
            for k in range(TB):
                n = nc.vector.tensor_tensor(pb[:, k].rearrange("p (o h) -> p o h", h=H),
                                            pbr[:].rearrange("p (o h) -> p o h", h=H),
                                            early[:, k].unsqueeze(2).to_broadcast([P, NO, H]), ALU.add)
            n.then_inc(setup, 1)
            v.wait_ge(setup, 2)

            def statistics(b):
                for k in range(TB):
                    nc.vector.bn_stats(stat[:, k, :], x[:, bass.ds(b.x * TB + k, 1), :].rearrange("p a d -> p (a d)")
                                       ).then_inc(dve_a, 1)

            def moments(b):
                v.wait_ge(dve_a, b.x * TB + TB)
                hold(v, a_read, A, b, 0)
                nc.vector.tensor_copy(ca[:], modT[:, 1, 1, bass.ds(b.x, 1)])
                nc.vector.tensor_copy(sa[:], modT[:, 1, 0, bass.ds(b.x, 1)])
                for k in range(TB):
                    n = nc.vector.bn_aggr(mv[:, k, :], stat[:, k, :])
                n.then_inc(stats_done, 1)

            def normalise(b):
                v.wait_ge(rstd_done, b.x * 2 + 2)
                for k in range(TB):
                    n = nc.vector.tensor_scalar(y[:, k, :], x[:, bass.ds(b.x * TB + k, 1), :].rearrange("p a d -> p (a d)"),
                                                mv[:, k, 0:1], rstd[:, k:k + 1], ALU.subtract, ALU.mult)
                n.then_inc(y_done, 1)

            def products(u):
                def step(b):
                    if u == 0:
                        v.wait_ge(a_read, b.x * A + 2)
                        hold(v, qk_full, 1, b, 0)
                    for o0, n in runs(UNITS[u]):
                        m = nc.vector.tensor_tensor(prod[:, o0:o0 + n, :],
                                                    q[:, b.k % 3].unsqueeze(1).to_broadcast([P, n, L]),
                                                    shift(kp, b, o0, n), ALU.mult)
                    m.then_inc(prod_v, 1)
                return step

            def logits(b):
                v.wait_ge(qk_full, b.x + 1)
                v.wait_ge(g_read, b.x * G + G)
                hold(v, exp_done, NU, b, 0)
                nc.vector.tensor_tensor(lg[:].rearrange("p (k w) -> p k w", k=TB),
                                        ps[:, 4:7].rearrange("p b n -> p (b n)")[:, 0:TB * WK]
                                        .rearrange("p (k w) -> p k w", k=TB)[:, :, 0:W],
                                        g[:].rearrange("p (k w) -> p k w", k=TB), ALU.mult
                                        ).then_inc(qk_read, 1)
                v.wait_ge(qk_read, b.x + 1)
                nc.vector.tensor_tensor(lg[:], lg[:], pb[:].rearrange("p k w -> p (k w)"), ALU.add
                                        ).then_inc(biased, 1)

            def softmax_shift(b):
                byoffset = lg[:].rearrange("p (k o h) -> p k o h", h=H, k=TB)
                v.wait_ge(biased, b.x + 1)
                nc.vector.tensor_reduce(mx[:], lg[:].rearrange("p (k o h) -> p k h o", h=H, k=TB), AX_X, ALU.max
                                        ).then_inc(max_done, 1)
                v.wait_ge(max_done, b.x + 1)
                for k in range(TB):
                    n = nc.vector.tensor_tensor(byoffset[:, k], byoffset[:, k],
                                                mx[:, k].unsqueeze(1).to_broadcast([P, NO, H]), ALU.subtract)
                n.then_inc(shifted, 1)

            def weighted(u):
                def step(b):
                    v.wait_ge(pv_full, b.x * NU + u + 1)
                    if u:
                        hold(v, added, NU + 1, b + -1, u)
                    dst = yv[:, (u - 1) % RING] if u else acc[:, b.k % 3]
                    for o0, n in runs(UNITS[u]):
                        a = o0 - UNITS[u][0]
                        pt = ps[:, 2 * (u % 2):2 * (u % 2) + 2, :].rearrange("p b (a n) -> p (b a) n", n=L)
                        m = nc.vector.tensor_tensor(dst[:, a:a + n, :], pt[:, a:a + n, :], shift(vp, b, o0, n), ALU.mult)
                    m.then_inc(pv_read, 1)
                return step

            def sums(b):
                v.wait_ge(exp_done, b.x * NU + NU)
                nc.vector.tensor_reduce(den[:], pe8[:, :, :, 0].rearrange("p k (o h) -> p k h o", h=H), AX_X, ALU.add
                                        ).then_inc(summed, 1)

            def reciprocals(b):
                v.wait_ge(summed, b.x * 2 + 1)
                nc.vector.reciprocal(den[:], den[:]).then_inc(summed, 1)
                v.wait_ge(summed, b.x * 2 + 2)
                nc.vector.tensor_copy(denw[:].rearrange("p k (h d) -> p k h d", d=HD),
                                      den[:].unsqueeze(3).to_broadcast([P, TB, H, HD])).then_inc(den_done, 1)

            def gate_over_sums(b):
                v.wait_ge(r_full, b.x + 1)
                v.wait_ge(gs_done, b.x + 1)
                nc.vector.tensor_tensor(gs[:, b.k % 3], gs[:, b.k % 3], ps[:, 7, 0:L], ALU.mult).then_inc(r_read, 1)

            def gated(b):
                v.wait_ge(added, b.x * (NU + 1) + NU + 1)
                nc.vector.tensor_copy(ga[:, 0:1], modT[:, 1, 2, bass.ds(b.x, 1)])
                nc.vector.tensor_copy(ga[:, 1:2], gabo[:, bass.ds(b.x, 1)])
                v.wait_ge(r_read, b.x + 1)
                nc.vector.tensor_tensor(og[:], acc[:, b.k % 3, 0], gs[:, b.k % 3], ALU.mult).then_inc(og_done, 1)

            def residual(b):
                v.wait_ge(d_full, b.x * DD + 2)
                xs = x[:, bass.ds(b.x * TB, TB), :]
                nc.vector.tensor_tensor(xs, xs, ps[:, 7, 0:L].rearrange("p (k d) -> p k d", d=D), ALU.add
                                        ).then_inc(d_read, 1)

            run(v, [("Q", products(2)), ("Q", products(3)), ("V", weighted(0)), ("Q", products(4)),
                    ("V", weighted(1)), ("A", statistics), ("D", gated), ("A", moments), ("V", weighted(2)),
                    ("Q", products(5)), ("V", weighted(3)), ("A", normalise), ("V", weighted(4)),
                    ("R", sums), ("D", residual), ("Q", products(6)), ("V", weighted(5)), ("R", reciprocals),
                    ("Q", products(9)), ("V", weighted(6)), ("R", gate_over_sums), ("V", weighted(7)),
                    ("V", weighted(8)), ("Q", logits),
                    ("N", products(0)), ("V", weighted(9)), ("N", products(1)), ("Q", softmax_shift)])


def store_stream(nc, s, out):
    with nc.semaphore("st_stored") as stored, nc.Block() as block:
        @block.sync
        def _(sp):
            sp.dma_start(out.rearrange("b (k p) d -> p (b k) d", p=P), s["x"][:]).then_inc(stored, 16)
            sp.wait_ge(stored, 16)


def layout(inputs):
    a = {k: np.ascontiguousarray(v) for k, v in inputs.items()}
    swap = np.arange(D).reshape(-1, 2)[:, ::-1].reshape(-1)
    t = {
        "L0_attn_x": a["L0_attn_x"],
        "L0_attn_bv": a["L0_attn_bv"],
        "L0_attn_scale": a["L0_attn_scale"],
        "cT": np.stack([a["L0_c"].T, a["L1_c"].T], 1),
        "wmod": np.stack([a["L0_wmod"], a["L1_wmod"]], 1),
        "a0_w": np.stack([a["L0_attn_Wq"].T, a["L0_attn_Wq"][swap].T, a["L0_attn_Wk"].T, a["L0_attn_Wk"][swap].T,
                          a["L0_attn_Wv"].T, a["L0_attn_Wo"].T], 1),
        "a0_b": np.stack([a["L0_attn_bq"], a["L0_attn_bq"][swap], a["L0_attn_bk"], a["L0_attn_bk"][swap],
                          a["L0_attn_bo"]], 1),
    }
    gu = a["L0_ffn_gate_up_proj"].reshape(PAIRS, 2, 2, I0, D)
    pack = lambda w, first: np.concatenate([first.T[None], w.transpose(0, 3, 1, 2).reshape(PAIRS, D, P)]).transpose(1, 0, 2)
    t["e0_wg"] = pack(gu[:, :, 0], a["L0_ffn_shared_gate_w"])
    t["e0_wu"] = pack(gu[:, :, 1], a["L0_ffn_shared_up_w"])
    down = a["L0_ffn_down_proj"].reshape(PAIRS, 2, D, I0).transpose(0, 1, 3, 2).reshape(PAIRS, P, D)
    t["e0_wd"] = np.concatenate([a["L0_ffn_shared_down_w"].T[None], down]).transpose(1, 0, 2)
    t["e0_wr"] = a["L0_ffn_router_weight"].T
    t["L0_ffn_e_score_bias"] = a["L0_ffn_e_score_bias"]
    qkv, qb = a["L1_attn_qkv_w"].reshape(3, D, D), a["L1_attn_qkv_b"].reshape(3, D)
    t["a1_w"] = np.stack([*qkv, a["L1_attn_gate_w"], a["L1_attn_out_w"]]).transpose(2, 0, 1)
    t["a1_b"] = np.stack([*qb, a["L1_attn_gate_b"], a["L1_attn_out_b"]], 1)
    t["a1_ifg"] = np.repeat(a["L1_attn_if_gain"], HD)[:, None]
    emb = np.zeros((H, HD, NO, H), np.float32)
    for h in range(H):
        emb[h, :, :, h] = a["L1_attn_scale_embed"][::-1].T
    t["a1_emb"] = emb.reshape(D, NO * H)
    t["a1_pb"] = a["L1_attn_pos_bias"][::-1].reshape(-1)
    t["e1_w1"] = a["L1_ffn_W1"].transpose(1, 0, 2)
    t["e1_w2"] = a["L1_ffn_W2"].transpose(1, 0, 2)
    t["e1_b1"] = a["L1_ffn_b1"].T
    for name in ("L1_ffn_b2", "L1_ffn_Wr", "L1_ffn_br"):
        t[name] = a[name]
    t.update(shape_constants())
    return {k: np.ascontiguousarray(v) for k, v in t.items()}


def kernel(**inputs):
    import concourse.bacc as bacc
    from concourse.bass_utils import run_bass_kernel_spmd

    nc = bacc.Bacc("TRN2", target_bir_lowering=False, num_devices=1)
    arrays = layout(inputs)
    t = {name: nc.dram_tensor(name + "_dram", a.shape, mybir.dt.from_np(a.dtype), kind="ExternalInput").ap()
         for name, a in arrays.items()}
    out = nc.dram_tensor("out_dram", (B, L, D), F32, kind="ExternalOutput").ap()
    build(nc, t, out)
    r = run_bass_kernel_spmd(nc, [{name + "_dram": a for name, a in arrays.items()}], core_ids=[0])
    return r.results[0]["out_dram"]
```

```python
from contextlib import ExitStack

import numpy as np

import concourse.bass as bass
from concourse import mybir

ALU = mybir.AluOpType
ACT = mybir.ActivationFunctionType
AX_X = mybir.AxisListType.X
F32 = mybir.dt.float32
BF16 = mybir.dt.bfloat16

P = 128
B, L, D = 16, 256, 128
T = B * L
NT = T // P
TB = L // P
H, HD = 16, 8
HJ, HG = 4, 4
E0, I0, TOP_K = 32, 64, 6
PAIRS = E0 // 2
E1 = 8
CAP = T // E1
MT = 512
OFFSETS = sorted(set(range(33)) | {48, 64, 96, 128, 192})
NO = len(OFFSETS)
ORDER = OFFSETS[::-1]
PAD = max(OFFSETS)
EPS = 1e-5
NEG = -1e30
THETA = 10000.0
NORM_MIN = 1e-12


class Count:

    def __init__(self, base=0):
        self.base, self.n = base, 0

    def up(self, k=1):
        self.n += k
        return k

    def now(self):
        return self.base + self.n


def shape_constants():
    freqs = (THETA ** (-np.arange(0, HD, 2, dtype=np.float32) / HD)).astype(np.float32)
    ang = np.arange(L, dtype=np.float32)[:, None] * freqs
    cos = np.repeat(np.cos(ang), 2, axis=1)
    sin = np.repeat(np.sin(ang), 2, axis=1)
    sin[:, 0::2] *= -1
    q, k = np.arange(P)[:, None], np.arange(P)[None, :]
    later = np.where(k > q, NEG, 0.0).astype(np.float32)
    masks = np.stack([np.tile(later[:, None], (1, 4, 1)), np.tile(later.T[:, None], (1, 4, 1))], 1)
    n = np.arange(L).reshape(TB, P).T[:, :, None]
    early = np.where(n < np.array(ORDER)[None, None, :], NEG, 0.0).astype(np.float32)
    pair = np.zeros((96, PAIRS, P), np.float32)
    one = np.zeros((96, E1 + 1, P), np.float32)
    for part in range(3):
        for e in range(E0):
            pair[32 * part + e, e // 2, 64 * (e % 2):64 * (e % 2) + 64] = 1
        for e in range(E1):
            one[32 * part + e, e] = 1
            one[32 * part + e, E1] = 1
    return {
        "c_ident": np.eye(P, dtype=np.float32),
        "c_cos": np.repeat(cos.T, H, axis=0).astype(np.float32),
        "c_sin": np.repeat(sin.T, H, axis=0).astype(np.float32),
        "c_masks": masks,
        "c_early": early,
        "c_pair": pair,
        "c_one": one,
        "c_upto": np.triu(np.ones((P, P), np.float32)),
        "c_headsum": np.pad(np.kron(np.eye(H, dtype=np.float32), np.ones((HD, 1), np.float32)),
                            ((0, 0), (3 * H, 3 * H))),
    }


def build(nc, t, out):
    ctx = ExitStack()
    with ctx:
        def sb(name, shape, dt=F32):
            return ctx.enter_context(nc.sbuf_tensor(name, shape, dt))

        def sem(name):
            return ctx.enter_context(nc.semaphore(name))

        ps = ctx.enter_context(nc.psum_tensor("ps", [P, 8, 512], F32))

        s = {}
        s["ident"] = sb("ident", [P, P])
        s["identb"] = sb("identb", [P, P], BF16)
        s["x"] = sb("x", [P, NT, D])
        s["modT"] = sb("modT", [P, 2, 6, B])
        s["pm5"] = sb("pm5", [P, TB * 2])
        s["eps"] = sb("eps", [P, TB * 2])

        load_stream(nc, s, t, ps, sb, sem)
        attention0(nc, s, t, ps)
        experts0(nc, s, t, ps)
        attention1(nc, s, t, ps)
        experts1(nc, s, t, ps)
        store_stream(nc, s, out)


def load_stream(nc, s, t, ps, sb, sem):
    x, modT = s["x"], s["modT"]
    with ExitStack() as ctx:
        cT = ctx.enter_context(nc.sbuf_tensor("ls_cT", [P, 2, B], F32))
        sT = ctx.enter_context(nc.sbuf_tensor("ls_sT", [P, 2, B], F32))
        wm = ctx.enter_context(nc.sbuf_tensor("ls_wm", [P, 2, 6 * D], F32))
        g1 = ctx.enter_context(nc.sbuf_tensor("ls_g1", [P, 2, 2, B], F32))
        g2 = ctx.enter_context(nc.sbuf_tensor("ls_g2", [P, 2, 2, B], F32))
        loaded = ctx.enter_context(nc.semaphore("ls_loaded"))
        silu_done = ctx.enter_context(nc.semaphore("ls_silu"))
        mod_done = ctx.enter_context(nc.semaphore("ls_mod"))
        dve = ctx.enter_context(nc.semaphore("ls_dve"))
        block = ctx.enter_context(nc.Block())

        @block.sync
        def _(sp):
            sp.dma_start(cT[:], t["cT"]).then_inc(loaded, 16)
            sp.dma_start(wm[:], t["wmod"]).then_inc(loaded, 16)
            sp.dma_start(s["ident"][:], t["c_ident"]).then_inc(loaded, 16)
            sp.dma_start(x[:], t["L0_attn_x"].rearrange("b (k p) d -> p (b k) d", p=P)).then_inc(loaded, 16)

        @block.scalar
        def _(act):
            act.wait_ge(loaded, 64)
            nc.scalar.activation(sT[:], cT[:], ACT.Silu).then_inc(silu_done, 1)

        @block.tensor
        def _(pe):
            pe.wait_ge(silu_done, 1)
            for layer in range(2):
                for j in range(6):
                    mm = nc.tensor.matmul(ps[:, layer, j * B:(j + 1) * B], wm[:, layer, j * D:(j + 1) * D],
                                          sT[:, layer, :], start=True, stop=True)
            mm.then_inc(mod_done, 1)

        @block.vector
        def _(v):
            c = Count()
            v.wait_ge(loaded, 64)
            nc.vector.tensor_copy(s["identb"][:], s["ident"][:]).then_inc(dve, c.up())
            nc.vector.memset(s["pm5"][:], -0.5).then_inc(dve, c.up())
            nc.vector.memset(s["eps"][:], EPS).then_inc(dve, c.up())
            v.wait_ge(mod_done, 1)
            for layer in range(2):
                nc.vector.tensor_copy(modT[:, layer], ps[:, layer, 0:6 * B].rearrange("p (j b) -> p j b", b=B)
                                      ).then_inc(dve, c.up())
            v.wait_ge(dve, c.now())
            for layer in range(2):
                scales, gates = modT[:, layer, 1:6:3, :], modT[:, layer, 2:6:3, :]
                nc.vector.tensor_scalar(scales, scales, 1.0, None, ALU.add).then_inc(dve, c.up())
                nc.vector.tensor_scalar(g1[:, layer], gates, 0.0, 2.0, ALU.is_ge, ALU.mult).then_inc(dve, c.up())
                nc.vector.tensor_scalar(g2[:, layer], gates, -1.0, None, ALU.mult).then_inc(dve, c.up())
                v.wait_ge(dve, c.now())
                nc.vector.tensor_tensor(g2[:, layer], g2[:, layer], gates, ALU.max).then_inc(dve, c.up())
                v.wait_ge(dve, c.now())
                nc.vector.tensor_scalar(g2[:, layer], g2[:, layer], 0.25, None, ALU.max).then_inc(dve, c.up())
                v.wait_ge(dve, c.now())
                nc.vector.scalar_tensor_tensor(gates, g1[:, layer], -1.0, g2[:, layer], ALU.add, ALU.mult
                                               ).then_inc(dve, c.up())
                v.wait_ge(dve, c.now())


class Batch:

    def __init__(self, x, k):
        self.x, self.k = x, k

    def __add__(self, n):
        return Batch(self.x + n, self.k + n)


def hold(eng, sem, per, b, n):
    if per * b.k + n > 0:
        eng.wait_ge(sem, b.x * per + n)


def pipeline(eng, first, last, start, end, body, turns=3):
    passes = (end - start) // turns
    for k in range(first, start):
        body(Batch(k, k))
    with eng.Fori(0, passes) as i:
        for r in range(turns):
            body(Batch(i * turns + (start + r), start + r))
    for k in range(start + passes * turns, last):
        body(Batch(k, k))


def attention0(nc, s, t, ps):
    x, modT, ident, identb = s["x"], s["modT"], s["ident"], s["identb"]
    TERMS = [(0, 0), (0, 1), (0, 2), (1, 0), (1, 1), (2, 0)]
    ROWS = HD * len(TERMS)
    TOP = ROWS
    UN = 12
    with ExitStack() as ctx:
        def sb(name, shape, dt=F32):
            return ctx.enter_context(nc.sbuf_tensor("a0_" + name, shape, dt))

        def sem(name):
            return ctx.enter_context(nc.semaphore("a0_" + name))

        w = sb("w", [P, 6, D])
        bcol = sb("bcol", [P, 5])
        bvrow = sb("bvrow", [P, D])
        scale = sb("scale", [P, 1])
        cosq, sinq = sb("cosq", [P, L]), sb("sinq", [P, L])
        cosk, sink = sb("cosk", [P, L]), sb("sink", [P, L])
        maskf = sb("maskf", [P, 2, 4, P])
        mask = sb("mask", [P, 2, 4, P], BF16)
        gabo = sb("gabo", [P, B])
        ga, ca, sa = sb("ga", [P, 2]), sb("ca", [P, 1]), sb("sa", [P, 1])
        stat, mv, rstd = sb("stat", [P, TB, 6]), sb("mv", [P, TB, 2]), sb("rstd", [P, TB])
        y = sb("y", [P, TB, D])
        hT = sb("hT", [P, L])
        ra, rb = sb("ra", [P, 2, L]), sb("rb", [P, 2, L])
        parts = sb("parts", [P, 2, 3, L], BF16)
        vv = sb("vv", [P, 3, TB, H, 32])
        qs = sb("qs", [TOP + 3, 3, H, L], BF16)
        ks = sb("ks", [TOP + 3, 3, H, L], BF16)
        nmax = sb("nmax", [P, 3, TB, HJ, HG])
        nT, nparts = sb("nT", [H, 2, L]), sb("nparts", [H, 3, L], BF16)
        pr = sb("pr", [P, 2, HJ, L + P])
        o = sb("o", [P, HG, L])
        rden = sb("rden", [P, TB, HG, HJ])
        on = sb("on", [P, TB, HJ, HG, HD])
        onT = sb("onT", [P, L])
        yo = sb("yo", [P, L])
        unit = sb("unit", [P, 1])
        parts_d = nc.dram_tensor("a0_parts_d", [2 * 3, P, L], BF16).ap()
        nparts_d = nc.dram_tensor("a0_nparts_d", [H, 3, L], BF16).ap()

        loaded, cleared, masks_done = sem("loaded"), sem("cleared"), sem("masks_done")
        stats_done, rstd_done, y_done = sem("stats_done"), sem("rstd_done"), sem("y_done")
        a_full, a_read = sem("a_full"), sem("a_read")
        rotated, summed, split = sem("rotated"), sem("summed"), sem("split")
        stored, spread = sem("stored"), sem("spread")
        m_full, m_read = sem("m_full"), sem("m_read")
        nT_full, nT_read = sem("nT_full"), sem("nT_read")
        nsplit, nstored, nspread = sem("nsplit"), sem("nstored"), sem("nspread")
        c_full, exp_done = sem("c_full"), sem("exp_done")
        pv_done, o_read = sem("pv_done"), sem("o_read")
        d_full, d_read = sem("d_full"), sem("d_read")
        dve_a, dve_d = sem("dve_a"), sem("dve_d")
        block = ctx.enter_context(nc.Block())
        A_STEPS, D_STEPS = 4, 5
        RUNS = [(0, 3), (3, 2), (5, 1)]
        STORE, SPREAD = 16, 16 * 2 * len(RUNS)
        for n, m in RUNS:
            assert TERMS[n:n + m] == [(TERMS[n][0], i) for i in range(m)]

        def run(eng, order):
            ahead = {"D": -1, "C": 0, "M": 1, "N": 2, "S": 2, "A": 3, "L": 4}

            def body(b):
                for stage, step in order:
                    c = b + ahead[stage]
                    if 0 <= c.k < B:
                        step(c)
            pipeline(eng, -4, B + 1, 2, B - 4, body)

        @block.sync
        def _(sp):
            sp.dma_start(w[:], t["a0_w"]).then_inc(loaded, 16)
            sp.dma_start(bcol[:], t["a0_b"]).then_inc(loaded, 16)
            sp.dma_start(bvrow[:], t["L0_attn_bv"].partition_broadcast(P)).then_inc(loaded, 16)
            sp.dma_start(scale[:], t["L0_attn_scale"].partition_broadcast(P)).then_inc(loaded, 16)
            sp.dma_start(cosk[:], t["c_cos"]).then_inc(loaded, 16)
            sp.dma_start(sink[:], t["c_sin"]).then_inc(loaded, 16)
            sp.dma_start(maskf[:], t["c_masks"]).then_inc(loaded, 16)
            sp.wait_ge(cleared, 2)

            def spread_parts(b):
                sp.wait_ge(split, b.x + 1)
                sp.dma_start(parts_d.rearrange("a p n -> p a n"), parts[:].rearrange("p w t n -> p (w t) n")
                             ).then_inc(stored, 16)
                sp.wait_ge(stored, b.x * STORE + STORE)
                for n, m in RUNS:
                    rows = slice(HD * n, HD * (n + m))
                    one = parts_d[TERMS[n][0]].rearrange("(d h) n -> d (h n)", h=H)
                    sp.dma_start(qs[rows, b.k % 3].rearrange("p h n -> p (h n)"),
                                 one.unsqueeze(0).to_broadcast([m, HD, H * L])).then_inc(spread, 16)
                    sp.dma_start(ks[rows, b.k % 3].rearrange("p h n -> p (h n)"),
                                 parts_d[3:3 + m].rearrange("t (d h) n -> (t d) (h n)", h=H)).then_inc(spread, 16)

            def spread_max(b):
                sp.wait_ge(nsplit, b.x * 4 + 4)
                sp.dma_start(nparts_d, nparts[:]).then_inc(nstored, 16)
                sp.wait_ge(nstored, b.x * 16 + 16)
                sp.dma_start(qs[TOP:TOP + 3, b.k % 3], nparts_d.rearrange("h t n -> t h n")).then_inc(nspread, 16)

            run(sp, [("S", spread_parts), ("M", spread_max)])

        @block.gpsimd
        def _(pool):
            nc.gpsimd.memset(unit[:], 1.0).then_inc(cleared, 1)
            pool.wait_ge(cleared, 2)

            def rstd_of(b):
                pool.wait_ge(stats_done, b.x + 1)
                nc.gpsimd.tensor_tensor(rstd[:], mv[:, :, 1], s["eps"][:, 0:TB], ALU.add).then_inc(rstd_done, 1)
                pool.wait_ge(rstd_done, b.x * 2 + 1)
                nc.gpsimd.tensor_tensor(rstd[:], rstd[:], s["pm5"][:, 0:TB], ALU.pow).then_inc(rstd_done, 1)

            def split_parts(b):
                pool.wait_ge(rotated, b.x * 2 + 2)
                pool.wait_ge(a_read, b.x * A_STEPS + 3)
                nc.gpsimd.tensor_tensor(ra[:], ra[:], rb[:], ALU.add).then_inc(summed, 1)
                pool.wait_ge(summed, b.x * 4 + 1)
                hold(pool, stored, STORE, b, 0)
                nc.gpsimd.tensor_tensor(parts[:, :, 0, :], ra[:], unit[:].unsqueeze(2).to_broadcast([P, 2, L]), ALU.mult).then_inc(summed, 1)
                pool.wait_ge(summed, b.x * 4 + 2)
                nc.gpsimd.tensor_tensor(ra[:], ra[:], parts[:, :, 0, :], ALU.subtract).then_inc(summed, 1)
                pool.wait_ge(summed, b.x * 4 + 3)
                nc.gpsimd.tensor_tensor(parts[:, :, 1, :], ra[:], unit[:].unsqueeze(2).to_broadcast([P, 2, L]), ALU.mult).then_inc(summed, 1)

            def last_part(b):
                pool.wait_ge(summed, b.x * 4 + 4)
                hold(pool, spread, SPREAD, b, 0)
                hold(pool, c_full, UN, b + -2, 0)
                nc.gpsimd.tensor_tensor(parts[:, :, 2, :], ra[:], parts[:, :, 1, :], ALU.subtract).then_inc(split, 1)

            run(pool, [("S", last_part), ("A", split_parts), ("L", rstd_of)])

        @block.scalar
        def _(act):
            def modulate(b):
                hold(act, a_full, A_STEPS, b, 1)
                nc.scalar.activation(hT[:], ps[:, 6, 0:L], ACT.Identity, bias=sa[:], scale=ca[:]).then_inc(a_read, 1)

            def exps(g, n):
                def step(b):
                    if n == 0:
                        hold(act, pv_done, HG, b, g - 1)
                    act.wait_ge(c_full, b.x * UN + 3 * g + n + 1)
                    bank = 2 + (3 * g + n) % 2
                    if n < 2:
                        dst, src = pr[:, g % 2, 2 * n:2 * n + 2, 0:L], ps[:, bank].rearrange("p (j n) -> p j n", j=2)
                    else:
                        dst, src = pr[:, g % 2, :, L:L + P], ps[:, bank].rearrange("p (j n) -> p j n", j=HJ)
                    nc.scalar.activation(dst, src, ACT.Exp).then_inc(exp_done, 1)
                return step

            def outputs(a):
                def step(b):
                    act.wait_ge(pv_done, b.x * HG + 2 * a + 2)
                    hold(act, d_full, D_STEPS, b, -3)
                    nc.scalar.activation(o[:, 2 * a:2 * a + 2], ps[:, 4 + a].rearrange("p (g n) -> p g n", n=L),
                                         ACT.Copy).then_inc(o_read, 1)
                return step

            def turned(b):
                act.wait_ge(d_full, b.x * D_STEPS + 3)
                nc.scalar.activation(onT[:], ps[:, 7, 0:L], ACT.Copy).then_inc(d_read, 1)

            def projected(b):
                act.wait_ge(d_full, b.x * D_STEPS + 4)
                nc.scalar.activation(yo[:], ps[:, 7, 0:L], ACT.Identity, bias=ga[:, 1:2], scale=ga[:, 0:1]
                                     ).then_inc(d_read, 1)

            run(act, [("C", exps(0, 0)), ("C", exps(0, 1)), ("C", exps(0, 2)), ("D", outputs(1)),
                      ("C", exps(1, 0)), ("C", exps(1, 1)), ("C", exps(1, 2)), ("A", modulate),
                      ("C", exps(2, 0)), ("D", turned), ("C", exps(2, 1)), ("C", exps(2, 2)),
                      ("C", outputs(0)), ("D", projected), ("C", exps(3, 0)), ("C", exps(3, 1)),
                      ("C", exps(3, 2))])

        @block.tensor
        def _(pe):
            pe.wait_ge(cleared, 2)
            pe.wait_ge(masks_done, 1)

            def causal(out, form, n):
                nc.tensor.matmul(out, identb[:], mask[:, form, 0:n], start=True, stop=False, skip_group_check=True)

            def scores_c(g, n):
                def step(b):
                    p = b.k % 3
                    if g == 0 and n == 0:
                        pe.wait_ge(spread, b.x * SPREAD + SPREAD)
                        pe.wait_ge(nspread, b.x * 16 + 16)
                    hold(pe, exp_done, UN, b, 3 * g + n - 1)
                    bank = ps[:, 2 + (3 * g + n) % 2]
                    if n < 2:
                        blocks = bank.rearrange("p (j n) -> p j n", j=2)
                        causal(blocks[:, :, 0:P], 1, 2)
                        for a in range(2):
                            h = HG * (2 * n + a) + g
                            mm = nc.tensor.matmul(blocks[:, a], ks[:, p, h, 0:P], qs[:, p, h, :],
                                                  start=False, stop=(a == 1), skip_group_check=True)
                    else:
                        blocks = bank.rearrange("p (j n) -> p j n", j=HJ)
                        causal(blocks, 1, HJ)
                        for j in range(HJ):
                            h = HG * j + g
                            mm = nc.tensor.matmul(blocks[:, j], ks[:, p, h, P:L], qs[:, p, h, P:L],
                                                  start=False, stop=(j == HJ - 1), skip_group_check=True)
                    mm.then_inc(c_full, 1)
                return step

            def scores_m(g, n):
                def step(b):
                    p = b.k % 3
                    if g == 0 and n == 0:
                        pe.wait_ge(spread, b.x * SPREAD + SPREAD)
                    hold(pe, m_read, UN, b, 3 * g + n - 1)
                    bank = ps[:, (3 * g + n) % 2]
                    if n < 2:
                        blocks = bank.rearrange("p (j n) -> p j n", j=2)
                        causal(blocks[:, :, P:L], 0, 2)
                        for a in range(2):
                            h = HG * (2 * n + a) + g
                            mm = nc.tensor.matmul(blocks[:, a], qs[0:ROWS, p, h, P:L], ks[0:ROWS, p, h, :],
                                                  start=False, stop=(a == 1), skip_group_check=True)
                    else:
                        blocks = bank.rearrange("p (j n) -> p j n", j=HJ)
                        causal(blocks, 0, HJ)
                        for j in range(HJ):
                            h = HG * j + g
                            mm = nc.tensor.matmul(blocks[:, j], qs[0:ROWS, p, h, 0:P], ks[0:ROWS, p, h, 0:P],
                                                  start=False, stop=(j == HJ - 1), skip_group_check=True)
                    mm.then_inc(m_full, 1)
                return step

            def turn_max(b):
                pe.wait_ge(m_read, b.x * UN + UN)
                pe.wait_ge(a_read, b.x * A_STEPS + 2 * A_STEPS + 3 if b.k + 2 < B else B * A_STEPS)
                hold(pe, nT_read, 1, b, 0)
                for k in range(TB):
                    mm = nc.tensor.transpose(ps[0:H, 6, k * P:(k + 1) * P],
                                             nmax[:, b.k % 3, k].rearrange("p j g -> p (j g)"), ident[:])
                mm.then_inc(nT_full, 1)

            def outputs(g):
                def step(b):
                    pe.wait_ge(exp_done, b.x * UN + 3 * g + 3)
                    if g == 0:
                        pe.wait_ge(a_read, b.x * A_STEPS + A_STEPS)
                    if g % 2 == 0:
                        hold(pe, o_read, 2, b, g // 2 - 1)
                    for j in range(HJ):
                        h = HG * j + g
                        oo = ps[32 * j:32 * j + 32, 4 + g // 2, (g % 2) * L:(g % 2 + 1) * L]
                        nc.tensor.matmul(oo, vv[:, b.k % 3, 0, h, :], pr[:, g % 2, j, 0:L], start=True, stop=False,
                                         skip_group_check=True, tile_position=(0, 32 * j))
                        mm = nc.tensor.matmul(oo[:, P:L], vv[:, b.k % 3, 1, h, :], pr[:, g % 2, j, L:L + P],
                                              start=False, stop=True, skip_group_check=True,
                                              tile_position=(0, 32 * j))
                    mm.then_inc(pv_done, 1)
                return step

            def turn_tokens(b):
                hold(pe, a_read, A_STEPS, b, 0)
                pe.wait_ge(y_done, b.x + 1)
                for k in range(TB):
                    mm = nc.tensor.transpose(ps[:, 6, k * P:(k + 1) * P], y[:, k, :], ident[:])
                mm.then_inc(a_full, 1)

            def project(which):
                def step(b):
                    pe.wait_ge(a_read, b.x * A_STEPS + which + 1)
                    if which == 2:
                        hold(pe, nT_read, 1, b, -1)
                    if which < 2:
                        for k in range(2):
                            mm = nc.tensor.matmul(ps[:, 6, k * L:(k + 1) * L], w[:, 2 * which + k, :], hT[:],
                                                  start=True, stop=True)
                    else:
                        for k in range(TB):
                            mm = nc.tensor.matmul(ps[:, 6, k * P:(k + 1) * P], hT[:, k * P:(k + 1) * P], w[:, 4, :],
                                                  start=True, stop=True)
                    mm.then_inc(a_full, 1)
                return step

            def turn_outputs(k):
                def step(b):
                    if k == 0:
                        pe.wait_ge(o_read, b.x * 2 + 2)
                        hold(pe, d_read, D_STEPS, b, 0)
                    else:
                        pe.wait_ge(d_read, b.x * D_STEPS + 1)
                    for g in range(HG):
                        mm = nc.tensor.transpose(ps[:, 7, g * P:(g + 1) * P], o[:, g, k * P:(k + 1) * P], ident[:])
                    mm.then_inc(d_full, 1)
                return step

            def turn_normal(b):
                pe.wait_ge(d_read, b.x * D_STEPS + 2)
                for k in range(TB):
                    mm = nc.tensor.transpose(ps[:, 7, k * P:(k + 1) * P], on[:, k].rearrange("p j g d -> p (j g d)"),
                                             ident[:])
                mm.then_inc(d_full, 1)

            def project_out(b):
                pe.wait_ge(d_read, b.x * D_STEPS + 3)
                nc.tensor.matmul(ps[:, 7, 0:L], w[:, 5, :], onT[:], start=True, stop=True).then_inc(d_full, 1)

            def turn_back(b):
                pe.wait_ge(d_read, b.x * D_STEPS + 4)
                for k in range(TB):
                    mm = nc.tensor.transpose(ps[:, 7, k * P:(k + 1) * P], yo[:, k * P:(k + 1) * P], ident[:])
                mm.then_inc(d_full, 1)

            run(pe, [("C", scores_c(0, 0)), ("M", scores_m(2, 0)), ("C", scores_c(0, 1)), ("M", scores_m(2, 1)),
                     ("C", scores_c(0, 2)), ("M", scores_m(2, 2)), ("D", outputs(3)), ("S", project(2)),
                     ("C", scores_c(1, 0)), ("M", scores_m(3, 0)), ("D", turn_outputs(0)), ("C", scores_c(1, 1)),
                     ("M", scores_m(3, 1)), ("A", turn_tokens), ("C", scores_c(1, 2)), ("M", scores_m(3, 2)),
                     ("C", outputs(0)), ("D", turn_outputs(1)), ("A", project(0)), ("C", scores_c(2, 0)),
                     ("D", turn_normal), ("N", scores_m(0, 0)), ("A", project(1)), ("C", scores_c(2, 1)),
                     ("M", turn_max), ("N", scores_m(0, 1)), ("C", scores_c(2, 2)), ("N", scores_m(0, 2)),
                     ("C", outputs(1)), ("D", project_out), ("C", scores_c(3, 0)), ("N", scores_m(1, 0)),
                     ("C", scores_c(3, 1)), ("N", scores_m(1, 1)), ("D", turn_back), ("C", scores_c(3, 2)),
                     ("N", scores_m(1, 2)), ("C", outputs(2))])

        @block.vector
        def _(v):
            nc.vector.memset(ks[32:TOP + 3], 1.0).then_inc(cleared, 1)
            v.wait_ge(loaded, 112)
            nc.vector.tensor_scalar(cosq[:], cosk[:], scale[:], None, ALU.mult)
            nc.vector.tensor_scalar(sinq[:], sink[:], scale[:], None, ALU.mult)
            nc.vector.tensor_scalar(gabo[:], modT[:, 0, 2, :], bcol[:, 4:5], None, ALU.mult)
            nc.vector.tensor_copy(mask[:], maskf[:]).then_inc(masks_done, 1)
            v.wait_ge(masks_done, 1)
            nc.vector.memset(vv[:], 0.0).then_inc(masks_done, 1)
            v.wait_ge(masks_done, 2)
            nc.vector.memset(vv[:, :, :, :, HD], 1.0)

            def statistics(b):
                for k in range(TB):
                    nc.vector.bn_stats(stat[:, k, :], x[:, bass.ds(b.x * TB + k, 1), :].rearrange("p a d -> p (a d)")
                                       ).then_inc(dve_a, 1)
                v.wait_ge(dve_a, b.x * TB + TB)
                hold(v, a_read, A_STEPS, b + -1, 1)
                nc.vector.tensor_copy(ca[:], modT[:, 0, 1, bass.ds(b.x, 1)])
                nc.vector.tensor_copy(sa[:], modT[:, 0, 0, bass.ds(b.x, 1)])
                for k in range(TB):
                    n = nc.vector.bn_aggr(mv[:, k, :], stat[:, k, :])
                n.then_inc(stats_done, 1)

            def normalise(b):
                v.wait_ge(rstd_done, b.x * 2 + 2)
                for k in range(TB):
                    n = nc.vector.tensor_scalar(y[:, k, :], x[:, bass.ds(b.x * TB + k, 1), :].rearrange("p a d -> p (a d)"),
                                                mv[:, k, 0:1], rstd[:, k:k + 1], ALU.subtract, ALU.mult)
                n.then_inc(y_done, 1)

            def rotate(which):
                def step(b):
                    cs, sn = ((cosq, sinq), (cosk, sink))[which]
                    if which == 0:
                        hold(v, split, 1, b, 0)
                    v.wait_ge(a_full, b.x * A_STEPS + 2 + which)
                    nc.vector.scalar_tensor_tensor(ra[:, which, :], ps[:, 6, 0:L], bcol[:, 2 * which:2 * which + 1],
                                                   cs[:], ALU.add, ALU.mult).then_inc(rotated, 1)
                    nc.vector.scalar_tensor_tensor(rb[:, which, :], ps[:, 6, L:2 * L],
                                                   bcol[:, 2 * which + 1:2 * which + 2], sn[:],
                                                   ALU.add, ALU.mult).then_inc(a_read, 1)
                return step

            def values(b):
                v.wait_ge(a_full, b.x * A_STEPS + 4)
                for k in range(TB):
                    n = nc.vector.tensor_tensor(vv[:, b.k % 3, k, :, 0:HD],
                                                ps[:, 6, k * P:(k + 1) * P].rearrange("p (h d) -> p h d", d=HD),
                                                bvrow[:].rearrange("p (h d) -> p h d", d=HD), ALU.add)
                n.then_inc(a_read, 1)

            def maxima(g, n):
                def step(b):
                    v.wait_ge(m_full, b.x * UN + 3 * g + n + 1)
                    bank = ps[:, (3 * g + n) % 2]
                    if n < 2:
                        dst, src = nmax[:, b.k % 3, 1, 2 * n:2 * n + 2, g], bank.rearrange("p (j n) -> p j n", j=2)
                    else:
                        dst, src = nmax[:, b.k % 3, 0, :, g], bank.rearrange("p (j n) -> p j n", j=HJ)
                    nc.vector.tensor_reduce(dst, src, AX_X, ALU.max, negate=True).then_inc(m_read, 1)
                return step

            def take_max(b):
                v.wait_ge(nT_full, b.x + 1)
                nc.vector.tensor_copy(nT[:, 0], ps[0:H, 6, 0:L]).then_inc(nT_read, 1)

            def split_max(b):
                v.wait_ge(nT_read, b.x + 1)
                hold(v, nstored, 16, b, 0)
                nc.vector.tensor_copy(nparts[:, 0], nT[:, 0]).then_inc(nsplit, 1)
                v.wait_ge(nsplit, b.x * 4 + 1)
                nc.vector.tensor_tensor(nT[:, 1], nT[:, 0], nparts[:, 0], ALU.subtract).then_inc(nsplit, 1)
                v.wait_ge(nsplit, b.x * 4 + 2)
                nc.vector.tensor_copy(nparts[:, 1], nT[:, 1]).then_inc(nsplit, 1)
                v.wait_ge(nsplit, b.x * 4 + 3)
                hold(v, nspread, 16, b, 0)
                nc.vector.tensor_tensor(nparts[:, 2], nT[:, 1], nparts[:, 1], ALU.subtract).then_inc(nsplit, 1)

            def divide(k):
                def step(b):
                    oT = ps[:, 7].rearrange("p (g j r) -> p g j r", g=HG, j=HJ)
                    v.wait_ge(d_full, b.x * D_STEPS + 1 + k)
                    nc.vector.reciprocal(rden[:, k], oT[:, :, :, HD]).then_inc(dve_d, 1)
                    if k == 0:
                        nc.vector.tensor_copy(ga[:, 0:1], modT[:, 0, 2, bass.ds(b.x, 1)])
                        nc.vector.tensor_copy(ga[:, 1:2], gabo[:, bass.ds(b.x, 1)])
                    v.wait_ge(dve_d, b.x * TB + k + 1)
                    nc.vector.tensor_tensor(on[:, k].rearrange("p j g d -> p g j d"), oT[:, :, :, 0:HD],
                                            rden[:, k].unsqueeze(3).to_broadcast([P, HG, HJ, HD]), ALU.mult
                                            ).then_inc(d_read, 1)
                return step

            def residual(b):
                v.wait_ge(d_full, b.x * D_STEPS + 5)
                xs = x[:, bass.ds(b.x * TB, TB), :]
                nc.vector.tensor_tensor(xs, xs, ps[:, 7, 0:L].rearrange("p (k d) -> p k d", d=D), ALU.add
                                        ).then_inc(d_read, 1)

            run(v, [("M", maxima(2, 0)), ("M", maxima(2, 1)), ("M", maxima(2, 2)), ("S", values),
                    ("M", maxima(3, 0)), ("D", divide(0)), ("M", maxima(3, 1)), ("M", maxima(3, 2)),
                    ("D", divide(1)), ("A", rotate(0)), ("N", maxima(0, 0)), ("A", rotate(1)),
                    ("M", take_max), ("M", split_max), ("N", maxima(0, 1)), ("N", maxima(0, 2)), ("N", maxima(1, 0)),
                    ("L", statistics), ("N", maxima(1, 1)), ("D", residual), ("N", maxima(1, 2)),
                    ("L", normalise)])


def experts0(nc, s, t, ps):
    x, modT, ident = s["x"], s["modT"], s["ident"]
    NI, K, UNITS = T // MT, MT // P, PAIRS + 1
    HALVES = MT // L
    with ExitStack() as ctx:
        def sb(name, shape, dt=F32):
            return ctx.enter_context(nc.sbuf_tensor("e0_" + name, shape, dt))

        def sem(name):
            return ctx.enter_context(nc.semaphore("e0_" + name))

        wg, wu, wd = sb("wg", [P, UNITS, P]), sb("wu", [P, UNITS, P]), sb("wd", [P, UNITS, D])
        wr = sb("wr", [P, E0])
        bias = sb("bias", [P, E0])
        pairf, pair = sb("pairf", [96, PAIRS, P]), sb("pair", [96, PAIRS, P], BF16)
        gb, cb, sbb = sb("gb", [P, HALVES]), sb("cb", [P, HALVES]), sb("sb", [P, HALVES])
        stat, mv, rstd = sb("stat", [P, K, 6]), sb("mv", [P, K, 2]), sb("rstd", [P, K])
        y, hT = sb("y", [P, K, D]), sb("hT", [P, 2, MT])
        mx, ex, den, rw = sb("mx", [P, K]), sb("ex", [P, K, E0]), sb("den", [P, K]), sb("rw", [P, K, E0])
        cor = sb("cor", [P, K, E0 + 2])
        top, rep, sel = sb("top", [P, K, 8]), sb("rep", [P, K, E0 + 2]), sb("sel", [P, K, E0])
        rest, c3 = sb("rest", [E0, 2, MT]), sb("c3", [96, 2, MT], BF16)
        sg, hm = sb("sg", [P, 2, MT]), sb("hm", [P, 2, MT])
        pause = sb("pause", [P, 1])
        up = sb("up", [P, 2, MT])
        yo = sb("yo", [P, MT])

        loaded, setup = sem("loaded"), sem("setup")
        stats_done, rstd_done, y_done = sem("stats_done"), sem("rstd_done"), sem("y_done")
        a_full, a_read = sem("a_full"), sem("a_read")
        o_full, o_read = sem("o_full"), sem("o_read")
        logits_done, exp_done, comb_done, split_done = sem("logits"), sem("exp"), sem("comb"), sem("split")
        gates_full, ups_full = sem("gates_full"), sem("ups_full")
        silu_done, up_done, hidden_done = sem("silu_done"), sem("up_done"), sem("hidden_done")
        down_done = sem("down_done")
        gate_done, sum_read = sem("gate_done"), sem("sum_read")
        dve = sem("dve")
        block = ctx.enter_context(nc.Block())
        A, DVE = 3, 25

        def run(eng, order):
            ahead = {"O": -1, "U": 0, "A": 1}

            def body(b):
                for stage, step in order:
                    c = b + ahead[stage]
                    if 0 <= c.k < NI:
                        step(c)
            pipeline(eng, -1, NI + 1, 1, NI - 1, body, turns=2)

        def between(units, others):
            out = []
            for u, step in enumerate(units):
                out.append(("U", step))
                out += [(stage, f) for at, stage, f in others if at == u]
            return out

        @block.sync
        def _(sp):
            for dst, name in ((wg, "e0_wg"), (wu, "e0_wu"), (wd, "e0_wd"), (wr, "e0_wr"), (pairf, "c_pair")):
                sp.dma_start(dst[:], t[name]).then_inc(loaded, 16)
            sp.dma_start(bias[:], t["L0_ffn_e_score_bias"].partition_broadcast(P)).then_inc(loaded, 16)

        @block.gpsimd
        def _(pool):
            def rstd_of(b):
                pool.wait_ge(stats_done, b.x + 1)
                nc.gpsimd.tensor_tensor(rstd[:], mv[:, :, 1], s["eps"][:, 0:K], ALU.add).then_inc(rstd_done, 1)
                pool.wait_ge(rstd_done, b.x * 2 + 1)
                nc.gpsimd.tensor_tensor(rstd[:], rstd[:], s["pm5"][:, 0:K], ALU.pow).then_inc(rstd_done, 1)

            run(pool, [("A", rstd_of)])

        @block.scalar
        def _(act):
            def modulate(b):
                act.wait_ge(a_full, b.x * A + 1)
                for k in range(HALVES):
                    a = nc.scalar.activation(hT[:, b.k % 2, k * L:(k + 1) * L], ps[:, 1, k * L:(k + 1) * L],
                                             ACT.Identity, bias=sbb[:, k:k + 1], scale=cb[:, k:k + 1])
                a.then_inc(a_read, 1)

            def router_exp(b):
                act.wait_ge(logits_done, b.x + 1)
                nc.scalar.activation(ex[:], ex[:], ACT.Exp).then_inc(exp_done, 1)

            def silu(u):
                def step(b):
                    par = (b.k + u) % 2
                    act.wait_ge(gates_full, b.x * UNITS + u + 1)
                    hold(act, up_done, UNITS, b, u - 1)
                    nc.scalar.activation(sg[:, par], ps[:, 2 + par], ACT.Silu).then_inc(silu_done, 1)
                return step

            def gated(b):
                act.wait_ge(down_done, b.x * UNITS + UNITS)
                act.wait_ge(gate_done, b.x + 1)
                for k in range(HALVES):
                    a = nc.scalar.activation(yo[:, k * L:(k + 1) * L], ps[:, 0, k * L:(k + 1) * L], ACT.Copy,
                                             scale=gb[:, k:k + 1])
                a.then_inc(sum_read, 1)

            run(act, between([silu(u) for u in range(UNITS)],
                             [(1, "O", gated), (4, "A", modulate), (7, "A", router_exp)]))

        @block.tensor
        def _(pe):
            pe.wait_ge(setup, 1)

            def unit(u):
                def step(b):
                    par = (b.k + u) % 2
                    if u == 0:
                        pe.wait_ge(a_read, b.x * A + 3)
                        pe.wait_ge(split_done, b.x * 2 + 2)
                    hold(pe, silu_done, UNITS, b, u - 1)
                    nc.tensor.matmul(ps[:, 2 + par, :], wg[:, u, :], hT[:, b.k % 2, :], start=True, stop=True
                                     ).then_inc(gates_full, 1)
                    if u >= 2:
                        down(u - 2)(b)
                    elif b.k > 0:
                        down(UNITS + u - 2)(b + -1)
                    hold(pe, hidden_done, UNITS, b, u - 1)
                    mm = nc.tensor.matmul(ps[:, 4 + par, :], wu[:, u, :], hT[:, b.k % 2, :], start=True, stop=True)
                    if u >= 1:
                        mm = nc.tensor.matmul(ps[:, 6 + par, :], pair[:, u - 1, :], c3[:, b.k % 2, :],
                                              start=True, stop=True)
                    mm.then_inc(ups_full, 1)
                return step

            def down(u):
                def step(b):
                    pe.wait_ge(hidden_done, b.x * UNITS + u + 1)
                    if u == 0:
                        hold(pe, sum_read, 1, b, 0)
                    nc.tensor.matmul(ps[:, 0, :], wd[:, u, :], hm[:, (b.k + u) % 2, :],
                                     start=(u == 0), stop=(u == UNITS - 1), skip_group_check=True
                                     ).then_inc(down_done, 1)
                return step

            def last_downs(b):
                if b.k == NI - 1:
                    down(UNITS - 2)(b)
                    down(UNITS - 1)(b)

            def turn_back(b):
                pe.wait_ge(sum_read, b.x + 1)
                pe.wait_ge(a_read, b.x * A + 2 * A if b.k + 1 < NI else NI * A)
                for k in range(K):
                    mm = nc.tensor.transpose(ps[:, 1, k * P:(k + 1) * P], yo[:, k * P:(k + 1) * P], ident[:])
                mm.then_inc(o_full, 1)

            def turn_tokens(b):
                pe.wait_ge(y_done, b.x + 1)
                hold(pe, a_read, A, b, 0)
                hold(pe, o_read, 1, b + -1, 0)
                for k in range(K):
                    mm = nc.tensor.transpose(ps[:, 1, k * P:(k + 1) * P], y[:, k, :], ident[:])
                mm.then_inc(a_full, 1)

            def route(b):
                pe.wait_ge(a_read, b.x * A + 1)
                for k in range(K):
                    mm = nc.tensor.matmul(ps[:, 1, k * E0:(k + 1) * E0], hT[:, b.k % 2, k * P:(k + 1) * P], wr[:],
                                          start=True, stop=True)
                mm.then_inc(a_full, 1)

            def turn_weights(b):
                pe.wait_ge(a_read, b.x * A + 2)
                pe.wait_ge(comb_done, b.x + 1)
                for k in range(K):
                    mm = nc.tensor.transpose(ps[0:E0, 1, k * P:(k + 1) * P], sel[:, k, :], ident[:])
                mm.then_inc(a_full, 1)

            run(pe, [("O", last_downs)] + between([unit(u) for u in range(UNITS)],
                [(2, "O", turn_back), (4, "A", turn_tokens), (5, "A", route), (13, "A", turn_weights)]))

        @block.vector
        def _(v):
            v.wait_ge(loaded, 96)
            nc.vector.memset(cor[:], NEG)
            nc.vector.tensor_copy(pair[:], pairf[:]).then_inc(setup, 1)
            v.wait_ge(setup, 1)
            wide = [P, K, E0]
            lg = ps[:, 1, 0:K * E0].rearrange("p (k e) -> p k e", e=E0)

            def statistics(b):
                for k in range(K):
                    nc.vector.bn_stats(stat[:, k, :], x[:, bass.ds(b.x * K + k, 1), :].rearrange("p a d -> p (a d)")
                                       ).then_inc(dve, 1)

            def moments(b):
                v.wait_ge(dve, b.x * DVE + 4)
                hold(v, a_read, A, b, 0)
                nc.vector.tensor_copy(cb[:], modT[:, 0, 4, bass.ds(b.x * HALVES, HALVES)])
                nc.vector.tensor_copy(sbb[:], modT[:, 0, 3, bass.ds(b.x * HALVES, HALVES)])
                for k in range(K):
                    n = nc.vector.bn_aggr(mv[:, k, :], stat[:, k, :])
                n.then_inc(stats_done, 1)

            def normalise(b):
                v.wait_ge(rstd_done, b.x * 2 + 2)
                for k in range(K):
                    n = nc.vector.tensor_scalar(y[:, k, :], x[:, bass.ds(b.x * K + k, 1), :].rearrange("p a d -> p (a d)"),
                                                mv[:, k, 0:1], rstd[:, k:k + 1], ALU.subtract, ALU.mult)
                n.then_inc(y_done, 1)

            def logits(b):
                c = Count(b.x * DVE + 4)
                v.wait_ge(a_full, b.x * A + 2)
                nc.vector.tensor_reduce(mx[:], lg, AX_X, ALU.max).then_inc(dve, c.up())
                v.wait_ge(dve, c.now())
                nc.vector.tensor_tensor(ex[:], lg, mx[:].unsqueeze(2).to_broadcast(wide), ALU.subtract
                                        ).then_inc(logits_done, 1)
                v.wait_ge(logits_done, b.x + 1)
                nc.vector.memset(pause[:], 0.0).then_inc(a_read, 1)

            def softmax(b):
                c = Count(b.x * DVE + 5)
                v.wait_ge(exp_done, b.x + 1)
                nc.vector.tensor_reduce(den[:], ex[:], AX_X, ALU.add).then_inc(dve, c.up())
                v.wait_ge(dve, c.now())
                nc.vector.reciprocal(den[:], den[:]).then_inc(dve, c.up())
                v.wait_ge(dve, c.now())
                nc.vector.tensor_tensor(rw[:], ex[:], den[:].unsqueeze(2).to_broadcast(wide), ALU.mult
                                        ).then_inc(dve, c.up())
                v.wait_ge(dve, c.now())
                nc.vector.tensor_tensor(cor[:, :, 0:E0], rw[:], bias[:].unsqueeze(1).to_broadcast(wide), ALU.add
                                        ).then_inc(dve, c.up())

            def top_eight(b):
                c = Count(b.x * DVE + 9)
                v.wait_ge(dve, c.now())
                nc.vector.memset(pause[:], 0.0)
                for k in range(K):
                    nc.vector.max(top[:, k, :], cor[:, k, :]).then_inc(dve, c.up())

            def replace_six(b):
                c = Count(b.x * DVE + 13)
                v.wait_ge(dve, c.now())
                nc.vector.memset(top[:, :, TOP_K:8], NEG).then_inc(dve, c.up())
                v.wait_ge(dve, c.now())
                nc.vector.memset(pause[:], 0.0)
                for k in range(K):
                    nc.vector.match_replace(rep[:, k, :], top[:, k, :], cor[:, k, :], -NEG).then_inc(dve, c.up())

            def chosen(b):
                c = Count(b.x * DVE + 18)
                v.wait_ge(dve, c.now())
                nc.vector.tensor_tensor(sel[:], rep[:, :, 0:E0], cor[:, :, 0:E0], ALU.not_equal).then_inc(dve, c.up())
                v.wait_ge(dve, c.now())
                nc.vector.tensor_tensor(sel[:], sel[:], rw[:], ALU.mult).then_inc(dve, c.up())
                v.wait_ge(dve, c.now())
                nc.vector.tensor_reduce(den[:], sel[:], AX_X, ALU.add).then_inc(dve, c.up())

            def weights(b):
                c = Count(b.x * DVE + 21)
                v.wait_ge(dve, c.now())
                nc.vector.tensor_scalar(den[:], den[:], NORM_MIN, None, ALU.max).then_inc(dve, c.up())
                v.wait_ge(dve, c.now())
                nc.vector.reciprocal(den[:], den[:]).then_inc(dve, c.up())
                v.wait_ge(dve, c.now())
                nc.vector.tensor_tensor(sel[:], sel[:], den[:].unsqueeze(2).to_broadcast(wide), ALU.mult
                                        ).then_inc(comb_done, 1)

            def split_first(b):
                c = Count(b.x * DVE + 23)
                cT, c3b = ps[0:E0, 1, :], c3[:, b.k % 2]
                v.wait_ge(a_full, b.x * A + 3)
                nc.vector.tensor_copy(c3b[0:E0, :], cT).then_inc(dve, c.up())
                v.wait_ge(dve, c.now())
                nc.vector.tensor_tensor(rest[:, 0, :], cT, c3b[0:E0, :], ALU.subtract).then_inc(a_read, 1)

            def split_rest(b):
                c, c3b = Count(b.x * DVE + 24), c3[:, b.k % 2]
                v.wait_ge(a_read, b.x * A + 3)
                nc.vector.tensor_copy(c3b[E0:2 * E0, :], rest[:, 0, :]).then_inc(dve, c.up())
                v.wait_ge(dve, c.now())
                nc.vector.tensor_tensor(rest[:, 1, :], rest[:, 0, :], c3b[E0:2 * E0, :], ALU.subtract
                                        ).then_inc(split_done, 1)
                v.wait_ge(split_done, b.x * 2 + 1)
                nc.vector.tensor_copy(c3b[2 * E0:3 * E0, :], rest[:, 1, :]).then_inc(split_done, 1)

            def hidden(u):
                def step(b):
                    par = (b.k + u) % 2
                    v.wait_ge(silu_done, b.x * UNITS + u + 1)
                    v.wait_ge(ups_full, b.x * UNITS + u + 1)
                    hold(v, down_done, UNITS, b, u - 1)
                    if u == 0:
                        nc.vector.tensor_tensor(hm[:, par], sg[:, par], ps[:, 4 + par], ALU.mult).then_inc(up_done, 1)
                        v.wait_ge(up_done, b.x * UNITS + 1)
                        nc.vector.memset(pause[:], 0.0).then_inc(hidden_done, 1)
                        return
                    nc.vector.tensor_tensor(up[:, par], sg[:, par], ps[:, 4 + par], ALU.mult).then_inc(up_done, 1)
                    v.wait_ge(up_done, b.x * UNITS + u + 1)
                    nc.vector.tensor_tensor(hm[:, par], up[:, par], ps[:, 6 + par], ALU.mult).then_inc(hidden_done, 1)
                return step

            def gate(b):
                hold(v, sum_read, 1, b, 0)
                nc.vector.tensor_copy(gb[:], modT[:, 0, 5, bass.ds(b.x * HALVES, HALVES)]).then_inc(gate_done, 1)

            def residual(b):
                v.wait_ge(o_full, b.x + 1)
                xs = x[:, bass.ds(b.x * K, K), :]
                nc.vector.tensor_tensor(xs, xs, ps[:, 1, :].rearrange("p (k d) -> p k d", d=D), ALU.add
                                        ).then_inc(o_read, 1)

            run(v, between([hidden(u) for u in range(UNITS)],
                           [(0, "A", statistics), (1, "A", moments), (2, "A", normalise), (3, "O", residual),
                            (6, "A", logits), (8, "A", softmax), (9, "A", top_eight), (10, "A", replace_six),
                            (11, "A", chosen), (12, "A", weights), (14, "A", split_first), (15, "A", split_rest),
                            (16, "U", gate)]))


def experts1(nc, s, t, ps):
    x, modT, ident = s["x"], s["modT"], s["ident"]
    NI, K = T // MT, MT // P
    HALVES = MT // L
    with ExitStack() as ctx:
        def sb(name, shape, dt=F32):
            return ctx.enter_context(nc.sbuf_tensor("e1_" + name, shape, dt))

        def sem(name):
            return ctx.enter_context(nc.semaphore("e1_" + name))

        w1, w2 = sb("w1", [P, E1, D]), sb("w2", [P, E1, D])
        b1, b2 = sb("b1", [P, E1]), sb("b2", [E1, D])
        wr, br = sb("wr", [P, E1]), sb("br", [P, E1])
        rank = sb("rank", [P, E1])
        onef, one = sb("onef", [96, E1 + 1, P]), sb("one", [96, E1 + 1, P], BF16)
        uptof, upto, ones = sb("uptof", [P, P]), sb("upto", [P, P], BF16), sb("ones", [P, P], BF16)
        gb, cb, sbb = sb("gb", [P, HALVES]), sb("cb", [P, HALVES]), sb("sb", [P, HALVES])
        stat, mv, rstd = sb("stat", [P, K, 6]), sb("mv", [P, K, 2]), sb("rstd", [P, K])
        y, hT, hg = sb("y", [P, K, D]), sb("hT", [P, MT]), sb("hg", [P, MT])
        lg, mx, den = sb("lg", [P, K, E1]), sb("mx", [P, K]), sb("den", [P, K])
        ex, oh, wt = sb("ex", [P, K, E1]), sb("oh", [P, K, E1]), sb("wt", [P, K, E1])
        gate = sb("gate", [P, K])
        ohb = sb("ohb", [P, K, E1], BF16)
        before = sb("before", [P, K + 1, E1])
        beforeb = sb("beforeb", [P, K, E1], BF16)
        rest, c3, wT = sb("rest", [E1, 2, MT]), sb("c3", [96, MT], BF16), sb("wT", [E1, MT])
        r, hm = sb("r", [P, 2, MT]), sb("hm", [P, 2, MT])
        yo = sb("yo", [P, MT])

        loaded = sem("loaded")
        stats_done, rstd_done, y_done, mod_done = sem("stats_done"), sem("rstd_done"), sem("y_done"), sem("mod_done")
        small_full, small_free = sem("small_full"), sem("small_free")
        logits_done, exp_done, chosen, w_done = sem("logits"), sem("exp"), sem("chosen"), sem("w_done")
        counted, split_done = sem("counted"), sem("split")
        sum_full, hg_done = sem("sum_full"), sem("hg_done")
        unit_full, relu_done, hidden_done = sem("unit_full"), sem("relu_done"), sem("hidden_done")
        down_done = sem("down_done")
        out_read, dve, setup = sem("out_read"), sem("dve"), sem("setup")
        block = ctx.enter_context(nc.Block())
        DVE, SMALL = 25, 4

        @block.sync
        def _(sp):
            for dst, name in ((w1, "e1_w1"), (w2, "e1_w2"), (b1, "e1_b1"), (b2, "L1_ffn_b2"), (wr, "L1_ffn_Wr"),
                              (onef, "c_one"), (uptof, "c_upto")):
                sp.dma_start(dst[:], t[name]).then_inc(loaded, 16)
            sp.dma_start(br[:], t["L1_ffn_br"].partition_broadcast(P)).then_inc(loaded, 16)

        @block.gpsimd
        def _(pool):
            with pool.Fori(0, NI) as i:
                pool.wait_ge(stats_done, i + 1)
                nc.gpsimd.tensor_tensor(rstd[:], mv[:, :, 1], s["eps"][:, 0:K], ALU.add).then_inc(rstd_done, 1)
                pool.wait_ge(rstd_done, i * 2 + 1)
                nc.gpsimd.tensor_tensor(rstd[:], rstd[:], s["pm5"][:, 0:K], ALU.pow).then_inc(rstd_done, 1)

        @block.scalar
        def _(act):
            with act.Fori(0, NI) as i:
                act.wait_ge(mod_done, i + 1)
                act.wait_ge(small_full, i * SMALL + 1)
                for k in range(HALVES):
                    a = nc.scalar.activation(hT[:, k * L:(k + 1) * L], ps[:, 1, k * L:(k + 1) * L], ACT.Identity,
                                             bias=sbb[:, k:k + 1], scale=cb[:, k:k + 1])
                a.then_inc(small_free, 1)
                act.wait_ge(logits_done, i + 1)
                nc.scalar.activation(ex[:], ex[:], ACT.Exp).then_inc(exp_done, 1)
                for u in range(E1):
                    act.wait_ge(unit_full, i * E1 + u + 1)
                    if u >= 2:
                        act.wait_ge(hidden_done, i * E1 + u - 1)
                    nc.scalar.activation(r[:, u % 2], ps[:, 2 + u % 2], ACT.Relu, bias=b1[:, u:u + 1]
                                         ).then_inc(relu_done, 1)
                act.wait_ge(down_done, (i + 1) * E1)
                for k in range(HALVES):
                    a = nc.scalar.activation(yo[:, k * L:(k + 1) * L], ps[:, 0, k * L:(k + 1) * L], ACT.Copy,
                                             scale=gb[:, k:k + 1])
                a.then_inc(out_read, 1)

        @block.tensor
        def _(pe):
            pe.wait_ge(setup, 1)
            with pe.Fori(0, NI) as i:
                pe.wait_ge(small_free, i * SMALL + 1)
                pe.wait_ge(y_done, i + 1)
                for k in range(K):
                    mm = nc.tensor.transpose(ps[:, 1, k * P:(k + 1) * P], y[:, k, :], ident[:])
                mm.then_inc(small_full, 1)
                pe.wait_ge(small_free, i * SMALL + 2)
                for k in range(K):
                    mm = nc.tensor.matmul(ps[:, 1, k * E1:(k + 1) * E1], hT[:, k * P:(k + 1) * P], wr[:],
                                          start=True, stop=True)
                mm.then_inc(small_full, 1)
                pe.wait_ge(chosen, i + 1)
                nc.tensor.matmul(ps[:, 7, 0:K * E1], upto[:], ohb[:].rearrange("p k e -> p (k e)"),
                                 start=True, stop=False)
                nc.tensor.matmul(ps[:, 7, 0:K * E1], ones[:], beforeb[:].rearrange("p k e -> p (k e)"),
                                 start=False, stop=True).then_inc(counted, 1)
                pe.wait_ge(w_done, i + 1)
                pe.wait_ge(small_free, i * SMALL + 3)
                for k in range(K):
                    mm = nc.tensor.transpose(ps[0:E1, 1, k * P:(k + 1) * P], wt[:, k, :], ident[:])
                mm.then_inc(small_full, 1)
                pe.wait_ge(split_done, i + 1)
                nc.tensor.matmul(ps[:, 6, :], one[:, E1, :], c3[:], start=True, stop=True).then_inc(sum_full, 1)
                nc.tensor.matmul(ps[:, 0, :], b2[:], wT[:], start=True, stop=False, skip_group_check=True)
                pe.wait_ge(hg_done, i + 1)
                for u in range(E1 + 1):
                    if u < E1:
                        if u >= 2:
                            pe.wait_ge(hidden_done, i * E1 + u - 1)
                        nc.tensor.matmul(ps[:, 2 + u % 2, :], w1[:, u, :], hg[:], start=True, stop=True)
                        nc.tensor.matmul(ps[:, 4 + u % 2, :], one[:, u, :], c3[:], start=True, stop=True
                                         ).then_inc(unit_full, 1)
                    if u >= 1:
                        pe.wait_ge(hidden_done, i * E1 + u)
                        nc.tensor.matmul(ps[:, 0, :], w2[:, u - 1, :], hm[:, (u - 1) % 2, :],
                                         start=False, stop=(u == E1), skip_group_check=True).then_inc(down_done, 1)
                pe.wait_ge(out_read, i + 1)
                pe.wait_ge(small_free, i * SMALL + 4)
                for k in range(K):
                    mm = nc.tensor.transpose(ps[:, 1, k * P:(k + 1) * P], yo[:, k * P:(k + 1) * P], ident[:])
                mm.then_inc(small_full, 1)

        @block.vector
        def _(v):
            v.wait_ge(loaded, 128)
            nc.vector.memset(ones[:], 1.0)
            nc.vector.memset(before[:], 0.0)
            nc.vector.memset(c3[:], 0.0)
            for e in range(E1):
                nc.vector.memset(rank[:, e:e + 1], float(E1 - e))
            nc.vector.tensor_copy(one[:], onef[:])
            nc.vector.tensor_copy(upto[:], uptof[:]).then_inc(setup, 1)
            nc.vector.memset(mx[:], 0.0).then_inc(small_free, 1)
            v.wait_ge(small_free, 1)
            with v.Fori(0, NI) as i:
                c = Count(i * DVE)
                for k in range(K):
                    nc.vector.bn_stats(stat[:, k, :], x[:, bass.ds(i * K + k, 1), :].rearrange("p a d -> p (a d)")
                                       ).then_inc(dve, c.up())
                v.wait_ge(dve, c.now())
                nc.vector.tensor_copy(gb[:], modT[:, 1, 5, bass.ds(i * HALVES, HALVES)])
                nc.vector.tensor_copy(cb[:], modT[:, 1, 4, bass.ds(i * HALVES, HALVES)])
                nc.vector.tensor_copy(sbb[:], modT[:, 1, 3, bass.ds(i * HALVES, HALVES)]).then_inc(mod_done, 1)
                for k in range(K):
                    n = nc.vector.bn_aggr(mv[:, k, :], stat[:, k, :])
                n.then_inc(stats_done, 1)
                v.wait_ge(rstd_done, i * 2 + 2)
                for k in range(K):
                    n = nc.vector.tensor_scalar(y[:, k, :], x[:, bass.ds(i * K + k, 1), :].rearrange("p a d -> p (a d)"),
                                                mv[:, k, 0:1], rstd[:, k:k + 1], ALU.subtract, ALU.mult)
                n.then_inc(y_done, 1)
                v.wait_ge(small_full, i * SMALL + 2)
                wide = [P, K, E1]
                nc.vector.tensor_tensor(lg[:], ps[:, 1, 0:K * E1].rearrange("p (k e) -> p k e", e=E1),
                                        br[:].unsqueeze(1).to_broadcast(wide), ALU.add).then_inc(small_free, 1)
                v.wait_ge(small_free, i * SMALL + 3)
                nc.vector.tensor_reduce(mx[:], lg[:], AX_X, ALU.max).then_inc(dve, c.up())
                v.wait_ge(dve, c.now())
                nc.vector.tensor_tensor(ex[:], lg[:], mx[:].unsqueeze(2).to_broadcast(wide), ALU.subtract
                                        ).then_inc(logits_done, 1)
                v.wait_ge(exp_done, i + 1)
                nc.vector.tensor_reduce(den[:], ex[:], AX_X, ALU.add).then_inc(dve, c.up())
                v.wait_ge(dve, c.now())
                nc.vector.reciprocal(den[:], den[:]).then_inc(dve, c.up())
                v.wait_ge(dve, c.now())
                nc.vector.tensor_tensor(ex[:], ex[:], den[:].unsqueeze(2).to_broadcast(wide), ALU.mult
                                        ).then_inc(dve, c.up())
                v.wait_ge(dve, c.now())
                nc.vector.tensor_reduce(gate[:], ex[:], AX_X, ALU.max).then_inc(dve, c.up())
                v.wait_ge(dve, c.now())
                nc.vector.tensor_tensor(oh[:], ex[:], gate[:].unsqueeze(2).to_broadcast(wide), ALU.is_equal
                                        ).then_inc(dve, c.up())
                v.wait_ge(dve, c.now())
                nc.vector.tensor_tensor(oh[:], oh[:], rank[:].unsqueeze(1).to_broadcast(wide), ALU.mult
                                        ).then_inc(dve, c.up())
                v.wait_ge(dve, c.now())
                nc.vector.tensor_reduce(mx[:], oh[:], AX_X, ALU.max).then_inc(dve, c.up())
                v.wait_ge(dve, c.now())
                nc.vector.tensor_tensor(oh[:], oh[:], mx[:].unsqueeze(2).to_broadcast(wide), ALU.is_equal
                                        ).then_inc(dve, c.up())
                v.wait_ge(dve, c.now())
                for k in range(K):
                    nc.vector.tensor_tensor(before[:, k + 1, :], before[:, k, :], oh[:, k, :], ALU.add
                                            ).then_inc(dve, c.up())
                    v.wait_ge(dve, c.now())
                nc.vector.tensor_copy(ohb[:], oh[:]).then_inc(dve, c.up())
                nc.vector.tensor_copy(beforeb[:], before[:, 0:K, :]).then_inc(chosen, 1)
                v.wait_ge(chosen, i + 1)
                nc.vector.tensor_copy(before[:, 0, :], before[:, K, :]).then_inc(dve, c.up())
                nc.vector.tensor_tensor(wt[:], oh[:], gate[:].unsqueeze(2).to_broadcast(wide), ALU.mult
                                        ).then_inc(dve, c.up())
                v.wait_ge(dve, c.now())
                v.wait_ge(counted, i + 1)
                nc.vector.tensor_scalar(oh[:], ps[:, 7, 0:K * E1].rearrange("p (k e) -> p k e", e=E1), float(CAP),
                                        None, ALU.is_lt).then_inc(dve, c.up())
                v.wait_ge(dve, c.now())
                nc.vector.tensor_tensor(wt[:], wt[:], oh[:], ALU.mult).then_inc(w_done, 1)
                v.wait_ge(small_full, i * SMALL + 3)
                nc.vector.tensor_copy(wT[:], ps[0:E1, 1, :]).then_inc(small_free, 1)
                v.wait_ge(small_free, i * SMALL + 4)
                nc.vector.tensor_copy(c3[0:E1, :], wT[:]).then_inc(dve, c.up())
                v.wait_ge(dve, c.now())
                nc.vector.tensor_tensor(rest[:, 0, :], wT[:], c3[0:E1, :], ALU.subtract).then_inc(dve, c.up())
                v.wait_ge(dve, c.now())
                nc.vector.tensor_copy(c3[32:32 + E1, :], rest[:, 0, :]).then_inc(dve, c.up())
                v.wait_ge(dve, c.now())
                nc.vector.tensor_tensor(rest[:, 1, :], rest[:, 0, :], c3[32:32 + E1, :], ALU.subtract
                                        ).then_inc(dve, c.up())
                v.wait_ge(dve, c.now())
                nc.vector.tensor_copy(c3[64:64 + E1, :], rest[:, 1, :]).then_inc(split_done, 1)
                v.wait_ge(sum_full, i + 1)
                nc.vector.tensor_tensor(hg[:], hT[:], ps[:, 6, :], ALU.mult).then_inc(hg_done, 1)
                for u in range(E1):
                    v.wait_ge(relu_done, i * E1 + u + 1)
                    if u >= 2:
                        v.wait_ge(down_done, i * E1 + u - 1)
                    nc.vector.tensor_tensor(hm[:, u % 2], r[:, u % 2], ps[:, 4 + u % 2], ALU.mult
                                            ).then_inc(hidden_done, 1)
                v.wait_ge(small_full, i * SMALL + 4)
                xs = x[:, bass.ds(i * K, K), :]
                nc.vector.tensor_tensor(xs, xs, ps[:, 1, :].rearrange("p (k d) -> p k d", d=D), ALU.add
                                        ).then_inc(small_free, 1)
                assert c.n == DVE, c.n


def attention1(nc, s, t, ps):
    x, modT, ident = s["x"], s["modT"], s["ident"]
    UNITS = [list(range(a, min(a + 4, NO))) for a in range(0, NO, 4)]
    NU = len(UNITS)
    GUNITS = [NU - 3, NU - 2]
    VUNITS = [u for u in range(NU) if u not in GUNITS]
    NG, NV = len(GUNITS), len(VUNITS)
    RING = NU - 1
    W = NO * H
    WK = -(-W // 64) * 64
    INV = float(1.0 / np.sqrt(np.float32(HD)))
    assert NU % 2 == 0
    with ExitStack() as ctx:
        def sb(name, shape, dt=F32):
            return ctx.enter_context(nc.sbuf_tensor("a1_" + name, shape, dt))

        def sem(name):
            return ctx.enter_context(nc.semaphore("a1_" + name))

        w = sb("w", [P, 5, D])
        bcol = sb("bcol", [P, 5])
        hbg = sb("hbg", [P, 1])
        ifg = sb("ifg", [P, 1])
        inv = sb("inv", [P, 1])
        emb = sb("emb", [P, W])
        headsum = sb("headsum", [P, 7 * H])
        pb = sb("pb", [P, TB, W])
        pbr = sb("pbr", [P, W])
        early = sb("early", [P, TB, NO])
        gabo = sb("gabo", [P, B])
        ga, ca, sa = sb("ga", [P, 2]), sb("ca", [P, 1]), sb("sa", [P, 1])
        stat, mv, rstd = sb("stat", [P, TB, 6]), sb("mv", [P, TB, 2]), sb("rstd", [P, TB])
        y, hT = sb("y", [P, TB, D]), sb("hT", [P, L])
        q = sb("q", [P, 3, L])
        kp, vp = sb("kp", [P, 3, PAD + L]), sb("vp", [P, 3, PAD + L])
        gs = sb("gs", [P, 3, L])
        acc = sb("acc", [P, 3, 4, L])
        th = sb("th", [P, L])
        prod = sb("prod", [P, NO, L])
        g = sb("g", [P, TB * W])
        lg = sb("lg", [P, TB * W])
        mx, den = sb("mx", [P, TB, H]), sb("den", [P, TB, H])
        pe8 = sb("pe8", [P, TB, W, HD])
        denw = sb("denw", [P, TB, D])
        yv = sb("yv", [P, RING, 4, L])
        og = sb("og", [P, L])
        yo = sb("yo", [P, L])

        loaded, setup = sem("loaded"), sem("setup")
        stats_done, rstd_done, y_done = sem("stats_done"), sem("rstd_done"), sem("y_done")
        a_full, a_read = sem("a_full"), sem("a_read")
        g_full, g_read = sem("g_full"), sem("g_read")
        d_full, d_read = sem("d_full"), sem("d_read")
        r_full, r_read = sem("r_full"), sem("r_read")
        th_done, gs_done = sem("th_done"), sem("gs_done")
        prod_v, prod_g = sem("prod_v"), sem("prod_g")
        qk_full, qk_read = sem("qk_full"), sem("qk_read")
        biased, max_done, shifted = sem("biased"), sem("max_done"), sem("shifted")
        exp_done = sem("exp_done")
        pv_full, pv_read = sem("pv_full"), sem("pv_read")
        added = sem("added")
        summed, den_done = sem("summed"), sem("den_done")
        og_done = sem("og_done")
        dve_a = sem("dve_a")
        block = ctx.enter_context(nc.Block())
        A, G, DD = 3, 3, 2

        def shift(pad, b, o0, n):
            a = pad[:, b.k % 3, PAD - ORDER[o0]:PAD - ORDER[o0] + L]
            return bass.AP(tensor=a.tensor, offset=a.offset, ap=[list(a.ap[0]), [1, n], [1, L]])

        def runs(unit):
            out = []
            for o in unit:
                if out and ORDER[o] == ORDER[out[-1][0] + out[-1][1] - 1] - 1:
                    out[-1][1] += 1
                else:
                    out.append([o, 1])
            return out

        def latest(b, n):
            return b + n if b.k + n < B else Batch(B - 1, B - 1)

        def run(eng, order):
            ahead = {"D": -1, "V": 0, "R": 0, "Q": 1, "A": 2, "N": 2}

            def body(b):
                for stage, step in order:
                    c = b + ahead[stage]
                    if 0 <= c.k < B:
                        step(c)
            pipeline(eng, -2, B + 1, 1, B - 2, body)

        @block.sync
        def _(sp):
            for dst, name in ((w, "a1_w"), (bcol, "a1_b"), (ifg, "a1_ifg"), (emb, "a1_emb"), (headsum, "c_headsum"),
                              (early, "c_early")):
                sp.dma_start(dst[:], t[name]).then_inc(loaded, 16)
            sp.dma_start(pbr[:], t["a1_pb"].partition_broadcast(P)).then_inc(loaded, 16)

        @block.gpsimd
        def _(pool):
            nc.gpsimd.memset(inv[:], INV)
            nc.gpsimd.memset(kp[:, :, 0:PAD], 0.0)
            nc.gpsimd.memset(vp[:, :, 0:PAD], 0.0).then_inc(setup, 1)
            pool.wait_ge(setup, 2)

            def rstd_of(b):
                pool.wait_ge(stats_done, b.x + 1)
                nc.gpsimd.tensor_tensor(rstd[:], mv[:, :, 1], s["eps"][:, 0:TB], ALU.add).then_inc(rstd_done, 1)
                pool.wait_ge(rstd_done, b.x * 2 + 1)
                nc.gpsimd.tensor_tensor(rstd[:], rstd[:], s["pm5"][:, 0:TB], ALU.pow).then_inc(rstd_done, 1)

            def products(u):
                def step(b):
                    pool.wait_ge(a_read, b.x * A + 2)
                    hold(pool, qk_full, 1, b, 0)
                    for o0, n in runs(UNITS[u]):
                        m = nc.gpsimd.tensor_tensor(prod[:, o0:o0 + n, :],
                                                    q[:, b.k % 3].unsqueeze(1).to_broadcast([P, n, L]),
                                                    shift(kp, b, o0, n), ALU.mult)
                    m.then_inc(prod_g, 1)
                return step

            def add(u):
                def step(b):
                    a = acc[:, b.k % 3]
                    if u < NU:
                        n = len(UNITS[u])
                        pool.wait_ge(pv_read, b.x * NU + u + 1)
                        hold(pool, added, NU + 1, b, u - 1)
                        nc.gpsimd.tensor_tensor(a[:, 0:n], a[:, 0:n], yv[:, (u - 1) % RING, 0:n], ALU.add
                                                ).then_inc(added, 1)
                    else:
                        pool.wait_ge(added, b.x * (NU + 1) + NU - 1)
                        nc.gpsimd.tensor_tensor(a[:, 0:2], a[:, 0:2], a[:, 2:4], ALU.add).then_inc(added, 1)
                        pool.wait_ge(added, b.x * (NU + 1) + NU)
                        nc.gpsimd.tensor_tensor(a[:, 0], a[:, 0], a[:, 1], ALU.add).then_inc(added, 1)
                return step

            run(pool, [("Q", products(GUNITS[0]))] + [("V", add(1)), ("A", rstd_of), ("V", add(2)),
                 ("V", add(3)), ("Q", products(GUNITS[1]))] + [("V", add(u)) for u in range(4, NU + 1)])

        @block.scalar
        def _(act):
            act.wait_ge(setup, 2)

            def modulate(b):
                act.wait_ge(a_full, b.x * A + 1)
                nc.scalar.activation(hT[:], ps[:, 7, 0:L], ACT.Identity, bias=sa[:], scale=ca[:]).then_inc(a_read, 1)

            def queries_keys(b):
                act.wait_ge(a_full, b.x * A + 2)
                hold(act, qk_full, 1, b + -2, 0)
                nc.scalar.activation(q[:, b.k % 3], ps[:, 7, 0:L], ACT.Identity, bias=bcol[:, 0:1])
                nc.scalar.activation(kp[:, b.k % 3, PAD:], ps[:, 7, L:2 * L], ACT.Identity, bias=bcol[:, 1:2]
                                     ).then_inc(a_read, 1)

            def values_gate(b):
                act.wait_ge(a_full, b.x * A + 3)
                hold(act, pv_read, NU, b + -2, 0)
                hold(act, og_done, 1, b + -2, 0)
                nc.scalar.activation(th[:], ps[:, 7, L:2 * L], ACT.Tanh, bias=hbg[:], scale=0.5).then_inc(th_done, 1)
                nc.scalar.activation(vp[:, b.k % 3, PAD:], ps[:, 7, 0:L], ACT.Identity, bias=bcol[:, 2:3]
                                     ).then_inc(a_read, 1)
                act.wait_ge(th_done, b.x + 1)
                nc.scalar.activation(gs[:, b.k % 3], th[:], ACT.Identity, bias=ifg[:], scale=ifg[:]
                                     ).then_inc(gs_done, 1)

            def factors(n):
                def step(b):
                    cols = slice(512 * n, min(512 * n + 512, TB * W))
                    act.wait_ge(g_full, b.x * G + n + 1)
                    hold(act, qk_read, 1, b, 0)
                    nc.scalar.activation(g[:, cols], ps[:, 7, 0:cols.stop - cols.start], ACT.Identity,
                                         bias=inv[:], scale=INV).then_inc(g_read, 1)
                return step

            def exps(u):
                def step(b):
                    act.wait_ge(shifted, b.x + 1)
                    rows = slice(UNITS[u][0] * H, (UNITS[u][-1] + 1) * H)
                    nc.scalar.activation(pe8[:, :, rows, :],
                                         lg[:].rearrange("p (k w) -> p k w", k=TB)[:, :, rows].unsqueeze(3)
                                         .to_broadcast([P, TB, len(UNITS[u]) * H, HD]), ACT.Exp).then_inc(exp_done, 1)
                return step

            def projected(b):
                act.wait_ge(d_full, b.x * DD + 1)
                nc.scalar.activation(yo[:], ps[:, 7, 0:L], ACT.Identity, bias=ga[:, 1:2], scale=ga[:, 0:1]
                                     ).then_inc(d_read, 1)

            run(act, [("V", exps(0)), ("Q", factors(2)), ("V", exps(1)), ("V", exps(2))] +
                [("V", exps(u)) for u in range(3, NU)] +
                [("D", projected), ("A", modulate), ("A", queries_keys), ("A", values_gate),
                 ("N", factors(0)), ("N", factors(1))])

        @block.tensor
        def _(pe):
            pe.wait_ge(setup, 2)

            def turn_tokens(b):
                hold(pe, d_read, DD, b + -2, 0)
                hold(pe, g_read, G, b, 0)
                hold(pe, a_read, A, b, 0)
                pe.wait_ge(y_done, b.x + 1)
                for k in range(TB):
                    mm = nc.tensor.transpose(ps[:, 7, k * P:(k + 1) * P], y[:, k, :], ident[:])
                mm.then_inc(a_full, 1)

            def project(which):
                def step(b):
                    pe.wait_ge(a_read, b.x * A + 1 + which)
                    if which == 0:
                        hold(pe, r_read, 1, b + -1, 0)
                    for k in range(2):
                        mm = nc.tensor.matmul(ps[:, 7, k * L:(k + 1) * L], w[:, 2 * which + k, :], hT[:],
                                              start=True, stop=True)
                    mm.then_inc(a_full, 1)
                return step

            def factors(n):
                def step(b):
                    if n == 0:
                        pe.wait_ge(a_read, b.x * A + 3)
                    else:
                        pe.wait_ge(g_read, b.x * G + n)
                    for k in range(TB):
                        lo, hi = max(512 * n, W * k), min(512 * n + 512, W * (k + 1))
                        if lo < hi:
                            mm = nc.tensor.matmul(ps[:, 7, lo - 512 * n:hi - 512 * n], q[:, b.k % 3, k * P:(k + 1) * P],
                                                  emb[:, lo - W * k:hi - W * k], start=True, stop=True)
                    mm.then_inc(g_full, 1)
                return step

            def head_sums(u):
                def step(b):
                    if u == 0:
                        hold(pe, qk_read, 1, b, 0)
                    if u in VUNITS:
                        pe.wait_ge(prod_v, b.x * NV + VUNITS.index(u) + 1)
                    else:
                        pe.wait_ge(prod_g, b.x * NG + GUNITS.index(u) + 1)
                    n = len(UNITS[u])
                    for k in range(TB):
                        col = k * WK + UNITS[u][0] * H
                        for j, o in enumerate(UNITS[u]):
                            mm = nc.tensor.matmul(ps[:, 4 + col // 512, col % 512:col % 512 + n * H],
                                                  prod[:, o, k * P:(k + 1) * P],
                                                  headsum[:, (3 - j) * H:(3 - j + n) * H], start=(j == 0), stop=(j == n - 1))
                    if u == NU - 1:
                        mm.then_inc(qk_full, 1)
                return step

            def turn_exps(u):
                def step(b):
                    hold(pe, pv_read, NU, b, u - 1)
                    pe.wait_ge(exp_done, b.x * NU + u + 1)
                    for n, o in enumerate(UNITS[u]):
                        for k in range(TB):
                            row = pe8[:, k, o * H:(o + 1) * H, :].rearrange("p h d -> p (h d)")
                            mm = nc.tensor.transpose(
                                ps[:, 2 * (u % 2) + n // 2, (n % 2) * L + k * P:(n % 2) * L + (k + 1) * P], row, ident[:])
                    mm.then_inc(pv_full, 1)
                return step

            def turn_reciprocals(b):
                hold(pe, d_read, DD, b, 0)
                pe.wait_ge(g_read, latest(b, 1).x * G + G)
                pe.wait_ge(a_read, b.x * A + 2 * A + 1 if b.k + 2 < B else B * A)
                pe.wait_ge(den_done, b.x + 1)
                for k in range(TB):
                    mm = nc.tensor.transpose(ps[:, 7, k * P:(k + 1) * P], denw[:, k, :], ident[:])
                mm.then_inc(r_full, 1)

            def project_out(b):
                pe.wait_ge(g_read, latest(b, 2).x * G + G)
                pe.wait_ge(r_read, b.x + 1)
                hold(pe, d_read, DD, b, 0)
                pe.wait_ge(og_done, b.x + 1)
                nc.tensor.matmul(ps[:, 7, 0:L], w[:, 4, :], og[:], start=True, stop=True).then_inc(d_full, 1)

            def turn_back(b):
                pe.wait_ge(d_read, b.x * DD + 1)
                for k in range(TB):
                    mm = nc.tensor.transpose(ps[:, 7, k * P:(k + 1) * P], yo[:, k * P:(k + 1) * P], ident[:])
                mm.then_inc(d_full, 1)

            run(pe, [("V", turn_exps(0)), ("V", turn_exps(1)), ("Q", head_sums(2)), ("V", turn_exps(2)),
                     ("Q", head_sums(7)), ("V", turn_exps(3)), ("Q", head_sums(3)), ("V", turn_exps(4)),
                     ("D", project_out), ("Q", head_sums(4)), ("V", turn_exps(5)), ("D", turn_back),
                     ("Q", head_sums(5)), ("V", turn_exps(6)), ("A", turn_tokens), ("Q", head_sums(6)),
                     ("V", turn_exps(7)), ("R", turn_reciprocals), ("Q", head_sums(8)), ("V", turn_exps(8)),
                     ("Q", head_sums(9)), ("A", project(0)), ("V", turn_exps(9)),
                     ("A", project(1)), ("N", factors(0)), ("N", head_sums(0)), ("N", factors(1)),
                     ("N", head_sums(1)), ("N", factors(2))])

        @block.vector
        def _(v):
            v.wait_ge(loaded, 112)
            v.wait_ge(setup, 1)
            nc.vector.tensor_scalar(hbg[:], bcol[:, 3:4], 0.5, None, ALU.mult)
            nc.vector.tensor_scalar(ifg[:], ifg[:], 0.5, None, ALU.mult)
            nc.vector.tensor_scalar(gabo[:], modT[:, 1, 2, :], bcol[:, 4:5], None, ALU.mult)
            for k in range(TB):
                n = nc.vector.tensor_tensor(pb[:, k].rearrange("p (o h) -> p o h", h=H),
                                            pbr[:].rearrange("p (o h) -> p o h", h=H),
                                            early[:, k].unsqueeze(2).to_broadcast([P, NO, H]), ALU.add)
            n.then_inc(setup, 1)
            v.wait_ge(setup, 2)

            def statistics(b):
                for k in range(TB):
                    nc.vector.bn_stats(stat[:, k, :], x[:, bass.ds(b.x * TB + k, 1), :].rearrange("p a d -> p (a d)")
                                       ).then_inc(dve_a, 1)

            def moments(b):
                v.wait_ge(dve_a, b.x * TB + TB)
                hold(v, a_read, A, b, 0)
                nc.vector.tensor_copy(ca[:], modT[:, 1, 1, bass.ds(b.x, 1)])
                nc.vector.tensor_copy(sa[:], modT[:, 1, 0, bass.ds(b.x, 1)])
                for k in range(TB):
                    n = nc.vector.bn_aggr(mv[:, k, :], stat[:, k, :])
                n.then_inc(stats_done, 1)

            def normalise(b):
                v.wait_ge(rstd_done, b.x * 2 + 2)
                for k in range(TB):
                    n = nc.vector.tensor_scalar(y[:, k, :], x[:, bass.ds(b.x * TB + k, 1), :].rearrange("p a d -> p (a d)"),
                                                mv[:, k, 0:1], rstd[:, k:k + 1], ALU.subtract, ALU.mult)
                n.then_inc(y_done, 1)

            def products(u):
                def step(b):
                    if u == 0:
                        v.wait_ge(a_read, b.x * A + 2)
                        hold(v, qk_full, 1, b, 0)
                    for o0, n in runs(UNITS[u]):
                        m = nc.vector.tensor_tensor(prod[:, o0:o0 + n, :],
                                                    q[:, b.k % 3].unsqueeze(1).to_broadcast([P, n, L]),
                                                    shift(kp, b, o0, n), ALU.mult)
                    m.then_inc(prod_v, 1)
                return step

            def logits(b):
                v.wait_ge(qk_full, b.x + 1)
                v.wait_ge(g_read, b.x * G + G)
                hold(v, exp_done, NU, b, 0)
                nc.vector.tensor_tensor(lg[:].rearrange("p (k w) -> p k w", k=TB),
                                        ps[:, 4:7].rearrange("p b n -> p (b n)")[:, 0:TB * WK]
                                        .rearrange("p (k w) -> p k w", k=TB)[:, :, 0:W],
                                        g[:].rearrange("p (k w) -> p k w", k=TB), ALU.mult
                                        ).then_inc(qk_read, 1)
                v.wait_ge(qk_read, b.x + 1)
                nc.vector.tensor_tensor(lg[:], lg[:], pb[:].rearrange("p k w -> p (k w)"), ALU.add
                                        ).then_inc(biased, 1)

            def softmax_shift(b):
                byoffset = lg[:].rearrange("p (k o h) -> p k o h", h=H, k=TB)
                v.wait_ge(biased, b.x + 1)
                nc.vector.tensor_reduce(mx[:], lg[:].rearrange("p (k o h) -> p k h o", h=H, k=TB), AX_X, ALU.max
                                        ).then_inc(max_done, 1)
                v.wait_ge(max_done, b.x + 1)
                for k in range(TB):
                    n = nc.vector.tensor_tensor(byoffset[:, k], byoffset[:, k],
                                                mx[:, k].unsqueeze(1).to_broadcast([P, NO, H]), ALU.subtract)
                n.then_inc(shifted, 1)

            def weighted(u):
                def step(b):
                    v.wait_ge(pv_full, b.x * NU + u + 1)
                    if u:
                        hold(v, added, NU + 1, b + -1, u)
                    dst = yv[:, (u - 1) % RING] if u else acc[:, b.k % 3]
                    for o0, n in runs(UNITS[u]):
                        a = o0 - UNITS[u][0]
                        pt = ps[:, 2 * (u % 2):2 * (u % 2) + 2, :].rearrange("p b (a n) -> p (b a) n", n=L)
                        m = nc.vector.tensor_tensor(dst[:, a:a + n, :], pt[:, a:a + n, :], shift(vp, b, o0, n), ALU.mult)
                    m.then_inc(pv_read, 1)
                return step

            def sums(b):
                v.wait_ge(exp_done, b.x * NU + NU)
                nc.vector.tensor_reduce(den[:], pe8[:, :, :, 0].rearrange("p k (o h) -> p k h o", h=H), AX_X, ALU.add
                                        ).then_inc(summed, 1)

            def reciprocals(b):
                v.wait_ge(summed, b.x * 2 + 1)
                nc.vector.reciprocal(den[:], den[:]).then_inc(summed, 1)
                v.wait_ge(summed, b.x * 2 + 2)
                nc.vector.tensor_copy(denw[:].rearrange("p k (h d) -> p k h d", d=HD),
                                      den[:].unsqueeze(3).to_broadcast([P, TB, H, HD])).then_inc(den_done, 1)

            def gate_over_sums(b):
                v.wait_ge(r_full, b.x + 1)
                v.wait_ge(gs_done, b.x + 1)
                nc.vector.tensor_tensor(gs[:, b.k % 3], gs[:, b.k % 3], ps[:, 7, 0:L], ALU.mult).then_inc(r_read, 1)

            def gated(b):
                v.wait_ge(added, b.x * (NU + 1) + NU + 1)
                nc.vector.tensor_copy(ga[:, 0:1], modT[:, 1, 2, bass.ds(b.x, 1)])
                nc.vector.tensor_copy(ga[:, 1:2], gabo[:, bass.ds(b.x, 1)])
                v.wait_ge(r_read, b.x + 1)
                nc.vector.tensor_tensor(og[:], acc[:, b.k % 3, 0], gs[:, b.k % 3], ALU.mult).then_inc(og_done, 1)

            def residual(b):
                v.wait_ge(d_full, b.x * DD + 2)
                xs = x[:, bass.ds(b.x * TB, TB), :]
                nc.vector.tensor_tensor(xs, xs, ps[:, 7, 0:L].rearrange("p (k d) -> p k d", d=D), ALU.add
                                        ).then_inc(d_read, 1)

            run(v, [("Q", products(2)), ("Q", products(3)), ("V", weighted(0)), ("Q", products(4)),
                    ("V", weighted(1)), ("A", statistics), ("D", gated), ("A", moments), ("V", weighted(2)),
                    ("Q", products(5)), ("V", weighted(3)), ("A", normalise), ("V", weighted(4)),
                    ("R", sums), ("D", residual), ("Q", products(6)), ("V", weighted(5)), ("R", reciprocals),
                    ("Q", products(9)), ("V", weighted(6)), ("R", gate_over_sums), ("V", weighted(7)),
                    ("V", weighted(8)), ("Q", logits),
                    ("N", products(0)), ("V", weighted(9)), ("N", products(1)), ("Q", softmax_shift)])


def store_stream(nc, s, out):
    with nc.semaphore("st_stored") as stored, nc.Block() as block:
        @block.sync
        def _(sp):
            sp.dma_start(out.rearrange("b (k p) d -> p (b k) d", p=P), s["x"][:]).then_inc(stored, 16)
            sp.wait_ge(stored, 16)


def layout(inputs):
    a = {k: np.ascontiguousarray(v) for k, v in inputs.items()}
    side = np.arange(D).reshape(H, HD).T.reshape(-1)
    swap = np.arange(D).reshape(-1, 2)[:, ::-1].reshape(-1)[side]
    t = {
        "L0_attn_x": a["L0_attn_x"],
        "L0_attn_bv": a["L0_attn_bv"],
        "L0_attn_scale": a["L0_attn_scale"],
        "cT": np.stack([a["L0_c"].T, a["L1_c"].T], 1),
        "wmod": np.stack([a["L0_wmod"], a["L1_wmod"]], 1),
        "a0_w": np.stack([a["L0_attn_Wq"][side].T, a["L0_attn_Wq"][swap].T, a["L0_attn_Wk"][side].T, a["L0_attn_Wk"][swap].T,
                          a["L0_attn_Wv"].T, a["L0_attn_Wo"].T], 1),
        "a0_b": np.stack([a["L0_attn_bq"][side], a["L0_attn_bq"][swap], a["L0_attn_bk"][side], a["L0_attn_bk"][swap],
                          a["L0_attn_bo"]], 1),
    }
    gu = a["L0_ffn_gate_up_proj"].reshape(PAIRS, 2, 2, I0, D)
    pack = lambda w, first: np.concatenate([first.T[None], w.transpose(0, 3, 1, 2).reshape(PAIRS, D, P)]).transpose(1, 0, 2)
    t["e0_wg"] = pack(gu[:, :, 0], a["L0_ffn_shared_gate_w"])
    t["e0_wu"] = pack(gu[:, :, 1], a["L0_ffn_shared_up_w"])
    down = a["L0_ffn_down_proj"].reshape(PAIRS, 2, D, I0).transpose(0, 1, 3, 2).reshape(PAIRS, P, D)
    t["e0_wd"] = np.concatenate([a["L0_ffn_shared_down_w"].T[None], down]).transpose(1, 0, 2)
    t["e0_wr"] = a["L0_ffn_router_weight"].T
    t["L0_ffn_e_score_bias"] = a["L0_ffn_e_score_bias"]
    qkv, qb = a["L1_attn_qkv_w"].reshape(3, D, D), a["L1_attn_qkv_b"].reshape(3, D)
    t["a1_w"] = np.stack([*qkv, a["L1_attn_gate_w"], a["L1_attn_out_w"]]).transpose(2, 0, 1)
    t["a1_b"] = np.stack([*qb, a["L1_attn_gate_b"], a["L1_attn_out_b"]], 1)
    t["a1_ifg"] = np.repeat(a["L1_attn_if_gain"], HD)[:, None]
    emb = np.zeros((H, HD, NO, H), np.float32)
    for h in range(H):
        emb[h, :, :, h] = a["L1_attn_scale_embed"][::-1].T
    t["a1_emb"] = emb.reshape(D, NO * H)
    t["a1_pb"] = a["L1_attn_pos_bias"][::-1].reshape(-1)
    t["e1_w1"] = a["L1_ffn_W1"].transpose(1, 0, 2)
    t["e1_w2"] = a["L1_ffn_W2"].transpose(1, 0, 2)
    t["e1_b1"] = a["L1_ffn_b1"].T
    for name in ("L1_ffn_b2", "L1_ffn_Wr", "L1_ffn_br"):
        t[name] = a[name]
    t.update(shape_constants())
    return {k: np.ascontiguousarray(v) for k, v in t.items()}


def kernel(**inputs):
    import concourse.bacc as bacc
    from concourse.bass_utils import run_bass_kernel_spmd

    nc = bacc.Bacc("TRN2", target_bir_lowering=False, num_devices=1)
    arrays = layout(inputs)
    t = {name: nc.dram_tensor(name + "_dram", a.shape, mybir.dt.from_np(a.dtype), kind="ExternalInput").ap()
         for name, a in arrays.items()}
    out = nc.dram_tensor("out_dram", (B, L, D), F32, kind="ExternalOutput").ap()
    build(nc, t, out)
    r = run_bass_kernel_spmd(nc, [{name + "_dram": a for name, a in arrays.items()}], core_ids=[0])
    return r.results[0]["out_dram"]
```
